# Optimizing a Trainium2 kernel written in Bass

```python
import numpy as np
import jax
import jax.numpy as jnp

def _softmax(x, axis=-1):
    return jax.nn.softmax(x, axis=axis)

def _gelu(x):
    return jax.nn.gelu(x, approximate=True)

def _silu(x):
    return jax.nn.silu(x)

def _sigmoid(x):
    return jax.nn.sigmoid(x)

def _layernorm(x, axis=-1, eps=1e-05):
    m = jnp.mean(x, axis=axis, keepdims=True)
    v = jnp.var(x, axis=axis, keepdims=True)
    return (x - m) / jnp.sqrt(v + eps)

def _scatter_add(tgt, idx, src, axis=0):
    return tgt.at[idx].add(src)

def _segment_sum(src, seg, n):
    return jax.ops.segment_sum(src, seg, n)
kernel_name = 'mk_hybrid_d2_jaxref_r8_10b596'

def setup_inputs(seed: int=0):
    np.random.seed(seed)
    _w = jnp.asarray

    def _L0_attn_a_setup():
        import jax, jax.numpy as jnp
        import numpy as np
        B, T, D = (1, 512, 128)
        H, KD, VD = (16, 64, 64)
        MIN_THETA, MAX_THETA = (1.0, 10000.0)

        def _sin_cos(t, d, dtype):
            half = d // 2
            p = jnp.arange(half, dtype=dtype) / (half - 1)
            thetas = MIN_THETA * (MAX_THETA / MIN_THETA) ** p
            pos = jnp.arange(t, dtype=dtype)[:, None] / thetas[None, :]
            return (jnp.sin(pos), jnp.cos(pos))

        def _rope(x, sin, cos):
            d = x.shape[-1] // 2
            x_hi, x_lo = (x[..., :d], x[..., d:])
            y_lo = x_lo * cos + x_hi * sin
            y_hi = x_hi * cos - x_lo * sin
            return jnp.concatenate([y_lo, y_hi], axis=-1)
        key = jax.random.key(seed)
        k0, k1, k2 = jax.random.split(key, 3)
        x = jax.random.normal(k0, (B, T, D), dtype=jnp.float32)
        W_in = jax.random.normal(k1, ((2 * KD + VD) * H, D), dtype=jnp.float32) * 0.02
        b_in = jnp.zeros(((2 * KD + VD) * H,), dtype=jnp.float32)
        W_out = jax.random.normal(k2, (D, H * VD), dtype=jnp.float32) * 0.02
        b_out = jnp.zeros((D,), dtype=jnp.float32)
        return {'x': x, 'W_in': W_in, 'b_in': b_in, 'W_out': W_out, 'b_out': b_out}
    _L0_attn_a_in = _L0_attn_a_setup()

    def _L0_attn_b_setup():
        import jax, jax.numpy as jnp
        import numpy as np
        EPS = 1e-05

        def _layernorm(x, gamma, beta):
            m = jnp.mean(x, axis=-1, keepdims=True)
            v = jnp.mean(jnp.square(x - m), axis=-1, keepdims=True)
            return (x - m) * jax.lax.rsqrt(v + EPS) * gamma + beta
        key = jax.random.key(seed)
        B, Q, C, H = (4, 512, 128, 16)
        hd = C // H
        ks = jax.random.split(key, 8)
        s_in = 1.0 / np.sqrt(C)
        return {'x': jax.random.normal(ks[0], (B, Q, C), jnp.float32), 'qkv_w': jax.random.normal(ks[1], (3 * C, C), jnp.float32) * s_in, 'qkv_b': jnp.zeros((3 * C,), jnp.float32), 'kn_g': jnp.ones((hd,), jnp.float32), 'kn_b': jnp.zeros((hd,), jnp.float32), 'vn_g': jnp.ones((hd,), jnp.float32), 'vn_b': jnp.zeros((hd,), jnp.float32), 'temperature': jnp.ones((H, 1, 1), jnp.float32), 'attn_bias': jnp.zeros((H, hd, hd), jnp.float32), 'p1_w': jax.random.normal(ks[2], (C, C), jnp.float32) * s_in, 'p1_b': jnp.zeros((C,), jnp.float32), 'p2_w': jax.random.normal(ks[3], (C, C), jnp.float32) * s_in, 'p2_b': jnp.zeros((C,), jnp.float32)}
    _L0_attn_b_in = _L0_attn_b_setup()

    def _L0_ffn_setup():
        import jax, jax.numpy as jnp
        import numpy as np
        B, S, H, F, E = (8, 256, 128, 512, 8)
        INIT_LAMBDA = 0.2
        key = jax.random.key(seed)
        ks = jax.random.split(key, 12)
        std = 0.02
        return {'hidden_states': jax.random.normal(ks[0], (B, S, H), jnp.float32), 'gate_w1': jax.random.normal(ks[1], (H, H), jnp.float32) * 0.01, 'gate_b1': jnp.zeros((H,), jnp.float32), 'gate_w2': jax.random.normal(ks[2], (E, H), jnp.float32) * 0.01, 'gate_b2': jnp.full((E,), INIT_LAMBDA, jnp.float32), 'W1': jax.random.normal(ks[3], (F, H), jnp.float32) * std, 'b1': jax.random.normal(ks[4], (F,), jnp.float32) * std, 'W2': jax.random.normal(ks[5], (H, F), jnp.float32) * std, 'b2': jax.random.normal(ks[6], (H,), jnp.float32) * std, 'TW1': jax.random.normal(ks[7], (E, F, H), jnp.float32) * std, 'Tb1': jax.random.normal(ks[8], (E, F), jnp.float32) * std, 'TW2': jax.random.normal(ks[9], (E, H, F), jnp.float32) * std, 'Tb2': jax.random.normal(ks[10], (E, H), jnp.float32) * std}
    _L0_ffn_in = _L0_ffn_setup()

    def _L1_attn_a_setup():
        import jax, jax.numpy as jnp
        import numpy as np
        N_HEADS = 16
        key = jax.random.key(seed)
        ks = jax.random.split(key, 9)
        B, S, E = (2, 256, 128)
        s = 1.0 / np.sqrt(E)
        return {'x': jax.random.normal(ks[0], (B, S, E), jnp.float32), 'Wq': jax.random.normal(ks[1], (E, E), jnp.float32) * s, 'bq': jax.random.normal(ks[2], (E,), jnp.float32) * 0.01, 'Wk': jax.random.normal(ks[3], (E, E), jnp.float32) * s, 'bk': jax.random.normal(ks[4], (E,), jnp.float32) * 0.01, 'Wv': jax.random.normal(ks[5], (E, E), jnp.float32) * s, 'bv': jax.random.normal(ks[6], (E,), jnp.float32) * 0.01, 'Wo': jax.random.normal(ks[7], (E, E), jnp.float32) * s, 'bo': jax.random.normal(ks[8], (E,), jnp.float32) * 0.01}
    _L1_attn_a_in = _L1_attn_a_setup()

    def _L1_attn_b_setup():
        import jax, jax.numpy as jnp
        import numpy as np
        D_MODEL = 128
        N_HEADS = 16
        D_HEAD = D_MODEL // N_HEADS
        EPS_LN = 1e-05
        EPS_GATE = 1e-05
        EPS_DEN = 1e-05

        def _linear(x, w, b):
            return jnp.einsum('btd,od->bto', x, w) + b
        key = jax.random.key(seed)
        ks = jax.random.split(key, 4)
        B, T, D = (1, 256, D_MODEL)
        x = jax.random.normal(ks[0], (B, T, D), dtype=jnp.float32)
        s = 1.0 / np.sqrt(D)
        qkv_w = jax.random.normal(ks[1], (3 * D, D), dtype=jnp.float32) * s
        gate_w = jax.random.normal(ks[2], (D, D), dtype=jnp.float32) * s
        proj_w = jax.random.normal(ks[3], (D, D), dtype=jnp.float32) * s
        return {'x': x, 'ln_g': jnp.ones((D,), jnp.float32), 'ln_b': jnp.zeros((D,), jnp.float32), 'qkv_w': qkv_w, 'qkv_b': jnp.zeros((3 * D,), jnp.float32), 'gate_w': gate_w, 'gate_b': jnp.zeros((D,), jnp.float32), 'proj_w': proj_w, 'proj_b': jnp.zeros((D,), jnp.float32)}
    _L1_attn_b_in = _L1_attn_b_setup()

    def _L1_ffn_setup():
        import jax, jax.numpy as jnp
        import numpy as np
        DIM = 128

        def _reference_tuple_inner(x, W_r, W_k, W_v, mu_r, mu_k):
            B, T, C = x.shape
            x_prev = jnp.concatenate([jnp.zeros((B, 1, C), x.dtype), x[:, :-1, :]], axis=1)
            xr = mu_r * x + (1.0 - mu_r) * x_prev
            xk = mu_k * x + (1.0 - mu_k) * x_prev
            r = jax.nn.sigmoid(jnp.einsum('btc,dc->btd', xr, W_r))
            k = jnp.einsum('btc,dc->btd', xk, W_k)
            k_act = jnp.square(jax.nn.relu(k))
            out = r * jnp.einsum('btc,dc->btd', k_act, W_v)
            new_state = x[:, -1, :]
            return (out, new_state)
        key = jax.random.key(seed)
        ks = jax.random.split(key, 6)
        B, T, C = (8, 256, DIM)
        x = jax.random.normal(ks[0], (B, T, C), dtype=jnp.float32)
        s = 1.0 / np.sqrt(C)
        W_r = jax.random.uniform(ks[1], (C, C), jnp.float32, -s, s)
        W_k = jax.random.uniform(ks[2], (C, C), jnp.float32, -s, s)
        W_v = jax.random.uniform(ks[3], (C, C), jnp.float32, -s, s)
        mu_r = jax.random.uniform(ks[4], (C,), jnp.float32)
        mu_k = jax.random.uniform(ks[5], (C,), jnp.float32)
        return {'x': x, 'W_r': W_r, 'W_k': W_k, 'W_v': W_v, 'mu_r': mu_r, 'mu_k': mu_k}
    _L1_ffn_in = _L1_ffn_setup()
    _d = {'L0_attn_a_x': _L0_attn_a_in['x'], 'L0_attn_a_W_in': _L0_attn_a_in['W_in'], 'L0_attn_a_b_in': _L0_attn_a_in['b_in'], 'L0_attn_a_W_out': _L0_attn_a_in['W_out'], 'L0_attn_a_b_out': _L0_attn_a_in['b_out'], 'L0_attn_b_qkv_w': _L0_attn_b_in['qkv_w'], 'L0_attn_b_qkv_b': _L0_attn_b_in['qkv_b'], 'L0_attn_b_kn_g': _L0_attn_b_in['kn_g'], 'L0_attn_b_kn_b': _L0_attn_b_in['kn_b'], 'L0_attn_b_vn_g': _L0_attn_b_in['vn_g'], 'L0_attn_b_vn_b': _L0_attn_b_in['vn_b'], 'L0_attn_b_temperature': _L0_attn_b_in['temperature'], 'L0_attn_b_attn_bias': _L0_attn_b_in['attn_bias'], 'L0_attn_b_p1_w': _L0_attn_b_in['p1_w'], 'L0_attn_b_p1_b': _L0_attn_b_in['p1_b'], 'L0_attn_b_p2_w': _L0_attn_b_in['p2_w'], 'L0_attn_b_p2_b': _L0_attn_b_in['p2_b'], 'L0_ffn_gate_w1': _L0_ffn_in['gate_w1'], 'L0_ffn_gate_b1': _L0_ffn_in['gate_b1'], 'L0_ffn_gate_w2': _L0_ffn_in['gate_w2'], 'L0_ffn_gate_b2': _L0_ffn_in['gate_b2'], 'L0_ffn_W1': _L0_ffn_in['W1'], 'L0_ffn_b1': _L0_ffn_in['b1'], 'L0_ffn_W2': _L0_ffn_in['W2'], 'L0_ffn_b2': _L0_ffn_in['b2'], 'L0_ffn_TW1': _L0_ffn_in['TW1'], 'L0_ffn_Tb1': _L0_ffn_in['Tb1'], 'L0_ffn_TW2': _L0_ffn_in['TW2'], 'L0_ffn_Tb2': _L0_ffn_in['Tb2'], 'L1_attn_a_Wq': _L1_attn_a_in['Wq'], 'L1_attn_a_bq': _L1_attn_a_in['bq'], 'L1_attn_a_Wk': _L1_attn_a_in['Wk'], 'L1_attn_a_bk': _L1_attn_a_in['bk'], 'L1_attn_a_Wv': _L1_attn_a_in['Wv'], 'L1_attn_a_bv': _L1_attn_a_in['bv'], 'L1_attn_a_Wo': _L1_attn_a_in['Wo'], 'L1_attn_a_bo': _L1_attn_a_in['bo'], 'L1_attn_b_ln_g': _L1_attn_b_in['ln_g'], 'L1_attn_b_ln_b': _L1_attn_b_in['ln_b'], 'L1_attn_b_qkv_w': _L1_attn_b_in['qkv_w'], 'L1_attn_b_qkv_b': _L1_attn_b_in['qkv_b'], 'L1_attn_b_gate_w': _L1_attn_b_in['gate_w'], 'L1_attn_b_gate_b': _L1_attn_b_in['gate_b'], 'L1_attn_b_proj_w': _L1_attn_b_in['proj_w'], 'L1_attn_b_proj_b': _L1_attn_b_in['proj_b'], 'L1_ffn_W_r': _L1_ffn_in['W_r'], 'L1_ffn_W_k': _L1_ffn_in['W_k'], 'L1_ffn_W_v': _L1_ffn_in['W_v'], 'L1_ffn_mu_r': _L1_ffn_in['mu_r'], 'L1_ffn_mu_k': _L1_ffn_in['mu_k']}
    _x0 = _d['L0_attn_a_x']
    _d['L0_attn_a_x'] = jax.random.normal(jax.random.fold_in(jax.random.key(seed), 1), (1, 2048, 128), dtype=_x0.dtype)
    del _x0
    return _d

def reference(L0_attn_a_x, L0_attn_a_W_in, L0_attn_a_b_in, L0_attn_a_W_out, L0_attn_a_b_out, L0_attn_b_qkv_w, L0_attn_b_qkv_b, L0_attn_b_kn_g, L0_attn_b_kn_b, L0_attn_b_vn_g, L0_attn_b_vn_b, L0_attn_b_temperature, L0_attn_b_attn_bias, L0_attn_b_p1_w, L0_attn_b_p1_b, L0_attn_b_p2_w, L0_attn_b_p2_b, L0_ffn_gate_w1, L0_ffn_gate_b1, L0_ffn_gate_w2, L0_ffn_gate_b2, L0_ffn_W1, L0_ffn_b1, L0_ffn_W2, L0_ffn_b2, L0_ffn_TW1, L0_ffn_Tb1, L0_ffn_TW2, L0_ffn_Tb2, L1_attn_a_Wq, L1_attn_a_bq, L1_attn_a_Wk, L1_attn_a_bk, L1_attn_a_Wv, L1_attn_a_bv, L1_attn_a_Wo, L1_attn_a_bo, L1_attn_b_ln_g, L1_attn_b_ln_b, L1_attn_b_qkv_w, L1_attn_b_qkv_b, L1_attn_b_gate_w, L1_attn_b_gate_b, L1_attn_b_proj_w, L1_attn_b_proj_b, L1_ffn_W_r, L1_ffn_W_k, L1_ffn_W_v, L1_ffn_mu_r, L1_ffn_mu_k):

    def _L0_attn_a_ref(x, W_in, b_in, W_out, b_out):
        import jax, jax.numpy as jnp
        import numpy as np
        B, T, D = (1, 512, 128)
        H, KD, VD = (16, 64, 64)
        MIN_THETA, MAX_THETA = (1.0, 10000.0)

        def _sin_cos(t, d, dtype):
            half = d // 2
            p = jnp.arange(half, dtype=dtype) / (half - 1)
            thetas = MIN_THETA * (MAX_THETA / MIN_THETA) ** p
            pos = jnp.arange(t, dtype=dtype)[:, None] / thetas[None, :]
            return (jnp.sin(pos), jnp.cos(pos))

        def _rope(x, sin, cos):
            d = x.shape[-1] // 2
            x_hi, x_lo = (x[..., :d], x[..., d:])
            y_lo = x_lo * cos + x_hi * sin
            y_hi = x_hi * cos - x_lo * sin
            return jnp.concatenate([y_lo, y_hi], axis=-1)
        b, t, _ = x.shape
        proj = x @ W_in.T + b_in
        i1, i2 = (KD * H, 2 * KD * H)
        q = proj[..., :i1].reshape(b, t, H, KD).transpose(0, 2, 1, 3)
        k = proj[..., i1:i2].reshape(b, t, H, KD).transpose(0, 2, 1, 3)
        v = proj[..., i2:].reshape(b, t, H, VD).transpose(0, 2, 1, 3)
        sin, cos = _sin_cos(t, KD, x.dtype)
        q = _rope(q, sin, cos)
        k = _rope(k, sin, cos)
        scale = 1.0 / np.sqrt(KD)
        att = jnp.einsum('bhqd,bhkd->bhqk', q, k) * jnp.asarray(scale, x.dtype)
        mask = jnp.tril(jnp.ones((t, t), dtype=bool))
        att = jnp.where(mask[None, None], att, jnp.asarray(-jnp.inf, x.dtype))
        att = jax.nn.softmax(att, axis=-1)
        y = jnp.einsum('bhqk,bhkd->bhqd', att, v)
        y = y.transpose(0, 2, 1, 3).reshape(b, t, H * VD)
        return y @ W_out.T + b_out

    def _L0_attn_b_ref(x, qkv_w, qkv_b, kn_g, kn_b, vn_g, vn_b, temperature, attn_bias, p1_w, p1_b, p2_w, p2_b):
        import jax, jax.numpy as jnp
        import numpy as np
        EPS = 1e-05

        def _layernorm(x, gamma, beta):
            m = jnp.mean(x, axis=-1, keepdims=True)
            v = jnp.mean(jnp.square(x - m), axis=-1, keepdims=True)
            return (x - m) * jax.lax.rsqrt(v + EPS) * gamma + beta
        B, Q, C = x.shape
        H = temperature.shape[0]
        hd = C // H
        qkv = (x @ qkv_w.T + qkv_b).reshape(B, Q, 3, H, hd)
        qkv = jnp.transpose(qkv, (2, 0, 3, 1, 4))
        q, k, v = (qkv[0], qkv[1], qkv[2])
        k = _layernorm(k, kn_g, kn_b)
        v = _layernorm(v, vn_g, vn_b)
        kv = jnp.einsum('bhqd,bhqe->bhde', k, v) / Q * temperature + attn_bias
        att = jnp.einsum('bhqd,bhde->bhqe', q, kv)
        att = jnp.transpose(att, (0, 2, 1, 3)).reshape(B, Q, C) + x
        h = jax.nn.gelu(att @ p1_w.T + p1_b, approximate=False)
        return h @ p2_w.T + p2_b + x

    def _L0_ffn_ref(hidden_states, gate_w1, gate_b1, gate_w2, gate_b2, W1, b1, W2, b2, TW1, Tb1, TW2, Tb2):
        import jax, jax.numpy as jnp
        import numpy as np
        B, S, H, F, E = (8, 256, 128, 512, 8)
        INIT_LAMBDA = 0.2
        x = hidden_states
        h = jax.nn.relu(jnp.einsum('bsh,oh->bso', x, gate_w1) + gate_b1)
        g = jnp.einsum('bso,eo->bse', h, gate_w2) + gate_b2
        g = g.mean(axis=1)
        mW1 = W1 + jnp.einsum('be,efh->bfh', g, TW1)
        mb1 = b1 + g @ Tb1
        mW2 = W2 + jnp.einsum('be,ehf->bhf', g, TW2)
        mb2 = b2 + g @ Tb2
        u = jax.nn.gelu(jnp.einsum('bsh,bfh->bsf', x, mW1) + mb1[:, None, :])
        out = jnp.einsum('bsf,bhf->bsh', u, mW2) + mb2[:, None, :]
        return out

    def _L1_attn_a_ref(x, Wq, bq, Wk, bk, Wv, bv, Wo, bo):
        import jax, jax.numpy as jnp
        import numpy as np
        N_HEADS = 16
        B, S, E = x.shape
        H = N_HEADS
        D = E // H
        q = (x @ Wq.T + bq).reshape(B, S, H, D)
        k = (x @ Wk.T + bk).reshape(B, S, H, D)
        v = (x @ Wv.T + bv).reshape(B, S, H, D)
        scores = jnp.einsum('bqnd,bknd->bnqk', q, k) / jnp.sqrt(jnp.float32(D))
        attn = jax.nn.softmax(scores, axis=1)
        out = jnp.einsum('bnqk,bknd->bnqd', attn, v)
        out = out.transpose(0, 2, 1, 3).reshape(B, S, E)
        return out @ Wo.T + bo

    def _L1_attn_b_ref(x, ln_g, ln_b, qkv_w, qkv_b, gate_w, gate_b, proj_w, proj_b):
        import jax, jax.numpy as jnp
        import numpy as np
        D_MODEL = 128
        N_HEADS = 16
        D_HEAD = D_MODEL // N_HEADS
        EPS_LN = 1e-05
        EPS_GATE = 1e-05
        EPS_DEN = 1e-05

        def _linear(x, w, b):
            return jnp.einsum('btd,od->bto', x, w) + b
        B, T, D = x.shape
        H, Dh = (N_HEADS, D_HEAD)
        mu = jnp.mean(x, axis=-1, keepdims=True)
        var = jnp.mean((x - mu) ** 2, axis=-1, keepdims=True)
        x_norm = (x - mu) / jnp.sqrt(var + EPS_LN) * ln_g + ln_b
        qkv = _linear(x_norm, qkv_w, qkv_b)
        q, k, v = jnp.split(qkv, 3, axis=-1)
        gate_sig = jax.nn.sigmoid(_linear(x, gate_w, gate_b))
        gate_norm = gate_sig / (jnp.mean(gate_sig, axis=-1, keepdims=True) + EPS_GATE)
        q = q * gate_norm
        k = k * gate_norm

        def heads(t):
            return t.reshape(B, T, H, Dh).transpose(0, 2, 1, 3)
        q, k, v = (heads(q).astype(jnp.float32), heads(k).astype(jnp.float32), heads(v).astype(jnp.float32))
        q = jax.nn.elu(q) + 1.0
        k = jax.nn.elu(k) + 1.0
        kv = jnp.einsum('bhtd,bhtm->bhtdm', k, v)
        kv_cum = jnp.cumsum(kv, axis=2)
        out_num = jnp.einsum('bhtd,bhtdm->bhtm', q, kv_cum)
        k_cum = jnp.cumsum(k, axis=2)
        out_den = jnp.einsum('bhtd,bhtd->bht', q, k_cum)[..., None] + EPS_DEN
        out = out_num / out_den
        out = out.astype(x_norm.dtype).transpose(0, 2, 1, 3).reshape(B, T, D)
        return _linear(out, proj_w, proj_b)

    def _L1_ffn_ref(x, W_r, W_k, W_v, mu_r, mu_k):
        import jax, jax.numpy as jnp
        import numpy as np
        DIM = 128

        def _reference_tuple_inner(x, W_r, W_k, W_v, mu_r, mu_k):
            B, T, C = x.shape
            x_prev = jnp.concatenate([jnp.zeros((B, 1, C), x.dtype), x[:, :-1, :]], axis=1)
            xr = mu_r * x + (1.0 - mu_r) * x_prev
            xk = mu_k * x + (1.0 - mu_k) * x_prev
            r = jax.nn.sigmoid(jnp.einsum('btc,dc->btd', xr, W_r))
            k = jnp.einsum('btc,dc->btd', xk, W_k)
            k_act = jnp.square(jax.nn.relu(k))
            out = r * jnp.einsum('btc,dc->btd', k_act, W_v)
            new_state = x[:, -1, :]
            return (out, new_state)
        return _reference_tuple_inner(x, W_r, W_k, W_v, mu_r, mu_k)[0]
    x = L0_attn_a_x
    x = x + _L0_attn_a_ref(_layernorm(x, axis=-1), L0_attn_a_W_in, L0_attn_a_b_in, L0_attn_a_W_out, L0_attn_a_b_out)
    x = x + _L0_ffn_ref(_layernorm(x, axis=-1), L0_ffn_gate_w1, L0_ffn_gate_b1, L0_ffn_gate_w2, L0_ffn_gate_b2, L0_ffn_W1, L0_ffn_b1, L0_ffn_W2, L0_ffn_b2, L0_ffn_TW1, L0_ffn_Tb1, L0_ffn_TW2, L0_ffn_Tb2)
    x = x + _L0_attn_b_ref(_layernorm(x, axis=-1), L0_attn_b_qkv_w, L0_attn_b_qkv_b, L0_attn_b_kn_g, L0_attn_b_kn_b, L0_attn_b_vn_g, L0_attn_b_vn_b, L0_attn_b_temperature, L0_attn_b_attn_bias, L0_attn_b_p1_w, L0_attn_b_p1_b, L0_attn_b_p2_w, L0_attn_b_p2_b)
    x = x + _L0_ffn_ref(_layernorm(x, axis=-1), L0_ffn_gate_w1, L0_ffn_gate_b1, L0_ffn_gate_w2, L0_ffn_gate_b2, L0_ffn_W1, L0_ffn_b1, L0_ffn_W2, L0_ffn_b2, L0_ffn_TW1, L0_ffn_Tb1, L0_ffn_TW2, L0_ffn_Tb2)
    x = x + _L1_attn_a_ref(_layernorm(x, axis=-1), L1_attn_a_Wq, L1_attn_a_bq, L1_attn_a_Wk, L1_attn_a_bk, L1_attn_a_Wv, L1_attn_a_bv, L1_attn_a_Wo, L1_attn_a_bo)
    x = x + _L1_ffn_ref(_layernorm(x, axis=-1), L1_ffn_W_r, L1_ffn_W_k, L1_ffn_W_v, L1_ffn_mu_r, L1_ffn_mu_k)
    x = x + _L1_attn_b_ref(_layernorm(x, axis=-1), L1_attn_b_ln_g, L1_attn_b_ln_b, L1_attn_b_qkv_w, L1_attn_b_qkv_b, L1_attn_b_gate_w, L1_attn_b_gate_b, L1_attn_b_proj_w, L1_attn_b_proj_b)
    x = x + _L1_ffn_ref(_layernorm(x, axis=-1), L1_ffn_W_r, L1_ffn_W_k, L1_ffn_W_v, L1_ffn_mu_r, L1_ffn_mu_k)
    return x

_drawn_inputs = setup_inputs


def setup_inputs(seed=0):
    import zlib

    import numpy as np

    out = dict(_drawn_inputs(seed))
    spreads = {'L0_attn_a_b_in': (0.0, 0.1),
     'L0_attn_a_b_out': (0.0, 0.1),
     'L0_attn_b_qkv_b': (0.0, 0.1),
     'L0_attn_b_kn_g': (1.0, 0.6),
     'L0_attn_b_kn_b': (0.0, 0.682),
     'L0_attn_b_vn_g': (1.0, 0.6),
     'L0_attn_b_vn_b': (0.0, 0.432),
     'L0_attn_b_temperature': (1.0, 0.6),
     'L0_attn_b_attn_bias': (0.0, 0.1),
     'L0_attn_b_p1_b': (0.0, 0.1),
     'L0_attn_b_p2_b': (0.0, 0.1),
     'L0_ffn_gate_b1': (0.0, 0.8),
     'L0_ffn_gate_b2': (0.20000000298023224, 0.6),
     'L1_attn_b_ln_g': (1.0, 0.6),
     'L1_attn_b_ln_b': (0.0, 2.0),
     'L1_attn_b_qkv_b': (0.0, 2.0),
     'L1_attn_b_gate_b': (0.0, 2.0),
     'L1_attn_b_proj_b': (0.0, 2.0)}
    factors = {'L0_attn_a_W_in': 3.275,
     'L0_ffn_gate_w1': 8.0,
     'L0_ffn_gate_w2': 8.0,
     'L0_ffn_Tb1': 3.564,
     'L1_attn_a_bq': 8.0,
     'L1_attn_a_bk': 6.287,
     'L1_attn_a_bo': 64.0,
     'L1_attn_b_gate_w': 64.0,
     'L1_ffn_W_r': 8.0,
     'L1_ffn_W_k': 7.774,
     'L1_ffn_W_v': 6.363,
     'L1_ffn_mu_r': 8.0,
     'L1_ffn_mu_k': 8.0,
     'L1_attn_b_qkv_w': 8.0,
     'L1_attn_b_proj_w': 8.0}
    for name, (base, spread) in spreads.items():
        noise = np.random.default_rng([zlib.crc32(name.encode()), seed]).standard_normal(out[name].shape)
        drawn = base * np.exp(spread * noise) if base else spread * noise
        out[name] = jnp.asarray(drawn.astype(out[name].dtype))
    for name, factor in factors.items():
        out[name] = (out[name] * factor).astype(out[name].dtype)
    return out
```

```python
from contextlib import ExitStack

import numpy as np
import concourse.bass as bass
from concourse import mybir

ALU = mybir.AluOpType
ACT = mybir.ActivationFunctionType
AX_X = mybir.AxisListType.X
F32 = mybir.dt.float32
F32R = mybir.dt.float32r
BF16 = mybir.dt.bfloat16

P = 128
T = 2048
CW = 512
NC = T // CW
NT = T // P
EPS = 1e-5
HEADS = 16


class Scope:

    def __init__(self, nc, stack, prefix):
        self.nc, self.stack, self.prefix = nc, stack, prefix

    def sb(self, name, shape, dt=F32):
        return self.stack.enter_context(self.nc.sbuf_tensor(f"{self.prefix}_{name}", shape, dt))

    def ps(self, name, shape, dt=F32):
        return self.stack.enter_context(self.nc.psum_tensor(f"{self.prefix}_{name}", shape, dt))

    def sem(self, name):
        return self.stack.enter_context(self.nc.semaphore(f"{self.prefix}_{name}"))


def chunk(c):
    return slice(c * CW, (c + 1) * CW)


def tile(t):
    return slice(t * P, (t + 1) * P)



class Norm:

    def __init__(self, scope):
        self.mean, self.centred, self.squared, self.var, self.std, self.diag, self.spread, self.out, self.recip = (
            scope.sem(n) for n in ("mean", "centred", "squared", "var", "std", "diag", "spread", "out", "recip"))
        self.runs = 0


def layernorm(nc, norm, const, x, out):
    b = NC * norm.runs
    norm.runs += 1
    with ExitStack() as stack:
        s = Scope(nc, stack, f"ln{norm.runs}")
        cen = s.sb("centred", [P, T])
        sq = s.sb("squared", [P, T])
        std = s.sb("std", [P, NC, 4])
        rstd = s.sb("rstd", [P, NC, 4])
        diag = s.sb("diag", [P, NC, 4, P])
        spread = s.ps("spread", [P, NC, CW])
        var = s.ps("var", [P, NC, CW])

        with nc.Block(no_gpsimd_drain=True) as block:
            @block.tensor
            def _(pe):
                def variances(c):
                    pe.wait_ge(norm.squared, b + c + 1)
                    for j in range(4):
                        last = nc.tensor.matmul(var[:, c, j:j + 1], sq[:, tile(4 * c + j)], const["mean"][:, 0:1],
                                                start=True, stop=True)
                    last.then_inc(norm.var, 1)

                def spread_out(c):
                    pe.wait_ge(norm.diag, b + c + 1)
                    nc.tensor.matmul(spread[:, c], const["ones"][:], diag[:, c].rearrange("p j q -> p (j q)"),
                                     start=True, stop=True).then_inc(norm.spread, 1)

                for c in range(NC):
                    nc.tensor.matmul(spread[:, c], const["mean"][:], x[:, chunk(c)],
                                     start=True, stop=True).then_inc(norm.mean, 1)
                variances(0)
                for c in range(1, NC):
                    variances(c)
                    spread_out(c - 1)
                spread_out(NC - 1)

            @block.scalar
            def _(act):
                def square(c):
                    act.wait_ge(norm.centred, b + c + 1)
                    nc.scalar.activation(sq[:, chunk(c)], cen[:, chunk(c)], ACT.Square).then_inc(norm.squared, 1)

                def root(c):
                    act.wait_ge(norm.var, b + c + 1)
                    nc.scalar.activation(std[:, c], var[:, c, 0:4], ACT.Sqrt, bias=const["eps"][:]).then_inc(norm.std, 1)

                square(0)
                for c in range(1, NC):
                    square(c)
                    root(c - 1)
                root(NC - 1)

            @block.vector
            def _(dve):
                def diagonal(c):
                    dve.wait_ge(norm.std, b + c + 1)
                    nc.vector.reciprocal(rstd[:, c], std[:, c]).then_inc(norm.recip, 1)
                    dve.wait_ge(norm.recip, b + c + 1)
                    nc.vector.tensor_tensor(diag[:, c], const["ident"][:, None, :].broadcast_to([P, 4, P]),
                                            rstd[:, c, :, None].broadcast_to([P, 4, P]),
                                            ALU.mult).then_inc(norm.diag, 1)

                def scale(c):
                    dve.wait_ge(norm.spread, b + c + 1)
                    dve.wait_ge(norm.centred, b + c + 1)
                    nc.vector.tensor_tensor(out[:, chunk(c)], spread[:, c], cen[:, chunk(c)],
                                            ALU.mult).then_inc(norm.out, 1)

                for c in range(NC):
                    dve.wait_ge(norm.mean, b + c + 1)
                    nc.vector.tensor_tensor(cen[:, chunk(c)], x[:, chunk(c)], spread[:, c],
                                            ALU.subtract).then_inc(norm.centred, 1)
                diagonal(0)
                for c in range(1, NC):
                    diagonal(c)
                    scale(c - 1)
                scale(NC - 1)



KD = 64
PAIRS = HEADS * KD // P
MAX_W = 2 * CW
SLOTS = 3
PROBS = 4
LAG = 2
PAIR_COLS = 6 * P


def pair_schedule():
    def needs(c):
        return ([("rope", "dve", 0, c), ("rope", "dve", 1, c), ("hi", None, 0, c), ("v", "dve", c), ("hi", None, 1, c),
                 ("lo", None, 0, c), ("lo", None, 1, c)] +
                [("max", "dve", h, qt, g) for qt in range(4 * c, 4 * c + 4) for h in range(2)
                 for g in range(qt // 8 + 1)])

    plan = needs(0) + [("turn", "act", 0)]
    late = []
    for c in range(NC):
        keys = 4 * c + 4
        ahead = (needs(c + 1) if c + 1 < NC else [])
        emitted = 0
        for kt in range(keys):
            plan.append(("score", "act", c, kt))
            late.append([LAG, ("value", None, c, kt)])
            if kt == keys - 1:
                late.append([LAG + 2, ("den", "act", c)])
                late.append([LAG + 5, ("out", "dve", c)])
            for item in late:
                item[0] -= 1
            plan += [item[1] for item in late if item[0] < 0]
            late = [item for item in late if item[0] >= 0]
            due = (kt + 1) * len(ahead) // keys
            if c == 0 or kt < keys - 1:
                plan += ahead[emitted:due]
                emitted = due
        plan += ahead[emitted:]
        if c + 1 < NC:
            plan.append(("turn", "act", c + 1))
    plan += [item[1] for item in sorted(late, key=lambda item: item[0])]
    return plan


def attention_a(nc, const, x, n, w_pairs, bias_pairs, value_bias, out_bias, trig):
    plan = pair_schedule()
    fills = [p for p in plan if p[1]]
    fill_no = {p: i for i, p in enumerate(fills)}
    dve_slots = {p: i for i, p in enumerate([p for p in fills if p[1] == "dve"])}
    act_slots = {p: i for i, p in enumerate([p for p in fills if p[1] == "act"])}
    scores = [p for p in plan if p[0] == "score"]
    step_no = {p[2:]: i for i, p in enumerate(scores)}
    NF, ND, NA, NS = len(fills), len(dve_slots), len(act_slots), len(scores)

    def width(c, kt):
        return CW - first(c, kt)

    def first(c, kt):
        return max(0, kt - 4 * c) * P

    pool_adds = [k for k in step_no if k[1] % 2 == 0 and (k[1] > 0 or k[0] == 0)]
    dve_adds = [k for k in step_no if k[1] % 2 == 1 and (k[1] > 1 or k[0] == 0)]
    added_no = {k: i for adds in (pool_adds, dve_adds) for i, k in enumerate(adds)}
    for c in range(1, NC):
        added_no[(c, 0)], added_no[(c, 1)] = added_no[(c, 2)], added_no[(c, 3)]
    NPA, NDA = len(pool_adds), len(dve_adds)
    last_needed = max(dve_slots[("rope", "dve", 1, NC - 1)], dve_slots[("v", "dve", NC - 1)]) + 1

    with ExitStack() as stack:
        s = Scope(nc, stack, "aa")
        w = s.sb("weights", [P, 5 * P])
        wo = s.sb("out_weights", [P, P])
        bias = s.sb("bias", [P, 4])
        vbias = s.sb("value_bias", [P, P])
        cos, sin = trig[:, 0], trig[:, 1]
        obias = s.sb("out_bias", [P, 1])
        t1 = s.sb("turned", [P, 2, CW])
        t2 = s.sb("straight", [P, 2, CW])
        y = s.sb("rotated", [P, 2, CW])
        q_hi = [s.sb(f"q_hi{h}", [P, T], F32R) for h in range(2)]
        q_lo = [s.sb(f"q_lo{h}", [KD + 1, T], F32R) for h in range(2)]
        k_st = [s.sb(f"k_stack{h}", [P, T], F32R) for h in range(2)]
        k_one = [s.sb(f"k_one{h}", [KD + 1, T], F32R) for h in range(2)]
        v = s.sb("values", [P, NT, P])
        part = s.sb("part_max", [P, NC, 2, 4, 2])
        mx = s.sb("maxima", [P, NC, 2, 4])
        rows = s.sb("max_rows", [8, 2, P], F32R)
        probs = s.sb("probs", [P, PROBS, 2, CW])
        acc_p = s.sb("den_even", [P, 2, 2, CW])
        acc_d = s.sb("den_odd", [P, 2, 2, CW])
        zero = s.sb("zero", [P, 2])
        log_den = s.sb("log_den", [P, CW])
        rden = s.sb("rden", [P, CW])
        yv = s.sb("attended", [P, 2, CW])
        slot = s.ps("slot", [P, SLOTS, 2, CW])
        acc_y = s.ps("acc_y", [P, 2, CW])

        loaded = s.sem("weights_loaded")
        out_loaded = s.sem("out_weights_and_bias_loaded")
        filled = s.sem("slots_filled")
        dve_read = s.sem("slots_read_dve")
        act_read = s.sem("slots_read_act")
        turned = s.sem("rope_turned")
        rotated = s.sem("rope_rotated")
        hi_done = s.sem("hi_written")
        lo_done = s.sem("lo_written")
        part_done = s.sem("part_max_done")
        max_done = s.sem("max_done")
        row_loaded = s.sem("max_rows_loaded")
        value_done = s.sem("value_products")
        pool_added = s.sem("added_even")
        dve_added = s.sem("added_odd")
        rden_done = s.sem("rden_done")
        y_done = s.sem("attended_done")
        prepared = s.sem("ones_and_zeros_prepared")
        cleared = s.sem("den_odd_cleared")
        x_biased = s.sem("x_biased")

        HI_PER_CHUNK = 8
        hi_rows = {0: slice(0, KD), 1: slice(KD, P)}

        with nc.Block(no_gpsimd_drain=True) as block:
            @block.sync
            def _(sp):
                sp.dma_start(obias[:], out_bias).then_inc(out_loaded, 16)

                def load(i):
                    sp.dma_start(w[:], w_pairs[:, bass.ts(i, PAIR_COLS)][:, 0:5 * P]).then_inc(loaded, 16)
                    sp.dma_start(bias[:], bias_pairs[:, bass.ts(i, 4)]).then_inc(loaded, 16)
                    sp.dma_start(vbias[:], value_bias[:, bass.ts(i, P)]).then_inc(loaded, 16)

                def load_out(i):
                    sp.dma_start(wo[:], w_pairs[:, bass.ts(i, PAIR_COLS)][:, 5 * P:]).then_inc(out_loaded, 16)

                def max_rows(i, c):
                    sp.wait_ge(act_read, i * NA + act_slots[("turn", "act", c)] + 1)
                    for h in range(2):
                        dst = q_lo[h][KD:KD + 1, chunk(c)].rearrange("o (j q) -> o j q", j=4)
                        sp.dma_start(dst.bitcast(F32), rows[4 * h:4 * h + 4, c % 2, :].bitcast(F32)).then_inc(row_loaded, 16)

                load(0)
                load_out(0)
                with sp.Fori(0, PAIRS - 1) as i:
                    for c in range(NC - 1):
                        max_rows(i, c)
                    sp.wait_ge(dve_read, i * ND + last_needed)
                    load(i + 1)
                    max_rows(i, NC - 1)
                    sp.wait_ge(filled, i * NF + fill_no[("out", "dve", NC - 1)] + 1)
                    load_out(i + 1)
                for c in range(NC):
                    max_rows(PAIRS - 1, c)

            @block.tensor
            def _(pe):
                pe.wait_ge(prepared, 3)
                with pe.Fori(0, PAIRS) as i:
                    pe.wait_ge(loaded, (i + 1) * 48)
                    for p in plan:
                        kind = p[0]
                        if p[1]:
                            no = fill_no[p]
                            if no >= SLOTS:
                                before = fills[no - SLOTS]
                                if before[1] == "dve":
                                    pe.wait_ge(dve_read, i * ND + dve_slots[before] + 1)
                                else:
                                    pe.wait_ge(act_read, i * NA + act_slots[before] + 1)
                            sl = slot[:, no % SLOTS]
                        if kind == "rope":
                            _, _, which, c = p
                            for b in range(2):
                                last = nc.tensor.matmul(sl[:, b], w[:, tile(2 * which + b)], n[:, chunk(c)],
                                                        start=True, stop=True)
                        elif kind == "v":
                            c = p[2]
                            for j in range(4):
                                last = nc.tensor.matmul(sl[:, 0, tile(j)], n[:, tile(4 * c + j)],
                                                        w[:, tile(4)], start=True, stop=True)
                        elif kind == "max":
                            _, _, h, qt, g = p
                            if h == 0 and g == 0 and qt % 4 == 0:
                                pe.wait_ge(hi_done, i * NC * HI_PER_CHUNK + (qt // 4 + 1) * HI_PER_CHUNK)
                                pe.wait_ge(lo_done, i * NC * 4 + (qt // 4 + 1) * 4)
                            keys = min(MAX_W, (qt + 1) * P - g * MAX_W)
                            for b in range((keys + CW - 1) // CW):
                                m = min(CW, keys - b * CW)
                                k0 = g * MAX_W + b * CW
                                diagonal = k0 + m == (qt + 1) * P
                                last = nc.tensor.matmul(sl[:, b, 0:m], q_hi[h][:, tile(qt)], k_st[h][:, k0:k0 + m],
                                                        start=True, stop=not diagonal)
                                if diagonal:
                                    last = nc.tensor.matmul(sl[:, b, m - P:m], const["ident_bf"][:], const["mask_q"][:],
                                                            start=False, stop=True)
                        elif kind == "turn":
                            c = p[2]
                            pe.wait_ge(max_done, i * NC + c + 1)
                            last = nc.tensor.transpose(sl[0:8, 0, 0:P], mx[:, c].rearrange("p h j -> p (h j)"),
                                                       const["ident"][:])
                        elif kind == "score":
                            _, _, c, kt = p
                            if kt == 0:
                                pe.wait_ge(row_loaded, i * NC * 32 + (c + 1) * 32)
                            a = first(c, kt)
                            q0 = c * CW + a
                            m = CW - a
                            diagonal = kt >= 4 * c
                            for h in range(2):
                                nc.tensor.matmul(sl[:, h, a:], k_st[h][:, tile(kt)], q_hi[h][:, q0:q0 + m],
                                                 start=True, stop=False)
                                last = nc.tensor.matmul(sl[:, h, a:], k_one[h][:, tile(kt)], q_lo[h][:, q0:q0 + m],
                                                        start=False, stop=not diagonal)
                                if diagonal:
                                    last = nc.tensor.matmul(sl[:, h, a:a + P], const["ident_bf"][:], const["mask_k"][:],
                                                            start=False, stop=True)
                        elif kind == "value":
                            _, _, c, kt = p
                            step = step_no[(c, kt)]
                            pe.wait_ge(act_read, i * NA + act_slots[("score", "act", c, kt)] + 1)
                            if kt == 0 and c < 2:
                                pe.wait_ge(y_done, i * NC)
                            elif kt == 0:
                                pe.wait_ge(y_done, i * NC + c - 1)
                            if kt == 4 * c:
                                pe.wait_ge(dve_read, i * ND + dve_slots[("v", "dve", c)] + 1)
                            a = first(c, kt)
                            for h in range(2):
                                last = nc.tensor.matmul(acc_y[KD * h:KD * h + KD, c % 2, a:], v[:, kt, KD * h:KD * h + KD],
                                                        probs[:, step % PROBS, h, a:],
                                                        start=(kt == 0), stop=(kt == 4 * c + 3))
                            last.then_inc(value_done, 1)
                        elif kind == "den":
                            c = p[2]
                            pe.wait_ge(pool_added, i * NPA + added_no[(c, 4 * c + 2)] + 1)
                            pe.wait_ge(dve_added, i * NDA + added_no[(c, 4 * c + 3)] + 1)
                            if c == 0:
                                pe.wait_ge(cleared, i + 1)
                            for h in range(2):
                                o = sl[KD * h:KD * h + KD, 0]
                                nc.tensor.matmul(o, const["ones"][:, 0:KD], acc_p[:, c % 2, h], start=True, stop=False)
                                last = nc.tensor.matmul(o, const["ones"][:, 0:KD], acc_d[:, c % 2, h],
                                                        start=False, stop=True)
                        elif kind == "out":
                            c = p[2]
                            if c == 0:
                                pe.wait_ge(out_loaded, 16 + (i + 1) * 16)
                            pe.wait_ge(y_done, i * NC + c + 1)
                            last = nc.tensor.matmul(sl[:, 0], wo[:], yv[:, c % 2], start=True, stop=True)
                        if p[1]:
                            last.then_inc(filled, 1)
                    pe.wait_ge(dve_read, (i + 1) * ND)
                    pe.wait_ge(act_read, (i + 1) * NA)

            @block.scalar
            def _(act):
                nc.scalar.preload_act_table_set("natural_log_exp_and_others")
                with act.Fori(0, PAIRS) as i:
                    for p in plan:
                        if p[0] == "hi":
                            _, _, which, c = p
                            act.wait_ge(rotated, i * NC * 2 + 2 * c + which + 1)
                            for h in range(2):
                                src = y[KD * h:KD * h + KD, which]
                                if which == 0:
                                    outs = (q_hi[h][0:KD, chunk(c)], q_hi[h][KD:P, chunk(c)])
                                else:
                                    outs = (k_st[h][hi_rows[h], chunk(c)], k_one[h][0:KD, chunk(c)])
                                for o in outs:
                                    nc.scalar.activation(o, src, ACT.Copy).then_inc(hi_done, 1)
                        if p[1] != "act":
                            continue
                        act.wait_ge(filled, i * NF + fill_no[p] + 1)
                        sl = slot[:, fill_no[p] % SLOTS]
                        if p[0] == "turn":
                            c = p[2]
                            if c >= 2:
                                act.wait_ge(row_loaded, i * NC * 32 + (c - 1) * 32)
                            else:
                                act.wait_ge(row_loaded, i * NC * 32)
                            nc.scalar.activation(rows[:, c % 2], sl[0:8, 0, 0:P], ACT.Copy,
                                                 scale=-1.0).then_inc(act_read, 1)
                        elif p[0] == "den":
                            c = p[2]
                            nc.scalar.activation(log_den[:], sl[:, 0], ACT.Ln).then_inc(act_read, 1)
                            act.wait_ge(act_read, i * NA + act_slots[p] + 1)
                            act.wait_ge(y_done, i * NC + c)
                            nc.scalar.activation(rden[:], log_den[:], ACT.Exp, scale=-1.0).then_inc(rden_done, 1)
                        else:
                            _, _, c, kt = p
                            step = step_no[(c, kt)]
                            old = scores[step - PROBS][2:] if step >= PROBS else None
                            if old:
                                act.wait_ge(value_done, i * NS + step - PROBS + 1)
                                old_add = old if old in pool_adds or old in dve_adds else (old[0], old[1] + 2)
                                if old[1] % 2 == 0:
                                    act.wait_ge(pool_added, i * NPA + added_no[old_add] + 1)
                                else:
                                    act.wait_ge(dve_added, i * NDA + added_no[old_add] + 1)
                            elif step == 0:
                                act.wait_ge(value_done, i * NS)
                                act.wait_ge(pool_added, i * NPA)
                                act.wait_ge(dve_added, i * NDA)
                            a = first(c, kt)
                            nc.scalar.activation(probs[:, step % PROBS, :, a:], sl[:, :, a:], ACT.Exp,
                                                 scale=1.0 / 8.0).then_inc(act_read, 1)

            @block.gpsimd
            def _(pool):
                nc.gpsimd.memset(zero[:], 0.0).then_inc(prepared, 1)
                pool.wait_ge(prepared, 3)

                def add(i, c, kt, los):
                    k = added_no[(c, kt)]
                    pool.wait_ge(lo_done, i * NC * 4 + los)
                    pool.wait_ge(act_read, i * NA + act_slots[("score", "act", c, kt)] + 1)
                    if k:
                        pool.wait_ge(pool_added, i * NPA + k)
                    a = first(c, kt)
                    src = probs[:, step_no[(c, kt)] % PROBS, :, a:]
                    dst = acc_p[:, c % 2, :, a:]
                    if kt == 2 and c >= 2:
                        pool.wait_ge(filled, i * NF + fill_no[("den", "act", c - 2)] + 1)
                    elif k == 0:
                        pool.wait_ge(filled, i * NF)
                    if kt == 0:
                        nc.gpsimd.tensor_tensor(dst, src, zero[:, :, None].broadcast_to([P, 2, CW]),
                                                ALU.add).then_inc(pool_added, 1)
                    elif kt == 2 and c >= 1:
                        nc.gpsimd.tensor_tensor(dst, probs[:, step_no[(c, 0)] % PROBS], src,
                                                ALU.add).then_inc(pool_added, 1)
                    else:
                        nc.gpsimd.tensor_tensor(dst, dst, src, ALU.add).then_inc(pool_added, 1)

                with pool.Fori(0, PAIRS) as i:
                    los = adds = 0
                    for p in plan:
                        if p[0] == "value" and p[2:] in pool_adds:
                            add(i, *p[2:], los)
                            adds += 1
                        elif p[0] == "lo":
                            _, _, which, c = p
                            pool.wait_ge(pool_added, i * NPA + adds)
                            for h in range(2):
                                pool.wait_ge(lo_done, i * NC * 4 + los)
                                los += 1
                                pool.wait_ge(hi_done, i * NC * 8 + c * 8 + 4 * which + 2 * h + 2)
                                if which == 0:
                                    r = slice(KD * h, KD * h + KD)
                                    src_hi, o = q_hi[h][r, chunk(c)], q_lo[h][0:KD, chunk(c)]
                                else:
                                    src_hi, o = k_st[h][hi_rows[h], chunk(c)], k_st[h][hi_rows[1 - h], chunk(c)]
                                nc.gpsimd.tensor_tensor(o, y[KD * h:KD * h + KD, which], src_hi.bitcast(F32),
                                                        ALU.subtract).then_inc(lo_done, 1)

            @block.vector
            def _(dve):
                for h in range(2):
                    nc.vector.memset(k_one[h][KD:KD + 1, :].bitcast(F32), 1.0).then_inc(prepared, 1)
                dve.wait_ge(out_loaded, 32)
                with dve.Fori(0, PAIRS) as i:
                    dve.wait_ge(loaded, (i + 1) * 48)

                    def add(c, kt):
                        if kt == 1 and c > 0:
                            return
                        dve.wait_ge(act_read, i * NA + act_slots[("score", "act", c, kt)] + 1)
                        k = added_no[(c, kt)]
                        dve.wait_ge(dve_added, i * NDA + k)
                        a = first(c, kt)
                        src = probs[:, step_no[(c, kt)] % PROBS, :, a:]
                        dst = acc_d[:, c % 2, :, a:]
                        if kt == 1:
                            nc.vector.memset(acc_d[:, c % 2, :, 0:a], 0.0).then_inc(cleared, 1)
                            nc.vector.tensor_copy(dst, src).then_inc(dve_added, 1)
                        elif kt == 3 and c > 0:
                            if c >= 2:
                                dve.wait_ge(filled, i * NF + fill_no[("den", "act", c - 2)] + 1)
                            nc.vector.tensor_tensor(dst, probs[:, step_no[(c, 1)] % PROBS], src,
                                                    ALU.add).then_inc(dve_added, 1)
                        else:
                            nc.vector.tensor_tensor(dst, dst, src, ALU.add).then_inc(dve_added, 1)

                    parts = 0
                    for p in plan:
                        kind = p[0]
                        if kind == "value":
                            if p[3] % 2 == 1:
                                add(p[2], p[3])
                            continue
                        if kind == "den":
                            c = p[2]
                            dve.wait_ge(rden_done, i * NC + c + 1)
                            dve.wait_ge(value_done, i * NS + step_no[(c, 4 * c + 3)] + 1)
                            nc.vector.tensor_tensor(yv[:, c % 2], acc_y[:, c % 2], rden[:],
                                                    ALU.mult).then_inc(y_done, 1)
                        if p[1] != "dve":
                            continue
                        no = fill_no[p]
                        sl = slot[:, no % SLOTS]
                        dve.wait_ge(filled, i * NF + no + 1)
                        if kind == "rope":
                            _, _, which, c = p
                            k = i * NC * 2 + 2 * c + which
                            nc.vector.scalar_tensor_tensor(t1[:, which], sl[:, 1], bias[:, 2 * which + 1:2 * which + 2],
                                                           cos[:, chunk(c)], ALU.add, ALU.mult).then_inc(turned, 1)
                            nc.vector.scalar_tensor_tensor(t2[:, which], sl[:, 0], bias[:, 2 * which:2 * which + 1],
                                                           sin[:, chunk(c)], ALU.add, ALU.mult).then_inc(dve_read, 1)
                            dve.wait_ge(turned, k + 1)
                            dve.wait_ge(dve_read, i * ND + dve_slots[p] + 1)
                            if c:
                                dve.wait_ge(hi_done, i * NC * 8 + (c - 1) * 8 + 4 * which + 4)
                                dve.wait_ge(lo_done, i * NC * 4 + (c - 1) * 4 + 2 * which + 2)
                            nc.vector.tensor_tensor(y[:, which], t1[:, which], t2[:, which],
                                                    ALU.add).then_inc(rotated, 1)
                        elif kind == "v":
                            c = p[2]
                            nc.vector.tensor_tensor(v[:, 4 * c:4 * c + 4], sl[:, 0].rearrange("p (t e) -> p t e", e=P),
                                                    vbias[:, None, :].broadcast_to([P, 4, P]),
                                                    ALU.add).then_inc(dve_read, 1)
                        elif kind == "max":
                            _, _, h, qt, g = p
                            c, j = qt // 4, qt % 4
                            keys = min(MAX_W, (qt + 1) * P - g * MAX_W)
                            o = part[:, c, h, j, g:g + 1] if c >= 2 else mx[:, c, h, j:j + 1]
                            nc.vector.tensor_reduce(o, sl.rearrange("p b m -> p (b m)")[:, 0:keys], AX_X,
                                                    ALU.max).then_inc(dve_read, 1)
                            if qt % 4 == 3 and h == 1 and g == qt // 8:
                                dve.wait_ge(dve_read, i * ND + dve_slots[p] + 1)
                                if c >= 2:
                                    nc.vector.tensor_reduce(mx[:, c], part[:, c], AX_X, ALU.max).then_inc(max_done, 1)
                                else:
                                    dve.sem_inc(max_done, 1)
                        elif kind == "out":
                            c = p[2]
                            nc.vector.tensor_tensor(x[:, chunk(c)], sl[:, 0], x[:, chunk(c)],
                                                    ALU.add).then_inc(dve_read, 1)
                dve.wait_ge(dve_read, PAIRS * ND)
                nc.vector.tensor_scalar(x[:], x[:], obias[:, 0:1], None, ALU.add).then_inc(x_biased, 1)



HD = P // HEADS
PARTS = 3
TERMS = [(0, 0), (0, 1), (1, 0), (0, 2), (2, 0), (1, 1)]
KROWS = len(TERMS) * HD
PAIRS_H = HEADS // 2
QUADS = HEADS // 4
INVERT_AFTER = 3
GROUPS = NT * NC
DVE_HEADS = 8


def head_at(pos):
    return pos // 4 + 4 * (pos % 4)


def project_narrow(nc, n, wq, wk, wv, bq, bk, bv, v, q_stack, scratch):
    with ExitStack() as stack:
        s = Scope(nc, stack, "ph")
        full = s.sb("full", [P, 2, T])
        rest = s.sb("rest", [P, 2, T])
        parts = s.sb("parts", [P, 2, PARTS, T], BF16)
        acc = s.ps("acc", [P, 8, CW])
        projected = s.sem("projected")
        full_done = s.sem("full_done")
        hi_done = s.sem("hi_done")
        rest_done = s.sem("rest_done")
        mid_done = s.sem("mid_done")
        lo_done = s.sem("lo_done")
        v_read = s.sem("v_read_q_stack_cleared")
        stored = s.sem("parts_stored")
        items = [(w, c) for c in range(NC) for w in range(2)]

        with nc.Block(no_gpsimd_drain=True) as block:
            @block.tensor
            def _(pe):
                for i, (w, c) in enumerate(items):
                    nc.tensor.matmul(acc[:, i], (wq, wk)[w], n[:, chunk(c)], start=True,
                                     stop=True).then_inc(projected, 1)
                for g in range(4):
                    pe.wait_ge(full_done, g + 1)
                    for j in range(4):
                        last = nc.tensor.matmul(acc[:, g, tile(j)], n[:, tile(4 * g + j)], wv, start=True, stop=True)
                    last.then_inc(projected, 1)

            @block.vector
            def _(dve):
                for i, (w, c) in enumerate(items):
                    dve.wait_ge(projected, i + 1)
                    nc.vector.tensor_scalar(full[:, w, chunk(c)], acc[:, i], (bq, bk)[w], None,
                                            ALU.add).then_inc(full_done, 1)
                for i, (w, c) in enumerate(items):
                    dve.wait_ge(full_done, i + 1)
                    dve.wait_ge(hi_done, i + 1)
                    nc.vector.tensor_tensor(rest[:, w, chunk(c)], full[:, w, chunk(c)], parts[:, w, 0, chunk(c)],
                                            ALU.subtract).then_inc(rest_done, 1)
                for i, (w, c) in enumerate(items):
                    dve.wait_ge(rest_done, i + 1)
                    dve.wait_ge(mid_done, i + 1)
                    nc.vector.tensor_tensor(parts[:, w, 2, chunk(c)], rest[:, w, chunk(c)], parts[:, w, 1, chunk(c)],
                                            ALU.subtract).then_inc(lo_done, 1)
                for g in range(4):
                    dve.wait_ge(projected, 8 + g + 1)
                    nc.vector.tensor_tensor(v[:, 4 * g:4 * g + 4], acc[:, g].rearrange("p (t e) -> p t e", t=4),
                                            bv[:, None, :].broadcast_to([P, 4, P]), ALU.add).then_inc(v_read, 1)

            @block.scalar
            def _(act):
                for i, (w, c) in enumerate(items):
                    act.wait_ge(full_done, i + 1)
                    nc.scalar.activation(parts[:, w, 0, chunk(c)], full[:, w, chunk(c)], ACT.Copy).then_inc(hi_done, 1)
                for i, (w, c) in enumerate(items):
                    act.wait_ge(rest_done, i + 1)
                    nc.scalar.activation(parts[:, w, 1, chunk(c)], rest[:, w, chunk(c)], ACT.Copy).then_inc(mid_done, 1)

            @block.gpsimd
            def _(pool):
                nc.gpsimd.memset(q_stack[:], 0.0).then_inc(v_read, 1)
                pool.wait_ge(v_read, 5)

            @block.sync
            def _(sp):
                sp.wait_ge(hi_done, len(items))
                for w in range(2):
                    sp.dma_start(scratch[w, 0], parts[:, w, 0]).then_inc(stored, 16)
                sp.wait_ge(mid_done, len(items))
                for w in range(2):
                    sp.dma_start(scratch[w, 1], parts[:, w, 1]).then_inc(stored, 16)
                sp.wait_ge(lo_done, len(items))
                for w in range(2):
                    sp.dma_start(scratch[w, 2], parts[:, w, 2]).then_inc(stored, 16)
                sp.wait_ge(stored, 2 * PARTS * 16)


def stack_parts(nc, q_stack, scratch, k_scratch):
    with ExitStack() as stack:
        s = Scope(nc, stack, "sp")
        k_stack = s.sb("k_stack", [112, PAIRS_H, T], BF16)
        stacked = s.sem("stacked")
        stored = s.sem("stored")
        with nc.Block(no_gpsimd_drain=True) as block:
            def load(eng, w, dst):
                for t, term in enumerate(TERMS):
                    src = scratch[w, term[w]].rearrange("(pair par d) x -> par d pair x", par=2, d=HD)
                    for par in range(2):
                        r = 64 * par + HD * t
                        eng.dma_start(dst[r:r + HD], src[par]).then_inc(stacked, 16)

            @block.sync
            def _(sp):
                load(sp, 1, k_stack)
                sp.wait_ge(stacked, 2 * len(TERMS) * 16 * 2)
                for par in range(2):
                    sp.dma_start(k_scratch[par], k_stack[64 * par:64 * par + KROWS]).then_inc(stored, 16)
                sp.wait_ge(stored, 32)

            @block.scalar
            def _(act):
                load(act, 0, q_stack)


def softmax_over_heads(nc, const, x, q_stack, v, k_scratch, w_out, b_out):
    scale = float(1.0 / np.sqrt(np.float32(HD)))
    with ExitStack() as stack:
        s = Scope(nc, stack, "hs")
        kt_stack = s.sb("k_tile", [P, 2, HEADS, P], BF16)
        v_pad = s.sb("v_padded", [P, 2, HEADS, 32])
        rounded = s.sb("rounded", [P, 2, HEADS, CW], BF16)
        mx = s.sb("maxima", [P, 2, CW], BF16)
        ex = s.sb("exps", [P, 2, HEADS, CW])
        total = s.sb("total", [P, 2, CW])
        rtot = s.sb("r_total", [P, 2, CW])
        slot = s.ps("slot", [P, 2, 2, CW])
        acc = s.ps("attended", [P, NC, CW])

        k_loaded = [s.sem(f"k_loaded{b}") for b in range(2)]
        v_copied = s.sem("v_copied")
        cleared = s.sem("v_and_k_cleared")
        filled = s.sem("slots_filled")
        read = s.sem("slots_read")
        tree = s.sem("max_tree")
        summed = s.sem("summed")
        logged = s.sem("logged")
        inverted = s.sem("inverted")
        dve_scaled = s.sem("scaled_dve")
        pool_scaled = s.sem("scaled_pool")
        accumulated = s.sem("accumulated")
        zeroed = s.sem("zeroed")
        out_copied = s.sem("out_copied")
        out_projected = s.sem("out_projected")
        x_added = s.sem("x_added")

        SL = HEADS // 2
        BODY = 8

        def loop(eng, emit):
            for step in (-2, -1, 0, 1):
                emit(step, 0, step % BODY, 0)
            with eng.Fori(0, (GROUPS - 8) // BODY) as i:
                for g in range(2, BODY + 2):
                    emit(g, i * BODY, g % BODY, i)
            for g in range(GROUPS - 6, GROUPS + 1):
                emit(g, 0, g % BODY, 0)

        def has(step, base, shift):
            if not isinstance(base, int):
                return True
            return 0 <= step + base + shift < GROUPS

        def exp_pass(g):
            return 2 * g + 2 - (1 if isinstance(g, int) and g == GROUPS - 1 else 0)

        def rounded_pass(g):
            return g if isinstance(g, int) and g < 2 else 2 * g - 1

        with nc.Block(no_gpsimd_drain=True) as block:
            @block.sync
            def _(sp):
                def load(kt, buf):
                    for par in range(2):
                        sp.dma_start(kt_stack[64 * par:64 * par + KROWS, buf].rearrange("r (pair two) k -> r pair two k", two=2)
                                     [:, :, par], k_scratch[par][:, :, bass.ts(kt, P)])\
                            .then_inc(k_loaded[buf], 16)

                sp.wait_ge(cleared, 2)
                load(0, 0)
                load(1, 1)
                with sp.Fori(0, NT // 2 - 1) as i:
                    for b in range(2):
                        last_step = 8 * i + 4 * b + 3
                        sp.wait_ge(filled, SL * (exp_pass(last_step) + 1))
                        sp.wait_ge(k_loaded[b], 32)
                        load(2 * i + 2 + b, b)

            @block.gpsimd
            def _(pool):
                nc.gpsimd.memset(v_pad[:], 0.0).then_inc(cleared, 1)
                pool.wait_ge(cleared, 2)

                def stage_values(kt, buf):
                    for r in range(QUADS):
                        nc.gpsimd.tensor_copy(v_pad[:, buf, 4 * r:4 * r + 4, HD * r:HD * r + HD],
                                              v[:, bass.ts(kt, 1)].rearrange("p o (j r d) -> p (o j) r d", j=4, r=4)
                                              [:, :, r]).then_inc(v_copied, 1)

                def emit(step, base, phase, turns):
                    if not has(step, base, -1):
                        return
                    g = base + step - 1
                    gp = (phase - 1) % BODY
                    if gp % 4 == 0:
                        kt = 2 * turns + (step - 1) // 4
                        if not (isinstance(g, int) and g < 8):
                            pool.wait_ge(accumulated, g - 4)
                        pool.wait_ge(cleared, 2)
                        stage_values(kt, gp // 4)
                    pool.wait_ge(inverted, g + 1)
                    nc.gpsimd.tensor_tensor(ex[:, gp % 2, DVE_HEADS:], ex[:, gp % 2, DVE_HEADS:],
                                            rtot[:, gp % 2, None, :].broadcast_to([P, HEADS - DVE_HEADS, CW]),
                                            ALU.mult).then_inc(pool_scaled, 1)

                loop(pool, emit)

            @block.tensor
            def _(pe):
                def scores(phase, first_fill, shifted, between=None):
                    kt_buf, c = (phase % BODY) // 4, phase % 4
                    for j in range(SL):
                        b = j % 2
                        if not (isinstance(first_fill, int) and first_fill + j < 2):
                            pe.wait_ge(read, first_fill + j - 1)
                        for e in range(2):
                            h = head_at(2 * j + e)
                            last = nc.tensor.matmul(slot[:, b, e], kt_stack[:, kt_buf, h], q_stack[:, h // 2, chunk(c)],
                                                    start=True, stop=not shifted)
                            if shifted:
                                last = nc.tensor.matmul(slot[:, b, e], const["neg_ident_bf"][:], mx[:, phase % 2],
                                                        start=False, stop=True)
                        last.then_inc(filled, 1)
                        if between and j % 2 == 1:
                            between(j // 2)

                def emit(step, base, phase, turns):
                    if step == 0 and isinstance(base, int) and base == 0:
                        for c in range(NC):
                            last = nc.tensor.matmul(acc[:, c], const["zero_bf"][0:32], q_stack[0:32, 0, chunk(c)],
                                                    start=True, stop=True)
                        last.then_inc(zeroed, 1)
                    first_fill = SL * exp_pass(base + step)
                    if has(step, base, 0):
                        pe.wait_ge(tree, 4 * (base + step) + 4)
                        scores(phase, first_fill, True)

                    def values(r):
                        g = base + step - 1
                        gp = (phase - 1) % BODY
                        if r == 0:
                            pe.wait_ge(dve_scaled, g + 1)
                            if gp % 4 == 0:
                                pe.wait_ge(v_copied, 4 * (2 * turns + (step - 1) // 4 + 1))
                        if 4 * r + 4 > DVE_HEADS:
                            pe.wait_ge(pool_scaled, g + 1)
                        for pos in range(4 * r, 4 * r + 4):
                            j = pos % 4
                            last = nc.tensor.matmul(acc[32 * j:32 * j + 32, gp % 4], v_pad[:, gp // 4, pos],
                                                    ex[:, gp % 2, pos], start=False, stop=False, skip_group_check=True)
                        if r == QUADS - 1:
                            last.then_inc(accumulated, 1)

                    if has(step, base, 2):
                        g2 = (phase + 2) % BODY
                        if g2 % 4 == 0:
                            t = (step + 2) // 4
                            pe.wait_ge(k_loaded[t % 2], 32 * (turns + t // 2 + 1))
                        scores(g2, SL * rounded_pass(base + step + 2), False, values if has(step, base, -1) else None)
                    elif has(step, base, -1):
                        for r in range(QUADS):
                            values(r)

                loop(pe, emit)
                for c in range(NC):
                    pe.wait_ge(out_copied, c + 1)
                    if c == 0:
                        pe.wait_ge(read, 2 * SL * GROUPS)
                    nc.tensor.matmul(slot[:, c // 2, c % 2], w_out, ex[:, 0, c], start=True,
                                     stop=True).then_inc(out_projected, 1)

            @block.scalar
            def _(act):
                nc.scalar.preload_act_table_set("natural_log_exp_and_others")

                def invert(g, b):
                    act.wait_ge(summed, g + 1)
                    nc.scalar.activation(total[:, b], total[:, b], ACT.Ln).then_inc(logged, 1)
                    act.wait_ge(logged, g + 1)
                    if not (isinstance(g, int) and g < 2):
                        act.wait_ge(dve_scaled, g - 1)
                        act.wait_ge(pool_scaled, g - 1)
                    nc.scalar.activation(rtot[:, b], total[:, b], ACT.Exp, scale=-1.0).then_inc(inverted, 1)

                def emit(step, base, phase, turns):
                    first_fill = SL * exp_pass(base + step)
                    if has(step, base, 0):
                        g = base + step
                        if not (isinstance(g, int) and g < 2):
                            act.wait_ge(accumulated, g - 1)
                        for j in range(SL):
                            act.wait_ge(filled, first_fill + j + 1)
                            nc.scalar.activation(ex[:, phase % 2, 2 * j:2 * j + 2], slot[:, j % 2], ACT.Exp,
                                                 scale=scale).then_inc(read, 1)
                            if j == INVERT_AFTER and has(step, base, -1):
                                invert(base + step - 1, (phase - 1) % 2)
                    elif has(step, base, -1):
                        invert(base + step - 1, (phase - 1) % 2)
                    if has(step, base, 2):
                        g = base + step + 2
                        if not (isinstance(g, int) and g < 2):
                            act.wait_ge(tree, 4 * (g - 2) + 4)
                        first_fill = SL * rounded_pass(g)
                        for j in range(SL):
                            act.wait_ge(filled, first_fill + j + 1)
                            nc.scalar.activation(rounded[:, phase % 2, 2 * j:2 * j + 2], slot[:, j % 2],
                                                 ACT.Copy).then_inc(read, 1)

                loop(act, emit)
                act.wait_ge(accumulated, GROUPS)
                act.wait_ge(zeroed, 1)
                for c in range(NC):
                    nc.scalar.activation(ex[:, 0, c], acc[:, c], ACT.Copy).then_inc(out_copied, 1)

            @block.vector
            def _(dve):
                nc.vector.memset(kt_stack[:], 0.0).then_inc(cleared, 1)

                def maxima(g, b, first_read):
                    dve.wait_ge(read, first_read)
                    r = rounded[:, b]
                    for k, m in enumerate((8, 4, 2, 1)):
                        if k:
                            dve.wait_ge(tree, 4 * g + k)
                        elif not (isinstance(g, int) and g < 2):
                            dve.wait_ge(filled, SL * (exp_pass(g - 2) + 1))
                        o = r[:, 0:m] if m > 1 else mx[:, b:b + 1]
                        nc.vector.tensor_tensor(o, r[:, 0:m], r[:, m:2 * m], ALU.max).then_inc(tree, 1)

                def emit(step, base, phase, turns):
                    if has(step, base, -1):
                        g = base + step - 1
                        b = (phase - 1) % 2
                        dve.wait_ge(read, SL * (exp_pass(g) + 1))
                        if not (isinstance(g, int) and g < 2):
                            dve.wait_ge(inverted, g - 1)
                        nc.vector.tensor_reduce(total[:, b], ex[:, b].rearrange("p n q -> p q n"), AX_X,
                                                ALU.add).then_inc(summed, 1)
                    if has(step, base, 1):
                        ahead = base + step + 1
                        maxima(ahead, (phase + 1) % 2, SL * (rounded_pass(ahead) + 1))
                    if has(step, base, -1):
                        dve.wait_ge(inverted, g + 1)
                        b = (phase - 1) % 2
                        nc.vector.tensor_tensor(ex[:, b, 0:DVE_HEADS], ex[:, b, 0:DVE_HEADS],
                                                rtot[:, b, None, :].broadcast_to([P, DVE_HEADS, CW]),
                                                ALU.mult).then_inc(dve_scaled, 1)

                loop(dve, emit)
                for c in range(NC):
                    dve.wait_ge(out_projected, c + 1)
                    nc.vector.scalar_tensor_tensor(x[:, chunk(c)], slot[:, c // 2, c % 2], b_out, x[:, chunk(c)],
                                                   ALU.add, ALU.add).then_inc(x_added, 1)
                dve.wait_ge(x_added, NC)



FF = 512
FT = FF // P
EXPERTS = 8


def modulated_ffn(nc, const, x, n, w, vec):
    with ExitStack() as stack:
        s = Scope(nc, stack, f"ff{const['ffn_runs']}")
        const["ffn_runs"] += 1
        relu = s.sb("relu", [P, CW])
        rsum = s.sb("relu_sum", [P, NC])
        rmean = s.sb("relu_mean", [P, 2])
        spread = s.sb("mean_spread", [P, P])
        gate = s.sb("gate", [P, EXPERTS])
        m1 = s.sb("mixed_w1", [P, FF])
        m2 = s.sb("mixed_w2", [P, FF])
        tmp = s.sb("tmp", [P, FT + 1, EXPERTS])
        mb = s.sb("mixed_b", [P, FT + 1])
        u = s.sb("hidden", [P, 2, FT, CW])
        ps = s.ps("acc", [P, 8, CW])
        gated = s.sem("gate_hidden")
        summed = s.sem("relu_summed")
        averaged = s.sem("averaged")
        gate_ps = s.sem("gate_product")
        gate_done = s.sem("gate_done")
        mixed1 = s.sem("w1_mixed")
        mixed2 = s.sem("w2_mixed")
        mixed_b = s.sem("b_mixed")
        hidden_ps = s.sem("hidden_product")
        hidden = s.sem("hidden_done")
        out_ps = s.sem("out_product")
        added = s.sem("x_added")

        with nc.Block(no_gpsimd_drain=True) as block:
            @block.tensor
            def _(pe):
                for c in range(NC):
                    nc.tensor.matmul(ps[:, c], w["gate1"], n[:, chunk(c)], start=True, stop=True).then_inc(gated, 1)
                pe.wait_ge(averaged, 3)
                nc.tensor.matmul(ps[:, 4, 0:EXPERTS], spread[:], w["gate2"], start=True, stop=True).then_inc(gate_ps, 1)
                pe.wait_ge(mixed1, EXPERTS)

                def up(c):
                    for f in range(FT):
                        k = c * FT + f
                        if k >= 4:
                            pe.wait_ge(hidden, k - 3)
                        nc.tensor.matmul(ps[:, k % 4], m1[:, tile(f)], n[:, chunk(c)], start=True,
                                         stop=True).then_inc(hidden_ps, 1)

                def down(c):
                    pe.wait_ge(hidden, c * FT + FT)
                    if c == 0:
                        pe.wait_ge(mixed2, EXPERTS)
                        pe.wait_ge(gate_done, 1)
                    if c >= 2:
                        pe.wait_ge(added, c - 1)
                    for f in range(FT):
                        last = nc.tensor.matmul(ps[:, 4 + c % 2], m2[:, tile(f)], u[:, c % 2, f], start=(f == 0),
                                                stop=(f == FT - 1))
                    last.then_inc(out_ps, 1)

                up(0)
                for c in range(1, NC):
                    up(c)
                    down(c - 1)
                down(NC - 1)

            @block.scalar
            def _(act):
                for c in range(NC):
                    act.wait_ge(gated, c + 1)
                    if c:
                        act.wait_ge(summed, c)
                    nc.scalar.activation(relu[:], ps[:, c], ACT.Relu, bias=vec["gate_b1"],
                                         accum_out=rsum[:, c:c + 1]).then_inc(summed, 1)
                act.wait_ge(mixed_b, 3)
                for c in range(NC):
                    for f in range(FT):
                        act.wait_ge(hidden_ps, c * FT + f + 1)
                        if c >= 2 and f == 0:
                            act.wait_ge(out_ps, c - 1)
                        nc.scalar.activation(u[:, c % 2, f], ps[:, (c * FT + f) % 4], ACT.Gelu_apprx_tanh,
                                             bias=mb[:, f:f + 1]).then_inc(hidden, 1)

            @block.vector
            def _(dve):
                dve.wait_ge(summed, NC)
                nc.vector.tensor_reduce(rmean[:, 0:1], rsum[:], AX_X, ALU.add).then_inc(averaged, 1)
                dve.wait_ge(averaged, 1)
                nc.vector.tensor_scalar(rmean[:, 1:2], rmean[:, 0:1], 1.0 / T, None, ALU.mult).then_inc(averaged, 1)
                dve.wait_ge(averaged, 2)
                nc.vector.tensor_scalar(spread[:], const["ones"][:], rmean[:, 1:2], None, ALU.mult).then_inc(averaged, 1)
                dve.wait_ge(gate_ps, 1)
                nc.vector.tensor_tensor(gate[:], ps[:, 4, 0:EXPERTS], w["gate_b2"], ALU.add).then_inc(gate_done, 1)
                dve.wait_ge(gate_done, 1)
                nc.vector.tensor_tensor(tmp[:], w["tb"], gate[:, None, :].broadcast_to([P, FT + 1, EXPERTS]),
                                        ALU.mult).then_inc(mixed_b, 1)
                dve.wait_ge(mixed_b, 1)
                nc.vector.tensor_reduce(mb[:], tmp[:], AX_X, ALU.add).then_inc(mixed_b, 1)
                dve.wait_ge(mixed_b, 2)
                nc.vector.tensor_tensor(mb[:], mb[:], vec["ffn_b"], ALU.add).then_inc(mixed_b, 1)
                for mixed, base, experts, done in ((m1, w["w1"], w["tw1"], mixed1), (m2, w["w2"], w["tw2"], mixed2)):
                    for e in range(EXPERTS):
                        if e:
                            dve.wait_ge(done, e)
                        nc.vector.scalar_tensor_tensor(mixed[:], experts[:, e * FF:(e + 1) * FF], gate[:, e:e + 1],
                                                       mixed[:] if e else base, ALU.mult, ALU.add).then_inc(done, 1)
                for c in range(NC):
                    dve.wait_ge(out_ps, c + 1)
                    if c == 0:
                        dve.wait_ge(mixed_b, 3)
                    nc.vector.scalar_tensor_tensor(x[:, chunk(c)], ps[:, 4 + c % 2], mb[:, FT:FT + 1], x[:, chunk(c)],
                                                   ALU.add, ALU.add).then_inc(added, 1)


def mix_ffn(nc, const, x, n, w, mu):
    with ExitStack() as stack:
        s = Scope(nc, stack, f"mf{const['mix_runs']}")
        const["mix_runs"] += 1
        rest = s.sb("one_less_mu", [P, 2])
        old = s.sb("before", [P, 2, T])
        xm = s.sb("mixed", [P, 2, T])
        r = s.sb("gate", [P, T])
        k = s.sb("relu", [P, T])
        k2 = s.sb("squared", [P, T])
        o = s.sb("product", [P, T])
        ps = s.ps("acc", [P, 8, CW])
        rested = s.sem("rest_done")
        scaled = s.sem("before_scaled")
        mixed = s.sem("mixed")
        product = s.sem("products")
        gated = s.sem("gated")
        relu = s.sem("relu_done")
        squared = s.sem("squared")
        value = s.sem("value_products")
        multiplied = s.sem("multiplied")
        added = s.sem("x_added")
        with nc.Block(no_gpsimd_drain=True) as block:
            @block.gpsimd
            def _(pool):
                pool.wait_ge(rested, 1)
                for c in range(NC):
                    for m in range(2):
                        nc.gpsimd.tensor_scalar(old[:, m, chunk(c)], n[:, c * CW:(c + 1) * CW], rest[:, m:m + 1], 0.0,
                                                ALU.mult, ALU.add).then_inc(scaled, 1)

            @block.vector
            def _(dve):
                nc.vector.tensor_scalar(rest[:], mu, -1.0, 1.0, ALU.mult, ALU.add).then_inc(rested, 1)
                for c in range(NC):
                    for m in range(2):
                        dve.wait_ge(scaled, 2 * c + m + 1)
                        nc.vector.scalar_tensor_tensor(xm[:, m, chunk(c)], n[:, 1 + c * CW:1 + (c + 1) * CW],
                                                       mu[:, m:m + 1], old[:, m, chunk(c)], ALU.mult,
                                                       ALU.add).then_inc(mixed, 1)
                for c in range(NC):
                    dve.wait_ge(relu, c + 1)
                    nc.vector.tensor_tensor(k2[:, chunk(c)], k[:, chunk(c)], k[:, chunk(c)], ALU.mult)\
                        .then_inc(squared, 1)
                for c in range(NC):
                    dve.wait_ge(value, c + 1)
                    dve.wait_ge(gated, c + 1)
                    nc.vector.tensor_tensor(o[:, chunk(c)], ps[:, c], r[:, chunk(c)], ALU.mult).then_inc(multiplied, 1)
                for c in range(NC):
                    dve.wait_ge(multiplied, c + 1)
                    nc.vector.tensor_tensor(x[:, chunk(c)], o[:, chunk(c)], x[:, chunk(c)], ALU.add).then_inc(added, 1)

            @block.tensor
            def _(pe):
                for c in range(NC):
                    for m in range(2):
                        pe.wait_ge(mixed, 2 * c + m + 1)
                        nc.tensor.matmul(ps[:, 4 * m + c], (w["r"], w["k"])[m], xm[:, m, chunk(c)], start=True,
                                         stop=True).then_inc(product, 1)
                for c in range(NC):
                    pe.wait_ge(squared, c + 1)
                    pe.wait_ge(gated, c + 1)
                    nc.tensor.matmul(ps[:, c], w["v"], k2[:, chunk(c)], start=True, stop=True).then_inc(value, 1)

            @block.scalar
            def _(act):
                for c in range(NC):
                    act.wait_ge(product, 2 * c + 1)
                    nc.scalar.activation(r[:, chunk(c)], ps[:, c], ACT.Sigmoid).then_inc(gated, 1)
                    act.wait_ge(product, 2 * c + 2)
                    nc.scalar.activation(k[:, chunk(c)], ps[:, 4 + c], ACT.Relu).then_inc(relu, 1)


GH = HEADS


def channel_attention(nc, const, x, n, w, vec):
    with ExitStack() as stack:
        s = Scope(nc, stack, "ca")
        q = s.sb("q", [P, T])
        kv = s.sb("kv", [P, NT, 2, GH, HD])
        cen = s.sb("centred", [P, NT, 2, GH, HD])
        sq = s.sb("squared", [P, NT, 2, GH, HD])
        mean = s.sb("mean", [P, NT, 2, GH])
        var = s.sb("var", [P, NT, 2, GH])
        std = s.sb("std", [P, NT, 2, GH])
        rstd = s.sb("rstd", [P, NT, 2, GH])
        head = s.sb("head_matrix", [P, 2, P])
        att = s.sb("att", [P, T])
        h = s.sb("gelu", [P, T])
        o = s.sb("out", [P, T])
        ps = s.ps("acc", [P, 8, CW])
        kv_ps = s.sem("kv_products")
        q_ps = s.sem("q_products")
        kv_in = s.sem("kv_in")
        q_in = s.sem("q_in")
        step = s.sem("norm_steps")
        squared = s.sem("squared")
        rooted = s.sem("rooted")
        gained = s.sem("gained")
        head_ps = s.sem("head_product")
        head_done = s.sem("head_done")
        att_ps = s.sem("att_products")
        att_done = s.sem("att_done")
        p1_ps = s.sem("p1_products")
        gelu = s.sem("gelu_done")
        p2_ps = s.sem("p2_products")
        out_done = s.sem("out_done")
        added = s.sem("x_added")
        STEPS = 8
        HALF = NT // 2

        with nc.Block(no_gpsimd_drain=True) as block:
            @block.tensor
            def _(pe):
                for g in range(NT // 2):
                    if g >= 6:
                        pe.wait_ge(kv_in, g - 5)
                    for j in range(2):
                        last = nc.tensor.matmul(ps[:, g % 6, 2 * P * j:2 * P * j + 2 * P], n[:, tile(2 * g + j)], w["kv"],
                                                start=True, stop=True)
                    last.then_inc(kv_ps, 1)
                for c in range(NC):
                    if c >= 2:
                        pe.wait_ge(q_in, c - 1)
                    nc.tensor.matmul(ps[:, 6 + c % 2], w["q"], n[:, chunk(c)], start=True, stop=True).then_inc(q_ps, 1)
                pe.wait_ge(kv_in, NT // 2)
                for t in range(NT):
                    pe.wait_ge(step, STEPS * (t // HALF + 1))
                    last = nc.tensor.matmul(ps[:, 0, 0:P], kv[:, t, 0].rearrange("p g d -> p (g d)"),
                                            kv[:, t, 1].rearrange("p g d -> p (g d)"), start=(t == 0),
                                            stop=(t == NT - 1))
                last.then_inc(head_ps, 1)
                pe.wait_ge(head_done, 2)
                pe.wait_ge(q_in, NC)
                for c in range(NC):
                    nc.tensor.matmul(ps[:, 1 + c], head[:, 1], q[:, chunk(c)], start=True, stop=True).then_inc(att_ps, 1)
                for c in range(NC):
                    pe.wait_ge(att_done, c + 1)
                    nc.tensor.matmul(ps[:, 1 + c], w["p1"], att[:, chunk(c)], start=True, stop=True).then_inc(p1_ps, 1)
                for c in range(NC):
                    pe.wait_ge(gelu, c + 1)
                    nc.tensor.matmul(ps[:, 1 + c], w["p2"], h[:, chunk(c)], start=True, stop=True).then_inc(p2_ps, 1)

            @block.scalar
            def _(act):
                for half in range(2):
                    t = slice(HALF * half, HALF * half + HALF)
                    act.wait_ge(step, STEPS * half + 3)
                    nc.scalar.activation(sq[:, t], cen[:, t], ACT.Square).then_inc(squared, 1)
                    act.wait_ge(step, STEPS * half + 4)
                    nc.scalar.activation(std[:, t], var[:, t], ACT.Sqrt, bias=const["eps"][:],
                                         scale=1.0 / HD).then_inc(rooted, 1)
                for c in range(NC):
                    act.wait_ge(p1_ps, c + 1)
                    nc.scalar.activation(h[:, chunk(c)], ps[:, 1 + c], ACT.Gelu, bias=vec["p1_b"]).then_inc(gelu, 1)

            @block.vector
            def _(dve):
                for g in range(NT // 2):
                    dve.wait_ge(kv_ps, g + 1)
                    nc.vector.tensor_tensor(kv[:, 2 * g:2 * g + 2].rearrange("p t k g d -> p t (k g d)"),
                                            ps[:, g % 6].rearrange("p (t e) -> p t e", t=2),
                                            w["kv_b"][:, None, :].broadcast_to([P, 2, 2 * P]), ALU.add).then_inc(kv_in, 1)
                for c in range(NC):
                    dve.wait_ge(q_ps, c + 1)
                    nc.vector.tensor_scalar(q[:, chunk(c)], ps[:, 6 + c % 2], vec["q_b"], None, ALU.add).then_inc(q_in, 1)
                dve.wait_ge(kv_in, NT // 2)

                def spread(a, t):
                    return a[:, t].rearrange("p t k g -> p (t k g)")[:, :, None].broadcast_to([P, HALF * 2 * GH, HD])

                def flat(a, t):
                    return a[:, t].rearrange("p t k g d -> p (t k g) d")

                for half in range(2):
                    t = slice(HALF * half, HALF * half + HALF)
                    b = STEPS * half
                    nc.vector.tensor_reduce(mean[:, t], kv[:, t], AX_X, ALU.add).then_inc(step, 1)
                    dve.wait_ge(step, b + 1)
                    nc.vector.tensor_scalar(mean[:, t], mean[:, t], 1.0 / HD, None, ALU.mult).then_inc(step, 1)
                    dve.wait_ge(step, b + 2)
                    nc.vector.tensor_tensor(flat(cen, t), flat(kv, t), spread(mean, t), ALU.subtract).then_inc(step, 1)
                    dve.wait_ge(squared, half + 1)
                    nc.vector.tensor_reduce(var[:, t], sq[:, t], AX_X, ALU.add).then_inc(step, 1)
                    dve.wait_ge(rooted, half + 1)
                    nc.vector.reciprocal(rstd[:, t], std[:, t]).then_inc(step, 1)
                    dve.wait_ge(step, b + 5)
                    nc.vector.tensor_tensor(flat(sq, t), flat(cen, t), spread(rstd, t), ALU.mult).then_inc(step, 1)
                    dve.wait_ge(step, b + 6)
                    for k in range(2):
                        view = lambda a: a[:, t, k].rearrange("p t g d -> p t (g d)")
                        gain = w["gain"][:, 2 * k, None, :].broadcast_to([P, HALF, P])
                        shift = w["gain"][:, 2 * k + 1, None, :].broadcast_to([P, HALF, P])
                        nc.vector.tensor_tensor(view(cen), view(sq), gain, ALU.mult).then_inc(gained, 1)
                        dve.wait_ge(gained, 2 * half + k + 1)
                        nc.vector.tensor_tensor(view(kv), view(cen), shift, ALU.add).then_inc(step, 1)
                dve.wait_ge(head_ps, 1)
                nc.vector.scalar_tensor_tensor(head[:, 0], ps[:, 0, 0:P], vec["temp"], w["head_mask"], ALU.mult,
                                               ALU.mult).then_inc(head_done, 1)
                dve.wait_ge(head_done, 1)
                nc.vector.scalar_tensor_tensor(head[:, 1], head[:, 0], 1.0 / T, w["att_bias"], ALU.mult,
                                               ALU.add).then_inc(head_done, 1)
                for c in range(NC):
                    dve.wait_ge(att_ps, c + 1)
                    nc.vector.tensor_tensor(att[:, chunk(c)], ps[:, 1 + c], n[:, chunk(c)], ALU.add).then_inc(att_done, 1)
                for c in range(NC):
                    dve.wait_ge(p2_ps, c + 1)
                    nc.vector.scalar_tensor_tensor(o[:, chunk(c)], ps[:, 1 + c], vec["p2_b"], n[:, chunk(c)], ALU.add,
                                                   ALU.add).then_inc(out_done, 1)
                for c in range(NC):
                    dve.wait_ge(out_done, c + 1)
                    nc.vector.tensor_tensor(x[:, chunk(c)], o[:, chunk(c)], x[:, chunk(c)], ALU.add).then_inc(added, 1)





def gated_projections(nc, const, n, xn, w, vec, q, k, v_ext):
    with ExitStack() as stack:
        s = Scope(nc, stack, "gp")
        xg = s.sb("gained", [P, T])
        gate = s.sb("gate", [P, T])
        gsum = s.sb("gate_mean", [P, T])
        rsum = s.sb("r_gate_mean", [P, T])
        gn = s.sb("gate_normed", [P, T])
        lin = s.sb("linear", [P, 2, T])
        low = s.sb("below_zero", [P, 2, T])
        ex = s.sb("exp", [P, 2, T])
        ps = s.ps("acc", [P, 8, CW])
        gained = s.sem("gained")
        gate_ps = s.sem("gate_products")
        gated = s.sem("gated")
        mean_ps = s.sem("mean_products")
        mean_in = s.sem("mean_in")
        inverted = s.sem("inverted")
        normed = s.sem("gate_normed")
        qk_ps = s.sem("qk_products")
        lin_done = s.sem("linear_done")
        low_done = s.sem("low_done")
        ex_done = s.sem("exp_done")
        elu_done = s.sem("elu_done")
        v_ps = s.sem("v_products")
        v_in = s.sem("v_in")
        ones_in = s.sem("ones_in")
        items = [(m, c) for c in range(NC) for m in range(2)]
        with nc.Block(no_gpsimd_drain=True) as block:
            @block.tensor
            def _(pe):
                for c in range(NC):
                    nc.tensor.matmul(ps[:, c], w["gate"], n[:, chunk(c)], start=True, stop=True).then_inc(gate_ps, 1)
                for c in range(NC):
                    pe.wait_ge(gated, c + 1)
                    nc.tensor.matmul(ps[:, c], const["mean"][:], gate[:, chunk(c)], start=True, stop=True).then_inc(mean_ps, 1)
                for i, (m, c) in enumerate(items):
                    pe.wait_ge(gained, c + 1)
                    if i >= 4:
                        pe.wait_ge(lin_done, i - 3)
                    nc.tensor.matmul(ps[:, 4 + i % 4], (w["q"], w["k"])[m], xg[:, chunk(c)], start=True,
                                     stop=True).then_inc(qk_ps, 1)
                for g in range(4):
                    pe.wait_ge(mean_in, g + 1)
                    for j in range(4):
                        last = nc.tensor.matmul(ps[:, g, tile(j)], xg[:, tile(4 * g + j)], w["v"], start=True, stop=True)
                    last.then_inc(v_ps, 1)

            @block.scalar
            def _(act):
                for c in range(NC):
                    act.wait_ge(gate_ps, c + 1)
                    nc.scalar.activation(gate[:, chunk(c)], ps[:, c], ACT.Sigmoid, bias=vec["gate_b"]).then_inc(gated, 1)
                for i, (m, c) in enumerate(items):
                    act.wait_ge(low_done, i + 1)
                    nc.scalar.activation(ex[:, m, chunk(c)], low[:, m, chunk(c)], ACT.Exp).then_inc(ex_done, 1)

            @block.gpsimd
            def _(pool):
                nc.gpsimd.memset(v_ext[:, :, P:2 * P], 1.0).then_inc(ones_in, 1)

            @block.vector
            def _(dve):
                for c in range(NC):
                    nc.vector.tensor_scalar(xg[:, chunk(c)], xn[:, chunk(c)], vec["ln_g"], vec["ln_b"], ALU.mult,
                                            ALU.add).then_inc(gained, 1)
                for c in range(NC):
                    dve.wait_ge(mean_ps, c + 1)
                    nc.vector.tensor_scalar(gsum[:, chunk(c)], ps[:, c], EPS, None, ALU.add).then_inc(mean_in, 1)
                    dve.wait_ge(mean_in, c + 1)
                    nc.vector.reciprocal(rsum[:, chunk(c)], gsum[:, chunk(c)]).then_inc(inverted, 1)
                    dve.wait_ge(inverted, c + 1)
                    nc.vector.tensor_tensor(gn[:, chunk(c)], gate[:, chunk(c)], rsum[:, chunk(c)],
                                            ALU.mult).then_inc(normed, 1)
                for i, (m, c) in enumerate(items):
                    dve.wait_ge(qk_ps, i + 1)
                    dve.wait_ge(normed, c + 1)
                    nc.vector.scalar_tensor_tensor(lin[:, m, chunk(c)], ps[:, 4 + i % 4], (vec["q_b"], vec["k_b"])[m],
                                                   gn[:, chunk(c)], ALU.add, ALU.mult).then_inc(lin_done, 1)
                    dve.wait_ge(lin_done, i + 1)
                    nc.vector.tensor_scalar(low[:, m, chunk(c)], lin[:, m, chunk(c)], 0.0, None,
                                            ALU.min).then_inc(low_done, 1)
                for g in range(4):
                    dve.wait_ge(v_ps, g + 1)
                    nc.vector.tensor_tensor(v_ext[:, 4 * g:4 * g + 4, 0:P], ps[:, g].rearrange("p (t e) -> p t e", t=4),
                                            w["v_b"][:, None, :].broadcast_to([P, 4, P]), ALU.add).then_inc(v_in, 1)
                for i, (m, c) in enumerate(items):
                    dve.wait_ge(ex_done, i + 1)
                    nc.vector.scalar_tensor_tensor((q, k)[m][:, chunk(c)], lin[:, m, chunk(c)], 0.0, ex[:, m, chunk(c)],
                                                   ALU.max, ALU.add).then_inc(elu_done, 1)


def linear_attention(nc, const, x, q, k, v_ext, w, vec):
    with ExitStack() as stack:
        s = Scope(nc, stack, "la")
        k_tile = s.sb("k_tile", [P, 2, P])
        v_pad = s.sb("v_padded", [P, 2, HEADS, 32])
        k_tok = s.sb("k_by_token", [P, 2, P])
        q_spread = s.sb("q_spread", [P, 2, HEADS, P])
        prod = s.sb("products", [P, 2, HEADS, P])
        state = s.sb("state", [P, 2, 2 * P])
        nd = s.sb("num_den", [P, 2, T])
        rden = s.sb("r_den", [P, T])
        att = s.sb("attended", [P, T])
        qk = s.ps("qk", [P, 4, CW])
        nd_ps = s.ps("num_den_acc", [P, 2, CW])
        st_ps = s.ps("state_acc", [P, CW])
        kt_ps = s.ps("k_turned", [P, CW])

        cleared = s.sem("cleared")
        staged = s.sem("staged")
        spread = s.sem("q_spread")
        qk_ps = s.sem("qk_products")
        turned = s.sem("k_turned")
        tok_in = s.sem("k_tok_in")
        masked = s.sem("masked")
        nd_done = s.sem("num_den_products")
        nd_out = s.sem("num_den_out")
        st_done = s.sem("state_products")
        st_out = s.sem("state_out")
        inverted = s.sem("inverted")
        scaled = s.sem("scaled")
        projected = s.sem("projected")
        added = s.sem("x_added")
        COPIES = 5

        def loop(eng, emit):
            for step in (-1, 0, 1):
                emit(step, 0)
            with eng.Fori(0, NT // 2 - 2) as i:
                for step in (2, 3):
                    emit(step, 2 * i)
            for step in (NT - 2, NT - 1):
                emit(step, 0)

        def has(step, base, shift):
            return not isinstance(base, int) or 0 <= step + base + shift < NT

        with nc.Block(no_gpsimd_drain=True) as block:
            @block.gpsimd
            def _(pool):
                nc.gpsimd.memset(v_pad[:], 0.0).then_inc(cleared, 1)
                pool.wait_ge(cleared, 1)

                def emit(step, base):
                    if not has(step, base, 1):
                        return
                    t, b = base + step + 1, (step + 1) % 2
                    if not (isinstance(t, int) and t < 2):
                        pool.wait_ge(turned, t - 1)
                        pool.wait_ge(nd_done, t - 1)
                    pool.wait_ge(cleared, 1)
                    nc.gpsimd.tensor_copy(k_tile[:, b], k[:, bass.ts(t, P)]).then_inc(staged, 1)
                    for r in range(4):
                        src = v_ext[:, bass.ts(t, 1), 0:P].rearrange("p o (j r d) -> p (o j) r d", j=4, r=4)[:, :, r]
                        nc.gpsimd.tensor_copy(v_pad[:, b, 4 * r:4 * r + 4, HD * r:HD * r + HD], src).then_inc(staged, 1)

                loop(pool, emit)

            @block.tensor
            def _(pe):
                pe.wait_ge(cleared, 1)

                def emit(step, base):
                    if has(step, base, 1):
                        t, b = base + step + 1, (step + 1) % 2
                        pe.wait_ge(spread, t + 1)
                        pe.wait_ge(staged, COPIES * (t + 1))
                        if not (isinstance(t, int) and t < 1):
                            pe.wait_ge(masked, t)
                            pe.wait_ge(tok_in, t)
                        for g in range(4):
                            last = nc.tensor.matmul(qk[:, g], k_tile[:, b], q_spread[:, b, 4 * g:4 * g + 4]
                                                    .rearrange("p h q -> p (h q)"), start=True, stop=True)
                        last.then_inc(qk_ps, 1)
                        nc.tensor.transpose(kt_ps[:, 0:P], k_tile[:, b], const["ident"][:]).then_inc(turned, 1)
                    if has(step, base, 0):
                        t, b = base + step, step % 2
                        pe.wait_ge(masked, t + 1)
                        pe.wait_ge(st_out, t + 1)
                        if not (isinstance(t, int) and t < 2):
                            pe.wait_ge(nd_out, 2 * (t - 1))
                        for m in range(2):
                            nc.tensor.matmul(nd_ps[:, b, tile(m)], state[:, b, tile(m)], q[:, bass.ts(t, P)],
                                             start=(m == 0), stop=False, skip_group_check=True)
                        for m in range(2):
                            for pos in range(HEADS):
                                j = pos % 4
                                h = pos // 4 + 4 * j
                                lhs = v_pad[:, b, pos] if m == 0 else w["ones_pad"][:, pos]
                                last = nc.tensor.matmul(nd_ps[32 * j:32 * j + 32, b, tile(m)], lhs, prod[:, b, h],
                                                        start=False, stop=(pos >= 12), skip_group_check=True)
                        last.then_inc(nd_done, 1)
                        pe.wait_ge(tok_in, t + 1)
                        nc.tensor.matmul(st_ps[:, 0:2 * P], k_tok[:, b], v_ext[:, bass.ts(t, 1)].rearrange("p o e -> p (o e)"),
                                         start=False, stop=False, skip_group_check=True).then_inc(st_done, 1)

                nc.tensor.matmul(st_ps[:, 0:2 * P], const["zero_bf"], const["zero_bf2"], start=True, stop=False,
                                 skip_group_check=True)
                loop(pe, emit)
                for c in range(NC):
                    pe.wait_ge(scaled, c + 1)
                    nc.tensor.matmul(qk[:, c], w["proj"], att[:, chunk(c)], start=True, stop=True).then_inc(projected, 1)

            @block.scalar
            def _(act):
                def emit(step, base):
                    if has(step, base, 0):
                        t, b = base + step, step % 2
                        act.wait_ge(nd_done, t + 1)
                        nc.scalar.activation(nd[:, 0, bass.ts(t, P)], nd_ps[:, b, tile(0)], ACT.Copy).then_inc(nd_out, 1)
                        nc.scalar.activation(nd[:, 1, bass.ts(t, P)], nd_ps[:, b, tile(1)], ACT.Identity,
                                             bias=const["eps"][:]).then_inc(nd_out, 1)
                    if has(step, base, 1):
                        t, b = base + step + 1, (step + 1) % 2
                        act.wait_ge(turned, t + 1)
                        if not (isinstance(t, int) and t < 2):
                            act.wait_ge(st_done, t - 1)
                        nc.scalar.activation(k_tok[:, b], kt_ps[:, 0:P], ACT.Copy).then_inc(tok_in, 1)

                loop(act, emit)

            @block.vector
            def _(dve):
                nc.vector.memset(state[:, 0], 0.0).then_inc(st_out, 1)

                def spread_q(t, b):
                    if not (isinstance(t, int) and t < 2):
                        dve.wait_ge(qk_ps, t - 1)
                    nc.vector.tensor_tensor(q_spread[:, b], q[:, bass.ts(t, P)][:, None, :].broadcast_to([P, HEADS, P]),
                                            w["head_cols"][:, :, None].broadcast_to([P, HEADS, P]),
                                            ALU.mult).then_inc(spread, 1)

                spread_q(0, 0)

                def emit(step, base):
                    if has(step, base, 2):
                        spread_q(base + step + 2, step % 2)
                    if has(step, base, 1):
                        t, b = base + step + 1, (step + 1) % 2
                        dve.wait_ge(qk_ps, t + 1)
                        if not (isinstance(t, int) and t < 2):
                            dve.wait_ge(nd_done, t - 1)
                        nc.vector.tensor_tensor(prod[:, b], qk[:].rearrange("p g (h q) -> p (g h) q", h=4),
                                                const["causal"][:, None, :].broadcast_to([P, HEADS, P]),
                                                ALU.mult).then_inc(masked, 1)
                    if has(step, base, 0) and has(step, base, 1):
                        t, b = base + step, step % 2
                        dve.wait_ge(st_done, t + 1)
                        nc.vector.tensor_tensor(state[:, 1 - b], st_ps[:, 0:2 * P], w["head_mask2"],
                                                ALU.mult).then_inc(st_out, 1)

                loop(dve, emit)
                for c in range(NC):
                    dve.wait_ge(nd_out, 2 * (4 * c + 4))
                    nc.vector.reciprocal(rden[:, chunk(c)], nd[:, 1, chunk(c)]).then_inc(inverted, 1)
                    dve.wait_ge(inverted, c + 1)
                    nc.vector.tensor_tensor(att[:, chunk(c)], nd[:, 0, chunk(c)], rden[:, chunk(c)],
                                            ALU.mult).then_inc(scaled, 1)
                for c in range(NC):
                    dve.wait_ge(projected, c + 1)
                    nc.vector.scalar_tensor_tensor(x[:, chunk(c)], qk[:, c], vec["proj_b"], x[:, chunk(c)], ALU.add,
                                                   ALU.add).then_inc(added, 1)



class Loads:

    def __init__(self, nc, scope, dram, names, label):
        self.nc, self.dram, self.names = nc, dram, names
        self.sem = scope.sem(f"{label}_loaded")
        self.tiles = {k: scope.sb(f"w_{k}", list(dram[k].shape), dram[k].dtype) for k in names}

    def start(self):
        with self.nc.Block(no_gpsimd_drain=True) as block:
            @block.sync
            def _(sp):
                for k in self.names:
                    sp.dma_start(self.tiles[k][:], self.dram[k]).then_inc(self.sem, 16)

    def finish(self):
        with self.nc.Block(no_gpsimd_drain=True) as block:
            @block.sync
            def _(sp):
                sp.wait_ge(self.sem, 16 * len(self.names))
        return self.tiles


CONST_NAMES = ("mean", "ones", "ident", "eps", "causal", "ident_bf", "neg_ident_bf", "mask_q", "mask_k", "zeros_bf")


def build(nc, dram, out):
    q_part_scratch = nc.dram_tensor("part_scratch", (2, PARTS, P, T), BF16, kind="Internal").ap()
    k_scratch = nc.dram_tensor("k_scratch", (2, KROWS, PAIRS_H, T), BF16, kind="Internal").ap()
    with ExitStack() as stack:
        s = Scope(nc, stack, "net")
        x = s.sb("x", [P, T])
        n_pad = s.sb("normed", [P, T + 1])
        n = n_pad[:, 1:T + 1]
        norm = Norm(s)
        x_loaded = s.sem("x_loaded")
        n_cleared = s.sem("n_cleared")
        stored = s.sem("stored")
        consts = Loads(nc, s, dram, CONST_NAMES, "const")
        consts.start()
        with nc.Block(no_gpsimd_drain=True) as block:
            @block.sync
            def _(sp):
                sp.dma_start(x[:], dram["x"]).then_inc(x_loaded, 16)
                sp.wait_ge(x_loaded, 16)

            @block.vector
            def _(dve):
                nc.vector.memset(n_pad[:, 0:1], 0.0).then_inc(n_cleared, 1)
                dve.wait_ge(n_cleared, 1)
        c = consts.finish()
        c["zero_bf"], c["zero_bf2"] = c["zeros_bf"][:, 0:P], c["zeros_bf"][:, 0:2 * P]
        c["ffn_runs"] = c["mix_runs"] = 0

        with ExitStack() as inner:
            trig = Loads(nc, Scope(nc, inner, "trig"), dram, ("trig",), "trig")
            trig.start()
            layernorm(nc, norm, c, x, n)
            tables = trig.finish()["trig"]
            attention_a(nc, c, x, n, dram["aa_pairs"], dram["aa_bias"], dram["aa_value_bias"], dram["aa_out_bias"],
                        tables)

        with ExitStack() as inner:
            weights = Loads(nc, Scope(nc, inner, "l0"), dram,
                            ("ff_gate1", "ff_gate2", "ff_gate_b2", "ff_vec", "ff_tb", "ff_w1", "ff_tw1", "ff_w2",
                             "ff_tw2", "ca_w", "ca_kv_b", "ca_gain", "ca_mats", "ca_vec"), "l0")
            weights.start()
            layernorm(nc, norm, c, x, n)
            w = weights.finish()
            ffn = dict(gate1=w["ff_gate1"][:], gate2=w["ff_gate2"][:], gate_b2=w["ff_gate_b2"][:], w1=w["ff_w1"][:],
                          w2=w["ff_w2"][:], tw1=w["ff_tw1"], tw2=w["ff_tw2"], tb=w["ff_tb"][:])
            ffn_vec = dict(gate_b1=w["ff_vec"][:, 0:1], ffn_b=w["ff_vec"][:, 1:FT + 2])
            modulated_ffn(nc, c, x, n, ffn, ffn_vec)
            layernorm(nc, norm, c, x, n)
            cw, cv = w["ca_w"], w["ca_vec"]
            channel_attention(nc, c, x, n,
                              dict(q=cw[:, 0:P], kv=cw[:, P:3 * P], p1=cw[:, 3 * P:4 * P], p2=cw[:, 4 * P:5 * P],
                                      kv_b=w["ca_kv_b"][:], gain=w["ca_gain"], head_mask=w["ca_mats"][:, 0:P],
                                      att_bias=w["ca_mats"][:, P:2 * P]),
                              dict(q_b=cv[:, 0:1], p1_b=cv[:, 1:2], p2_b=cv[:, 2:3], temp=cv[:, 3:4]))
            layernorm(nc, norm, c, x, n)
            modulated_ffn(nc, c, x, n, ffn, ffn_vec)

        with ExitStack() as inner:
            si = Scope(nc, inner, "l1a")
            weights = Loads(nc, si, dram, ("hs_w", "hs_vec", "hs_v_b"), "l1a")
            weights.start()
            layernorm(nc, norm, c, x, n)
            w = weights.finish()
            hw, hv = w["hs_w"], w["hs_vec"]
            q_stack = si.sb("q_stack", [P, PAIRS_H, T], BF16)
            v = si.sb("values", [P, NT, P])
            project_narrow(nc, n, hw[:, 0:P], hw[:, P:2 * P], hw[:, 2 * P:3 * P], hv[:, 0:1], hv[:, 1:2], w["hs_v_b"],
                           v, q_stack, q_part_scratch)
            stack_parts(nc, q_stack, q_part_scratch, k_scratch)
            softmax_over_heads(nc, c, x, q_stack, v, k_scratch, hw[:, 3 * P:4 * P], hv[:, 2:3])

        with ExitStack() as inner:
            si = Scope(nc, inner, "l1b")
            weights = Loads(nc, si, dram, ("mix_w", "mix_mu", "la_w", "la_vec", "la_v_b", "la_mask", "la_head_cols",
                                           "la_ones_pad"), "l1b")
            weights.start()
            layernorm(nc, norm, c, x, n)
            w = weights.finish()
            mw = w["mix_w"]
            mix = dict(r=mw[:, 0:P], k=mw[:, P:2 * P], v=mw[:, 2 * P:3 * P])
            mix_ffn(nc, c, x, n_pad, mix, w["mix_mu"][:])
            layernorm(nc, norm, c, x, n)
            with ExitStack() as deep:
                sd = Scope(nc, deep, "gla")
                xn = sd.sb("normed_twice", [P, T])
                q = sd.sb("q", [P, T])
                k = sd.sb("k", [P, T])
                v_ext = sd.sb("v_and_ones", [P, NT, 2 * P])
                layernorm(nc, norm, c, n, xn)
                lw, lv = w["la_w"], w["la_vec"]
                la = dict(q=lw[:, 0:P], k=lw[:, P:2 * P], v=lw[:, 2 * P:3 * P], gate=lw[:, 3 * P:4 * P],
                             proj=lw[:, 4 * P:5 * P], v_b=w["la_v_b"][:], head_mask2=w["la_mask"][:],
                             head_cols=w["la_head_cols"], ones_pad=w["la_ones_pad"])
                vec = dict(ln_g=lv[:, 0:1], ln_b=lv[:, 1:2], q_b=lv[:, 2:3], k_b=lv[:, 3:4], gate_b=lv[:, 4:5],
                              proj_b=lv[:, 5:6])
                gated_projections(nc, c, n, xn, la, vec, q, k, v_ext)
                linear_attention(nc, c, x, q, k, v_ext, la, vec)
            layernorm(nc, norm, c, x, n)
            mix_ffn(nc, c, x, n_pad, mix, w["mix_mu"][:])

        with nc.Block(no_gpsimd_drain=True) as block:
            @block.sync
            def _(sp):
                sp.dma_start(out, x[:]).then_inc(stored, 16)
                sp.wait_ge(stored, 16)



def shape_constants():
    f, b = np.float32, mybir.dt.np(BF16)
    masked = -1e30
    heads = np.kron(np.eye(HEADS), np.ones((HD, HD))).astype(f)
    ones_pad = np.zeros((P, HEADS, 32), f)
    for pos in range(HEADS):
        ones_pad[:, pos, HD * (pos // 4):HD * (pos // 4) + HD] = 1
    half = KD // 2
    theta = (f(1.0) * f(10000.0) ** (np.arange(half, dtype=f) / f(half - 1))).astype(f)
    angle = (np.arange(T, dtype=f)[:, None] / theta[None]).astype(f)
    sin, cos = np.sin(angle).astype(f).T, np.cos(angle).astype(f).T
    return {
        "mean": np.full((P, P), 1.0 / P, f), "ones": np.ones((P, P), f), "ident": np.eye(P, dtype=f),
        "eps": np.full((P, 1), EPS, f), "causal": np.triu(np.ones((P, P), f)),
        "ident_bf": np.eye(P).astype(b), "neg_ident_bf": (-np.eye(P)).astype(b),
        "mask_q": np.triu(np.full((P, P), masked), 1).astype(b), "mask_k": np.tril(np.full((P, P), masked), -1).astype(b),
        "zeros_bf": np.zeros((P, 2 * P), b),
        "trig": np.stack([np.concatenate([cos] * 4, 0), np.concatenate([sin, -sin, sin, -sin], 0)], 1),
        "heads": heads, "la_mask": np.concatenate([heads, heads], 1),
        "la_head_cols": np.repeat(np.eye(HEADS, dtype=f), HD, 0), "la_ones_pad": ones_pad,
    }


def lay_out(a):
    d = shape_constants()
    heads = d.pop("heads")
    rows = lambda r: np.broadcast_to(r, (P,) + r.shape)
    cols = lambda *v: np.stack(v, 1)
    weights = lambda *w: np.concatenate([m.T for m in w], 1)
    d["x"] = a["L0_attn_a_x"][0].T

    w, b, w_out = a["L0_attn_a_W_in"], a["L0_attn_a_b_in"], a["L0_attn_a_W_out"]
    hw = HEADS * KD
    swap = np.arange(hw).reshape(HEADS, 2, KD // 2)[:, ::-1].reshape(-1)
    pairs, biases = [], []
    for p in range(PAIRS):
        r = slice(P * p, P * p + P)
        qk = [(w[o:o + hw][i], b[o:o + hw][i]) for o in (0, hw) for i in (np.arange(hw)[r], swap[r])]
        pairs += [m.T for m, _ in qk] + [w[2 * hw:][r].T, w_out[:, r].T]
        biases += [v for _, v in qk]
    d["aa_pairs"] = np.concatenate(pairs, 1)
    d["aa_bias"] = cols(*biases)
    d["aa_value_bias"] = rows(b[2 * hw:])
    d["aa_out_bias"] = a["L0_attn_a_b_out"][:, None]

    f = {k[len("L0_ffn_"):]: v for k, v in a.items() if k.startswith("L0_ffn_")}
    down = lambda m: m.T.reshape(FT, P, P).transpose(1, 0, 2).reshape(P, FF)
    d["ff_gate1"], d["ff_gate2"], d["ff_gate_b2"] = f["gate_w1"].T, f["gate_w2"].T, rows(f["gate_b2"])
    d["ff_vec"] = cols(f["gate_b1"], *f["b1"].reshape(FT, P), f["b2"])
    d["ff_tb"] = np.concatenate([f["Tb1"].T.reshape(FT, P, EXPERTS), f["Tb2"].T[None]], 0).transpose(1, 0, 2)
    d["ff_w1"], d["ff_w2"] = f["W1"].T, down(f["W2"])
    d["ff_tw1"] = f["TW1"].transpose(2, 0, 1).reshape(P, EXPERTS * FF)
    d["ff_tw2"] = np.concatenate([down(m) for m in f["TW2"]], 1)

    c = {k[len("L0_attn_b_"):]: v for k, v in a.items() if k.startswith("L0_attn_b_")}
    d["ca_w"] = weights(c["qkv_w"], c["p1_w"], c["p2_w"])
    d["ca_kv_b"] = rows(c["qkv_b"][P:])
    d["ca_gain"] = rows(np.stack([np.tile(c[k], HEADS) for k in ("kn_g", "kn_b", "vn_g", "vn_b")]))
    bias = np.zeros((P, P), c["attn_bias"].dtype)
    for h in range(HEADS):
        bias[HD * h:HD * h + HD, HD * h:HD * h + HD] = c["attn_bias"][h]
    d["ca_mats"] = np.concatenate([heads, bias], 1)
    d["ca_vec"] = cols(c["qkv_b"][:P], c["p1_b"], c["p2_b"], np.repeat(c["temperature"].reshape(-1), HD))

    h = {k[len("L1_attn_a_"):]: v for k, v in a.items() if k.startswith("L1_attn_a_")}
    d["hs_w"] = weights(h["Wq"], h["Wk"], h["Wv"], h["Wo"])
    d["hs_vec"] = cols(h["bq"], h["bk"], h["bo"])
    d["hs_v_b"] = rows(h["bv"])

    m = {k[len("L1_ffn_"):]: v for k, v in a.items() if k.startswith("L1_ffn_")}
    d["mix_w"], d["mix_mu"] = weights(m["W_r"], m["W_k"], m["W_v"]), cols(m["mu_r"], m["mu_k"])

    g = {k[len("L1_attn_b_"):]: v for k, v in a.items() if k.startswith("L1_attn_b_")}
    d["la_w"] = weights(g["qkv_w"], g["gate_w"], g["proj_w"])
    d["la_vec"] = cols(g["ln_g"], g["ln_b"], g["qkv_b"][:P], g["qkv_b"][P:2 * P], g["gate_b"], g["proj_b"])
    d["la_v_b"] = rows(g["qkv_b"][2 * P:])
    return {k: np.ascontiguousarray(v) for k, v in d.items()}


def kernel(**inputs):
    import concourse.bacc as bacc
    from concourse.bass_utils import run_bass_kernel_spmd

    arrays = lay_out({k: np.asarray(v) for k, v in inputs.items()})
    nc = bacc.Bacc("TRN2", target_bir_lowering=False, num_devices=1)
    dram = {k: nc.dram_tensor(f"in_{k}", v.shape, mybir.dt.from_np(v.dtype), kind="ExternalInput").ap()
            for k, v in arrays.items()}
    out = nc.dram_tensor("out_x", (P, T), F32, kind="ExternalOutput").ap()
    build(nc, dram, out)
    result = run_bass_kernel_spmd(nc, [{f"in_{k}": v for k, v in arrays.items()}], core_ids=[0])
    return np.ascontiguousarray(result.results[0]["out_x"].T)[None]
```

```python
from contextlib import ExitStack

import numpy as np
import concourse.bass as bass
from concourse import mybir

ALU = mybir.AluOpType
ACT = mybir.ActivationFunctionType
AX_X = mybir.AxisListType.X
F32 = mybir.dt.float32
F32R = mybir.dt.float32r
BF16 = mybir.dt.bfloat16

P = 128
T = 2048
CW = 512
NC = T // CW
NT = T // P
EPS = 1e-5
HEADS = 16


class Scope:

    def __init__(self, nc, stack, prefix):
        self.nc, self.stack, self.prefix = nc, stack, prefix

    def sb(self, name, shape, dt=F32):
        return self.stack.enter_context(self.nc.sbuf_tensor(f"{self.prefix}_{name}", shape, dt))

    def ps(self, name, shape, dt=F32):
        return self.stack.enter_context(self.nc.psum_tensor(f"{self.prefix}_{name}", shape, dt))

    def sem(self, name):
        return self.stack.enter_context(self.nc.semaphore(f"{self.prefix}_{name}"))


def chunk(c):
    return slice(c * CW, (c + 1) * CW)


def tile(t):
    return slice(t * P, (t + 1) * P)



class Norm:

    def __init__(self, scope):
        self.mean, self.centred, self.squared, self.var, self.std, self.diag, self.spread, self.out, self.recip = (
            scope.sem(n) for n in ("mean", "centred", "squared", "var", "std", "diag", "spread", "out", "recip"))
        self.runs = 0


def layernorm(nc, norm, const, x, out):
    b = NC * norm.runs
    norm.runs += 1
    with ExitStack() as stack:
        s = Scope(nc, stack, f"ln{norm.runs}")
        cen = s.sb("centred", [P, T])
        sq = s.sb("squared", [P, T])
        std = s.sb("std", [P, NC, 4])
        rstd = s.sb("rstd", [P, NC, 4])
        diag = s.sb("diag", [P, NC, 4, P])
        spread = s.ps("spread", [P, NC, CW])
        var = s.ps("var", [P, NC, CW])

        with nc.Block(no_gpsimd_drain=True) as block:
            @block.tensor
            def _(pe):
                def variances(c):
                    pe.wait_ge(norm.squared, b + c + 1)
                    for j in range(4):
                        last = nc.tensor.matmul(var[:, c, j:j + 1], sq[:, tile(4 * c + j)], const["mean"][:, 0:1],
                                                start=True, stop=True)
                    last.then_inc(norm.var, 1)

                def spread_out(c):
                    pe.wait_ge(norm.diag, b + c + 1)
                    nc.tensor.matmul(spread[:, c], const["ones"][:], diag[:, c].rearrange("p j q -> p (j q)"),
                                     start=True, stop=True).then_inc(norm.spread, 1)

                for c in range(NC):
                    nc.tensor.matmul(spread[:, c], const["mean"][:], x[:, chunk(c)],
                                     start=True, stop=True).then_inc(norm.mean, 1)
                variances(0)
                for c in range(1, NC):
                    variances(c)
                    spread_out(c - 1)
                spread_out(NC - 1)

            @block.scalar
            def _(act):
                def square(c):
                    act.wait_ge(norm.centred, b + c + 1)
                    nc.scalar.activation(sq[:, chunk(c)], cen[:, chunk(c)], ACT.Square).then_inc(norm.squared, 1)

                def root(c):
                    act.wait_ge(norm.var, b + c + 1)
                    nc.scalar.activation(std[:, c], var[:, c, 0:4], ACT.Sqrt, bias=const["eps"][:]).then_inc(norm.std, 1)

                square(0)
                for c in range(1, NC):
                    square(c)
                    root(c - 1)
                root(NC - 1)

            @block.vector
            def _(dve):
                def diagonal(c):
                    dve.wait_ge(norm.std, b + c + 1)
                    nc.vector.reciprocal(rstd[:, c], std[:, c]).then_inc(norm.recip, 1)
                    dve.wait_ge(norm.recip, b + c + 1)
                    nc.vector.tensor_tensor(diag[:, c], const["ident"][:, None, :].broadcast_to([P, 4, P]),
                                            rstd[:, c, :, None].broadcast_to([P, 4, P]),
                                            ALU.mult).then_inc(norm.diag, 1)

                def scale(c):
                    dve.wait_ge(norm.spread, b + c + 1)
                    dve.wait_ge(norm.centred, b + c + 1)
                    nc.vector.tensor_tensor(out[:, chunk(c)], spread[:, c], cen[:, chunk(c)],
                                            ALU.mult).then_inc(norm.out, 1)

                for c in range(NC):
                    dve.wait_ge(norm.mean, b + c + 1)
                    nc.vector.tensor_tensor(cen[:, chunk(c)], x[:, chunk(c)], spread[:, c],
                                            ALU.subtract).then_inc(norm.centred, 1)
                diagonal(0)
                for c in range(1, NC):
                    diagonal(c)
                    scale(c - 1)
                scale(NC - 1)



KD = 64
PAIRS = HEADS * KD // P
MAX_W = 2 * CW
SLOTS = 3
PROBS = 5
LAG = 2
PAIR_COLS = 6 * P


def pair_schedule(following):
    ahead = {}

    def place(c, kts, items):
        for k, item in enumerate(items):
            ahead.setdefault((c, kts[k * len(kts) // len(items)]), []).append(item)

    place(0, range(0, 4), prepare(2))
    place(1, range(0, 4), maxima(2))
    place(1, [4], [TURN[2]])
    place(1, range(4, 8), prepare(3))
    place(2, range(0, 8), maxima(3))
    place(2, [8], [TURN[3]])
    if following:
        place(3, range(4, 8), prepare(0))
        place(3, range(8, 10), maxima(0))
        place(3, range(9, 11), prepare(1))
        place(3, [11], [TURN[0]])
        place(3, range(12, 16), maxima(1)[:8])

    plan = []
    for c in range(NC):
        keys = 4 * c + 4
        for kt in range(keys):
            plan.append(("score", "act", c, kt))
            if kt >= LAG:
                plan.append(("value", None, c, kt - LAG))
            elif c:
                plan.append(("value", None, c - 1, 4 * c + kt - LAG))
            if c and kt == DEN_STEP:
                plan.append(("den", "act", c - 1))
            if c and kt == OUT_STEP:
                plan.append(("out", "dve", c - 1))
            plan += ahead.get((c, kt), [])
    last = [TURN[1]] if following else []
    for item in [("value", None, NC - 1, NT - 2), ("value", None, NC - 1, NT - 1), ("den", "act", NC - 1),
                 ("out", "dve", NC - 1)]:
        plan += last[:2]
        last = last[2:]
        plan.append(item)
    return plan


def prepare(c):
    return [("rope", "dve", 1, c), ("rope", "dve", 0, c), ("v", "dve", c), ("hi", None, 1, c), ("hi", None, 0, c),
            ("lo", None, 1, c), ("lo", None, 0, c)]


def maxima(c):
    return [("max", "dve", h, qt, g) for qt in range(4 * c, 4 * c + 4) for h in range(2) for g in range(qt // 8 + 1)]


DEN_STEP = LAG
OUT_STEP = LAG + 1
TURN = [("turn", "act", c) for c in range(NC)]


def added_to(c, kt):
    return (c, kt + 2) if c and kt < 2 else (c, kt)


def last_maximum(c):
    return maxima(c)[-1]


INCREMENTS = {
    "filled": lambda p: 1 if p[1] else 0,
    "dve_read": lambda p: 1 if p[1] == "dve" else 0,
    "act_read": lambda p: 1 if p[1] == "act" else 0,
    "rotated": lambda p: 1 if p[0] == "rope" else 0,
    "hi_done": lambda p: 4 if p[0] == "hi" else 0,
    "lo_done": lambda p: 2 if p[0] == "lo" else 0,
    "max_done": lambda p: 1 if p[0] == "max" and p == last_maximum(p[3] // 4) else 0,
    "row_loaded": lambda p: 32 if p[0] == "turn" else 0,
    "value_done": lambda p: 1 if p[0] == "value" else 0,
    "pool_added": lambda p: 1 if p[0] == "value" and p[3] % 2 == 0 and added_to(*p[2:]) == p[2:] else 0,
    "dve_added": lambda p: 1 if p[0] == "value" and p[3] % 2 == 1 and added_to(*p[2:]) == p[2:] else 0,
    "cleared": lambda p: 1 if p[0] == "value" and p[2:] == (0, 1) else 0,
    "rden_done": lambda p: 1 if p[0] == "den" else 0,
    "y_done": lambda p: 1 if p[0] == "den" else 0,
}


class Section:

    def __init__(self, plan, start, turn=None, i=0):
        self.plan, self.start, self.turn, self.i = plan, start, turn, i
        self.fills = [p for p in plan if p[1]]
        self.scores = [p for p in plan if p[0] == "score"]

    def within(self, i):
        return Section(self.plan, self.start, self.turn, i)

    def before(self, sem):
        return self.start[sem] + (self.i * self.turn[sem] if self.turn else 0)

    def after(self, sem, step, pos=None):
        at = self.plan.index(step) if step in self.plan else None
        if at is None or (pos is not None and at >= pos):
            return self.before(sem)
        return self.before(sem) + sum(INCREMENTS[sem](p) for p in self.plan[:at + 1])


def attention_a(nc, const, x, n, w_pairs, bias_pairs, value_bias, out_bias, trig):
    first_plan = prepare(0) + prepare(1) + maxima(0) + [TURN[0]] + maxima(1) + [TURN[1]]
    loop_plan = pair_schedule(True)
    last_plan = pair_schedule(False)
    per_turn = {sem: sum(inc(p) for p in loop_plan) for sem, inc in INCREMENTS.items()}
    at_loop = {sem: sum(inc(p) for p in first_plan) for sem, inc in INCREMENTS.items()}
    lead = Section(first_plan, {sem: 0 for sem in INCREMENTS})
    body = Section(loop_plan, at_loop, per_turn)
    tail = Section(last_plan, {sem: at_loop[sem] + (PAIRS - 1) * per_turn[sem] for sem in INCREMENTS})

    def run(eng, section_of):
        section_of(lead)
        with eng.Fori(0, PAIRS - 1) as i:
            section_of(body.within(i))
        section_of(tail)

    def first(c, kt):
        return max(0, kt - 4 * c) * P

    with ExitStack() as stack:
        s = Scope(nc, stack, "aa")
        w = s.sb("weights", [P, 5 * P])
        wo = s.sb("out_weights", [P, P])
        bias = s.sb("bias", [P, 4])
        vbias = s.sb("value_bias", [P, P])
        cos, sin = trig[:, 0], trig[:, 1]
        obias = s.sb("out_bias", [P, 1])
        t1 = s.sb("turned", [P, 2, CW])
        t2 = s.sb("straight", [P, 2, CW])
        y = s.sb("rotated", [P, 2, CW])
        q_hi = [s.sb(f"q_hi{h}", [P, T], F32R) for h in range(2)]
        q_lo = [s.sb(f"q_lo{h}", [KD + 1, T], F32R) for h in range(2)]
        k_st = [s.sb(f"k_stack{h}", [P, T], F32R) for h in range(2)]
        k_one = [s.sb(f"k_one{h}", [KD + 1, T], F32R) for h in range(2)]
        v = s.sb("values", [P, NT, P])
        part = s.sb("part_max", [P, NC, 2, 4, 2])
        mx = s.sb("maxima", [P, NC, 2, 4])
        rows = s.sb("max_rows", [8, 2, P], F32R)
        probs = s.sb("probs", [P, PROBS, 2, CW])
        acc_p = s.sb("den_even", [P, 2, 2, CW])
        acc_d = s.sb("den_odd", [P, 2, 2, CW])
        zero = s.sb("zero", [P, 2])
        log_den = s.sb("log_den", [P, CW])
        rden = s.sb("rden", [P, CW])
        yv = s.sb("attended", [P, 2, CW])
        slot = s.ps("slot", [P, SLOTS, 2, CW])
        acc_y = s.ps("acc_y", [P, 2, CW])

        loaded = s.sem("weights_loaded")
        out_loaded = s.sem("out_weights_and_bias_loaded")
        filled = s.sem("slots_filled")
        dve_read = s.sem("slots_read_dve")
        act_read = s.sem("slots_read_act")
        turned = s.sem("rope_turned")
        rotated = s.sem("rope_rotated")
        hi_done = s.sem("hi_written")
        lo_done = s.sem("lo_written")
        max_done = s.sem("max_done")
        row_loaded = s.sem("max_rows_loaded")
        value_done = s.sem("value_products")
        pool_added = s.sem("added_even")
        dve_added = s.sem("added_odd")
        rden_done = s.sem("rden_done")
        y_done = s.sem("attended_done")
        prepared = s.sem("ones_and_zeros_prepared")
        cleared = s.sem("den_odd_cleared")
        x_biased = s.sem("x_biased")

        hi_rows = {0: slice(0, KD), 1: slice(KD, P)}

        def slot_of(sec, p):
            return slot[:, sec.fills.index(p) % SLOTS]

        def probs_of(sec, c, kt):
            return probs[:, sec.scores.index(("score", "act", c, kt)) % PROBS]

        with nc.Block(no_gpsimd_drain=True) as block:
            @block.sync
            def _(sp):
                def load(i):
                    sp.dma_start(w[:], w_pairs[:, bass.ts(i, PAIR_COLS)][:, 0:5 * P]).then_inc(loaded, 16)
                    sp.dma_start(bias[:], bias_pairs[:, bass.ts(i, 4)]).then_inc(loaded, 16)
                    sp.dma_start(vbias[:], value_bias[:, bass.ts(i, P)]).then_inc(loaded, 16)

                def load_out(i):
                    sp.dma_start(wo[:], w_pairs[:, bass.ts(i, PAIR_COLS)][:, 5 * P:]).then_inc(out_loaded, 16)

                load(0)
                sp.dma_start(obias[:], out_bias).then_inc(out_loaded, 16)
                load_out(0)

                def section(sec):
                    for p in sec.plan:
                        if p[0] == "turn":
                            c = p[2]
                            sp.wait_ge(act_read, sec.after("act_read", p))
                            for h in range(2):
                                dst = q_lo[h][KD:KD + 1, chunk(c)].rearrange("o (j q) -> o j q", j=4)
                                sp.dma_start(dst.bitcast(F32), rows[4 * h:4 * h + 4, c % 2, :].bitcast(F32))\
                                    .then_inc(row_loaded, 16)
                        elif p == ("v", "dve", NC - 1) and sec.turn:
                            sp.wait_ge(dve_read, sec.after("dve_read", p))
                            load(sec.i + 1)
                        elif p == ("out", "dve", NC - 1) and sec.turn:
                            sp.wait_ge(filled, sec.after("filled", p))
                            load_out(sec.i + 1)

                run(sp, section)

            @block.tensor
            def _(pe):
                pe.wait_ge(prepared, 3)

                def section(sec):
                    if sec is not lead:
                        pe.wait_ge(dve_read, sec.before("dve_read"))
                        pe.wait_ge(act_read, sec.before("act_read"))
                    for pos, p in enumerate(sec.plan):
                        kind = p[0]
                        if p[1]:
                            no = sec.fills.index(p)
                            if no >= SLOTS:
                                old = sec.fills[no - SLOTS]
                                if old[1] == "dve":
                                    pe.wait_ge(dve_read, sec.after("dve_read", old))
                                else:
                                    pe.wait_ge(act_read, sec.after("act_read", old))
                            sl = slot_of(sec, p)
                        if kind == "rope":
                            _, _, which, c = p
                            if c == 0 and which == 1:
                                pe.wait_ge(loaded, 48 if sec is lead else (sec.i + 2) * 48)
                            for b in range(2):
                                last = nc.tensor.matmul(sl[:, b], w[:, tile(2 * which + b)], n[:, chunk(c)],
                                                        start=True, stop=True)
                        elif kind == "v":
                            c = p[2]
                            for j in range(4):
                                last = nc.tensor.matmul(sl[:, 0, tile(j)], n[:, tile(4 * c + j)],
                                                        w[:, tile(4)], start=True, stop=True)
                        elif kind == "max":
                            _, _, h, qt, g = p
                            if p == maxima(qt // 4)[0]:
                                pe.wait_ge(hi_done, sec.after("hi_done", ("hi", None, 0, qt // 4), pos))
                            keys = min(MAX_W, (qt + 1) * P - g * MAX_W)
                            for b in range((keys + CW - 1) // CW):
                                m = min(CW, keys - b * CW)
                                k0 = g * MAX_W + b * CW
                                diagonal = k0 + m == (qt + 1) * P
                                last = nc.tensor.matmul(sl[:, b, 0:m], q_hi[h][hi_rows[h], tile(qt)], k_st[h][hi_rows[h], k0:k0 + m],
                                                        start=True, stop=not diagonal)
                                if diagonal:
                                    last = nc.tensor.matmul(sl[:, b, m - P:m], const["ident_bf"][:],
                                                            const["mask_q"][:], start=False, stop=True)
                        elif kind == "turn":
                            c = p[2]
                            pe.wait_ge(max_done, sec.after("max_done", last_maximum(c), pos))
                            last = nc.tensor.transpose(sl[0:8, 0, 0:P], mx[:, c].rearrange("p h j -> p (h j)"),
                                                       const["ident"][:])
                        elif kind == "score":
                            _, _, c, kt = p
                            if kt == 0:
                                pe.wait_ge(row_loaded, sec.after("row_loaded", TURN[c], pos))
                                pe.wait_ge(lo_done, sec.after("lo_done", ("lo", None, 0, c), pos))
                            a = first(c, kt)
                            q0 = c * CW + a
                            m = CW - a
                            diagonal = kt >= 4 * c
                            for h in range(2):
                                nc.tensor.matmul(sl[:, h, a:], k_st[h][:, tile(kt)], q_hi[h][:, q0:q0 + m],
                                                 start=True, stop=False)
                                last = nc.tensor.matmul(sl[:, h, a:], k_one[h][:, tile(kt)], q_lo[h][:, q0:q0 + m],
                                                        start=False, stop=not diagonal)
                                if diagonal:
                                    last = nc.tensor.matmul(sl[:, h, a:a + P], const["ident_bf"][:],
                                                            const["mask_k"][:], start=False, stop=True)
                        elif kind == "value":
                            _, _, c, kt = p
                            pe.wait_ge(act_read, sec.after("act_read", ("score", "act", c, kt)))
                            if kt == 0:
                                pe.wait_ge(y_done, sec.after("y_done", ("den", "act", (c - 2) % NC), pos))
                            if kt == 4 * c:
                                pe.wait_ge(dve_read, sec.after("dve_read", ("v", "dve", c), pos))
                            a = first(c, kt)
                            for h in range(2):
                                last = nc.tensor.matmul(acc_y[KD * h:KD * h + KD, c % 2, a:],
                                                        v[:, kt, KD * h:KD * h + KD], probs_of(sec, c, kt)[:, h, a:],
                                                        start=(kt == 0), stop=(kt == 4 * c + 3))
                            last.then_inc(value_done, 1)
                        elif kind == "den":
                            c = p[2]
                            pe.wait_ge(pool_added, sec.after("pool_added", ("value", None, c, 4 * c + 2)))
                            pe.wait_ge(dve_added, sec.after("dve_added", ("value", None, c, 4 * c + 3)))
                            if c == 0:
                                pe.wait_ge(cleared, sec.after("cleared", ("value", None, 0, 1)))
                            for h in range(2):
                                o = sl[KD * h:KD * h + KD, 0]
                                nc.tensor.matmul(o, const["ones"][:, 0:KD], acc_p[:, c % 2, h], start=True, stop=False)
                                last = nc.tensor.matmul(o, const["ones"][:, 0:KD], acc_d[:, c % 2, h],
                                                        start=False, stop=True)
                        elif kind == "out":
                            c = p[2]
                            if c == 0:
                                pe.wait_ge(out_loaded, 16 + ((sec.i if sec.turn else PAIRS - 1) + 1) * 16)
                            pe.wait_ge(y_done, sec.after("y_done", ("den", "act", c)))
                            last = nc.tensor.matmul(sl[:, 0], wo[:], yv[:, c % 2], start=True, stop=True)
                        if p[1]:
                            last.then_inc(filled, 1)

                run(pe, section)

            @block.scalar
            def _(act):
                nc.scalar.preload_act_table_set("natural_log_exp_and_others")

                def section(sec):
                    for pos, p in enumerate(sec.plan):
                        if p[0] == "hi":
                            _, _, which, c = p
                            act.wait_ge(rotated, sec.after("rotated", ("rope", "dve", which, c)))
                            for h in range(2):
                                src = y[KD * h:KD * h + KD, which]
                                if which == 0:
                                    outs = (q_hi[h][0:KD, chunk(c)], q_hi[h][KD:P, chunk(c)])
                                else:
                                    outs = (k_st[h][hi_rows[h], chunk(c)], k_one[h][0:KD, chunk(c)])
                                for o in outs:
                                    nc.scalar.activation(o, src, ACT.Copy).then_inc(hi_done, 1)
                        if p[1] != "act":
                            continue
                        sl = slot_of(sec, p)
                        if p[0] == "turn":
                            c = p[2]
                            act.wait_ge(filled, sec.after("filled", p))
                            if sec is not lead:
                                act.wait_ge(row_loaded, sec.after("row_loaded", TURN[(c - 2) % NC], pos))
                            nc.scalar.activation(rows[:, c % 2], sl[0:8, 0, 0:P], ACT.Copy,
                                                 scale=-1.0).then_inc(act_read, 1)
                        elif p[0] == "den":
                            act.wait_ge(filled, sec.after("filled", p))
                            nc.scalar.activation(log_den[:], sl[:, 0], ACT.Ln).then_inc(act_read, 1)
                            act.wait_ge(act_read, sec.after("act_read", p))
                            act.wait_ge(y_done, sec.after("y_done", ("den", "act", (p[2] - 1) % NC), pos))
                            nc.scalar.activation(rden[:], log_den[:], ACT.Exp, scale=-1.0).then_inc(rden_done, 1)
                        else:
                            _, _, c, kt = p
                            act.wait_ge(filled, sec.after("filled", p))
                            no = sec.scores.index(p)
                            if no < PROBS:
                                act.wait_ge(value_done, sec.before("value_done"))
                                act.wait_ge(pool_added, sec.before("pool_added"))
                                act.wait_ge(dve_added, sec.before("dve_added"))
                            else:
                                old = sec.scores[no - PROBS][2:]
                                act.wait_ge(value_done, sec.after("value_done", ("value", None) + old))
                                added = "pool_added" if old[1] % 2 == 0 else "dve_added"
                                act.wait_ge(pool_added if old[1] % 2 == 0 else dve_added,
                                            sec.after(added, ("value", None) + added_to(*old)))
                            a = first(c, kt)
                            nc.scalar.activation(probs_of(sec, c, kt)[:, :, a:], sl[:, :, a:], ACT.Exp,
                                                 scale=1.0 / 8.0).then_inc(act_read, 1)

                run(act, section)

            @block.gpsimd
            def _(pool):
                nc.gpsimd.memset(zero[:], 0.0).then_inc(prepared, 1)
                pool.wait_ge(prepared, 3)

                def section(sec):
                    adds, subtractions = sec.before("pool_added"), sec.before("lo_done")
                    for pos, p in enumerate(sec.plan):
                        if INCREMENTS["pool_added"](p):
                            _, _, c, kt = p
                            pool.wait_ge(pool_added, adds)
                            pool.wait_ge(lo_done, subtractions)
                            adds = sec.after("pool_added", p)
                            pool.wait_ge(act_read, sec.after("act_read", ("score", "act", c, kt)))
                            a = first(c, kt)
                            src = probs_of(sec, c, kt)[:, :, a:]
                            dst = acc_p[:, c % 2, :, a:]
                            if kt == 0 or (c and kt == 2):
                                pool.wait_ge(filled, sec.after("filled", ("den", "act", (c - 2) % NC), pos))
                            if kt == 0:
                                nc.gpsimd.tensor_tensor(dst, src, zero[:, :, None].broadcast_to([P, 2, CW]),
                                                        ALU.add).then_inc(pool_added, 1)
                            elif c and kt == 2:
                                nc.gpsimd.tensor_tensor(dst, probs_of(sec, c, 0), src,
                                                        ALU.add).then_inc(pool_added, 1)
                            else:
                                nc.gpsimd.tensor_tensor(dst, dst, src, ALU.add).then_inc(pool_added, 1)
                        elif p[0] == "lo":
                            _, _, which, c = p
                            pool.wait_ge(pool_added, adds)
                            for h in range(2):
                                pool.wait_ge(lo_done, subtractions)
                                subtractions = sec.after("lo_done", p) - 1 + h
                                pool.wait_ge(hi_done, sec.after("hi_done", ("hi", None, which, c)))
                                if which == 0:
                                    r = slice(KD * h, KD * h + KD)
                                    src_hi, o = q_hi[h][r, chunk(c)], q_lo[h][0:KD, chunk(c)]
                                else:
                                    src_hi, o = k_st[h][hi_rows[h], chunk(c)], k_st[h][hi_rows[1 - h], chunk(c)]
                                nc.gpsimd.tensor_tensor(o, y[KD * h:KD * h + KD, which], src_hi.bitcast(F32),
                                                        ALU.subtract).then_inc(lo_done, 1)

                run(pool, section)

            @block.vector
            def _(dve):
                for h in range(2):
                    nc.vector.memset(k_one[h][KD:KD + 1, :].bitcast(F32), 1.0).then_inc(prepared, 1)
                dve.wait_ge(out_loaded, 32)

                def section(sec):
                    def add(p, pos):
                        _, _, c, kt = p
                        dve.wait_ge(act_read, sec.after("act_read", ("score", "act", c, kt)))
                        dve.wait_ge(dve_added, sec.after("dve_added", p) - 1)
                        a = first(c, kt)
                        src = probs_of(sec, c, kt)[:, :, a:]
                        dst = acc_d[:, c % 2, :, a:]
                        if kt == 1:
                            nc.vector.memset(acc_d[:, c % 2, :, 0:a], 0.0).then_inc(cleared, 1)
                            nc.vector.tensor_copy(dst, src).then_inc(dve_added, 1)
                        elif kt == 3 and c:
                            dve.wait_ge(filled, sec.after("filled", ("den", "act", (c - 2) % NC), pos))
                            nc.vector.tensor_tensor(dst, probs_of(sec, c, 1), src, ALU.add).then_inc(dve_added, 1)
                        else:
                            nc.vector.tensor_tensor(dst, dst, src, ALU.add).then_inc(dve_added, 1)

                    for pos, p in enumerate(sec.plan):
                        kind = p[0]
                        if INCREMENTS["dve_added"](p):
                            add(p, pos)
                        if kind == "den":
                            c = p[2]
                            dve.wait_ge(rden_done, sec.after("rden_done", p))
                            dve.wait_ge(value_done, sec.after("value_done", ("value", None, c, 4 * c + 3)))
                            nc.vector.tensor_tensor(yv[:, c % 2], acc_y[:, c % 2], rden[:],
                                                    ALU.mult).then_inc(y_done, 1)
                        if p[1] != "dve":
                            continue
                        sl = slot_of(sec, p)
                        if kind == "rope":
                            _, _, which, c = p
                            if c == 0 and which == 1:
                                dve.wait_ge(loaded, 48 if sec is lead else (sec.i + 2) * 48)
                            dve.wait_ge(filled, sec.after("filled", p))
                            nc.vector.scalar_tensor_tensor(t1[:, which], sl[:, 1], bias[:, 2 * which + 1:2 * which + 2],
                                                           cos[:, chunk(c)], ALU.add, ALU.mult).then_inc(turned, 1)
                            nc.vector.scalar_tensor_tensor(t2[:, which], sl[:, 0], bias[:, 2 * which:2 * which + 1],
                                                           sin[:, chunk(c)], ALU.add, ALU.mult).then_inc(dve_read, 1)
                            dve.wait_ge(turned, sec.after("rotated", p))
                            dve.wait_ge(dve_read, sec.after("dve_read", p))
                            if not (sec is lead and c == 0):
                                dve.wait_ge(hi_done, sec.after("hi_done", ("hi", None, which, (c - 1) % NC), pos))
                                dve.wait_ge(lo_done, sec.after("lo_done", ("lo", None, which, (c - 1) % NC), pos))
                            nc.vector.tensor_tensor(y[:, which], t1[:, which], t2[:, which],
                                                    ALU.add).then_inc(rotated, 1)
                        elif kind == "v":
                            c = p[2]
                            dve.wait_ge(filled, sec.after("filled", p))
                            nc.vector.tensor_tensor(v[:, 4 * c:4 * c + 4], sl[:, 0].rearrange("p (t e) -> p t e", e=P),
                                                    vbias[:, None, :].broadcast_to([P, 4, P]),
                                                    ALU.add).then_inc(dve_read, 1)
                        elif kind == "max":
                            _, _, h, qt, g = p
                            c, j = qt // 4, qt % 4
                            keys = min(MAX_W, (qt + 1) * P - g * MAX_W)
                            dve.wait_ge(filled, sec.after("filled", p))
                            o = part[:, c, h, j, g:g + 1] if c >= 2 else mx[:, c, h, j:j + 1]
                            nc.vector.tensor_reduce(o, sl.rearrange("p b m -> p (b m)")[:, 0:keys], AX_X,
                                                    ALU.max).then_inc(dve_read, 1)
                            if p == last_maximum(c):
                                dve.wait_ge(dve_read, sec.after("dve_read", p))
                                if c >= 2:
                                    nc.vector.tensor_reduce(mx[:, c], part[:, c], AX_X, ALU.max).then_inc(max_done, 1)
                                else:
                                    dve.sem_inc(max_done, 1)
                        elif kind == "out":
                            c = p[2]
                            dve.wait_ge(filled, sec.after("filled", p))
                            nc.vector.tensor_tensor(x[:, chunk(c)], sl[:, 0], x[:, chunk(c)],
                                                    ALU.add).then_inc(dve_read, 1)

                run(dve, section)
                dve.wait_ge(dve_read, tail.after("dve_read", ("out", "dve", NC - 1)))
                nc.vector.tensor_scalar(x[:], x[:], obias[:, 0:1], None, ALU.add).then_inc(x_biased, 1)



HD = P // HEADS
PARTS = 3
TERMS = [(0, 0), (0, 1), (1, 0), (0, 2), (2, 0), (1, 1)]
KROWS = len(TERMS) * HD
PAIRS_H = HEADS // 2
QUADS = HEADS // 4
INVERT_AFTER = 3
GROUPS = NT * NC
DVE_HEADS = 8


def head_at(pos):
    return pos // 4 + 4 * (pos % 4)


def project_narrow(nc, n, wq, wk, wv, bq, bk, bv, v, q_stack, q_cleared, scratch, k_scratch):
    with ExitStack() as stack:
        s = Scope(nc, stack, "ph")
        full = s.sb("full", [P, 2, T])
        rest = s.sb("rest", [P, 2, T])
        parts = s.sb("parts", [P, 2, PARTS, T], BF16)
        acc = s.ps("acc", [P, 8, CW])
        projected = s.sem("projected")
        full_done = s.sem("full_done")
        hi_done = s.sem("hi_done")
        rest_done = s.sem("rest_done")
        mid_done = s.sem("mid_done")
        lo_done = s.sem("lo_done")
        v_read = s.sem("v_read")
        stored = [s.sem(f"part{j}_stored") for j in range(PARTS)]
        stacked = [s.sem(f"{name}_stacked") for name in ("q", "k")]
        items = [(w, c) for c in range(NC) for w in range(2)]

        def stack_rows(eng, w, j):
            eng.wait_ge(stored[j], 32)
            src = scratch[w, j].rearrange("(pair par d) x -> par d pair x", par=2, d=HD)
            for t, term in enumerate(TERMS):
                if term[w] == j:
                    for par in range(2):
                        r = slice(64 * par + HD * t, 64 * par + HD * t + HD)
                        dst = q_stack[r] if w == 0 else k_scratch[par][HD * t:HD * t + HD]
                        eng.dma_start(dst, src[par]).then_inc(stacked[w], 16)

        with nc.Block(no_gpsimd_drain=True) as block:
            @block.tensor
            def _(pe):
                for i, (w, c) in enumerate(items):
                    nc.tensor.matmul(acc[:, i], (wq, wk)[w], n[:, chunk(c)], start=True,
                                     stop=True).then_inc(projected, 1)
                for g in range(4):
                    pe.wait_ge(full_done, g + 1)
                    for j in range(4):
                        last = nc.tensor.matmul(acc[:, g, tile(j)], n[:, tile(4 * g + j)], wv, start=True, stop=True)
                    last.then_inc(projected, 1)

            @block.vector
            def _(dve):
                for i, (w, c) in enumerate(items):
                    dve.wait_ge(projected, i + 1)
                    nc.vector.tensor_scalar(full[:, w, chunk(c)], acc[:, i], (bq, bk)[w], None,
                                            ALU.add).then_inc(full_done, 1)
                for i, (w, c) in enumerate(items):
                    dve.wait_ge(full_done, i + 1)
                    dve.wait_ge(hi_done, i + 1)
                    nc.vector.tensor_tensor(rest[:, w, chunk(c)], full[:, w, chunk(c)], parts[:, w, 0, chunk(c)],
                                            ALU.subtract).then_inc(rest_done, 1)
                for i, (w, c) in enumerate(items):
                    dve.wait_ge(rest_done, i + 1)
                    dve.wait_ge(mid_done, i + 1)
                    nc.vector.tensor_tensor(parts[:, w, 2, chunk(c)], rest[:, w, chunk(c)], parts[:, w, 1, chunk(c)],
                                            ALU.subtract).then_inc(lo_done, 1)
                for g in range(4):
                    dve.wait_ge(projected, 8 + g + 1)
                    nc.vector.tensor_tensor(v[:, 4 * g:4 * g + 4], acc[:, g].rearrange("p (t e) -> p t e", t=4),
                                            bv[:, None, :].broadcast_to([P, 4, P]), ALU.add).then_inc(v_read, 1)

            @block.scalar
            def _(act):
                for i, (w, c) in enumerate(items):
                    act.wait_ge(full_done, i + 1)
                    nc.scalar.activation(parts[:, w, 0, chunk(c)], full[:, w, chunk(c)], ACT.Copy).then_inc(hi_done, 1)
                for i, (w, c) in enumerate(items):
                    act.wait_ge(rest_done, i + 1)
                    nc.scalar.activation(parts[:, w, 1, chunk(c)], rest[:, w, chunk(c)], ACT.Copy).then_inc(mid_done, 1)
                act.wait_ge(q_cleared, 1)
                for j in range(PARTS):
                    stack_rows(act, 0, j)
                act.wait_ge(stacked[0], 2 * len(TERMS) * 16)

            @block.sync
            def _(sp):
                for j, done in enumerate((hi_done, mid_done, lo_done)):
                    sp.wait_ge(done, len(items))
                    for w in range(2):
                        sp.dma_start(scratch[w, j], parts[:, w, j]).then_inc(stored[j], 16)
                    stack_rows(sp, 1, j)
                sp.wait_ge(stacked[1], 2 * len(TERMS) * 16)


def softmax_over_heads(nc, const, x, q_stack, v, k_scratch, w_out, b_out):
    scale = float(1.0 / np.sqrt(np.float32(HD)))
    with ExitStack() as stack:
        s = Scope(nc, stack, "hs")
        kt_stack = s.sb("k_tile", [P, 2, HEADS, P], BF16)
        v_pad = s.sb("v_padded", [P, 2, HEADS, 32])
        rounded = s.sb("rounded", [P, 2, HEADS, CW], BF16)
        mx = s.sb("maxima", [P, 2, CW], BF16)
        ex = s.sb("exps", [P, 2, HEADS, CW])
        total = s.sb("total", [P, 2, CW])
        rtot = s.sb("r_total", [P, 2, CW])
        slot = s.ps("slot", [P, 2, 2, CW])
        acc = s.ps("attended", [P, NC, CW])

        k_loaded = [s.sem(f"k_loaded{b}") for b in range(2)]
        v_copied = s.sem("v_copied")
        cleared = s.sem("v_and_k_cleared")
        filled = s.sem("slots_filled")
        read = s.sem("slots_read")
        tree = s.sem("max_tree")
        summed = s.sem("summed")
        logged = s.sem("logged")
        inverted = s.sem("inverted")
        dve_scaled = s.sem("scaled_dve")
        pool_scaled = s.sem("scaled_pool")
        accumulated = s.sem("accumulated")
        zeroed = s.sem("zeroed")
        out_copied = s.sem("out_copied")
        out_projected = s.sem("out_projected")
        x_added = s.sem("x_added")

        SL = HEADS // 2
        BODY = 8

        def loop(eng, emit):
            for step in (-2, -1, 0, 1):
                emit(step, 0, step % BODY, 0)
            with eng.Fori(0, (GROUPS - 8) // BODY) as i:
                for g in range(2, BODY + 2):
                    emit(g, i * BODY, g % BODY, i)
            for g in range(GROUPS - 6, GROUPS + 1):
                emit(g, 0, g % BODY, 0)

        def has(step, base, shift):
            if not isinstance(base, int):
                return True
            return 0 <= step + base + shift < GROUPS

        def exp_pass(g):
            return 2 * g + 2 - (1 if isinstance(g, int) and g == GROUPS - 1 else 0)

        def rounded_pass(g):
            return g if isinstance(g, int) and g < 2 else 2 * g - 1

        with nc.Block(no_gpsimd_drain=True) as block:
            @block.sync
            def _(sp):
                def load(kt, buf):
                    for par in range(2):
                        sp.dma_start(kt_stack[64 * par:64 * par + KROWS, buf].rearrange("r (pair two) k -> r pair two k", two=2)
                                     [:, :, par], k_scratch[par][:, :, bass.ts(kt, P)])\
                            .then_inc(k_loaded[buf], 16)

                sp.wait_ge(cleared, 2)
                load(0, 0)
                load(1, 1)
                with sp.Fori(0, NT // 2 - 1) as i:
                    for b in range(2):
                        last_step = 8 * i + 4 * b + 3
                        sp.wait_ge(filled, SL * (exp_pass(last_step) + 1))
                        sp.wait_ge(k_loaded[b], 32)
                        load(2 * i + 2 + b, b)

            @block.gpsimd
            def _(pool):
                nc.gpsimd.memset(v_pad[:], 0.0).then_inc(cleared, 1)
                pool.wait_ge(cleared, 2)

                def stage_values(kt, buf):
                    for r in range(QUADS):
                        nc.gpsimd.tensor_copy(v_pad[:, buf, 4 * r:4 * r + 4, HD * r:HD * r + HD],
                                              v[:, bass.ts(kt, 1)].rearrange("p o (j r d) -> p (o j) r d", j=4, r=4)
                                              [:, :, r]).then_inc(v_copied, 1)

                def emit(step, base, phase, turns):
                    if not has(step, base, -1):
                        return
                    g = base + step - 1
                    gp = (phase - 1) % BODY
                    if gp % 4 == 0:
                        kt = 2 * turns + (step - 1) // 4
                        if not (isinstance(g, int) and g < 8):
                            pool.wait_ge(accumulated, g - 4)
                        pool.wait_ge(cleared, 2)
                        stage_values(kt, gp // 4)
                    pool.wait_ge(inverted, g + 1)
                    nc.gpsimd.tensor_tensor(ex[:, gp % 2, DVE_HEADS:], ex[:, gp % 2, DVE_HEADS:],
                                            rtot[:, gp % 2, None, :].broadcast_to([P, HEADS - DVE_HEADS, CW]),
                                            ALU.mult).then_inc(pool_scaled, 1)

                loop(pool, emit)

            @block.tensor
            def _(pe):
                def scores(phase, first_fill, shifted, between=None):
                    kt_buf, c = (phase % BODY) // 4, phase % 4
                    for j in range(SL):
                        b = j % 2
                        if not (isinstance(first_fill, int) and first_fill + j < 2):
                            pe.wait_ge(read, first_fill + j - 1)
                        for e in range(2):
                            h = head_at(2 * j + e)
                            last = nc.tensor.matmul(slot[:, b, e], kt_stack[:, kt_buf, h], q_stack[:, h // 2, chunk(c)],
                                                    start=True, stop=not shifted)
                            if shifted:
                                last = nc.tensor.matmul(slot[:, b, e], const["neg_ident_bf"][:], mx[:, phase % 2],
                                                        start=False, stop=True)
                        last.then_inc(filled, 1)
                        if between and j % 2 == 1:
                            between(j // 2)

                def emit(step, base, phase, turns):
                    if step == 0 and isinstance(base, int) and base == 0:
                        for c in range(NC):
                            last = nc.tensor.matmul(acc[:, c], const["zero_bf"][0:32], q_stack[0:32, 0, chunk(c)],
                                                    start=True, stop=True)
                        last.then_inc(zeroed, 1)
                    first_fill = SL * exp_pass(base + step)
                    if has(step, base, 0):
                        pe.wait_ge(tree, 4 * (base + step) + 4)
                        scores(phase, first_fill, True)

                    def values(r):
                        g = base + step - 1
                        gp = (phase - 1) % BODY
                        if r == 0:
                            pe.wait_ge(dve_scaled, g + 1)
                            if gp % 4 == 0:
                                pe.wait_ge(v_copied, 4 * (2 * turns + (step - 1) // 4 + 1))
                        if 4 * r + 4 > DVE_HEADS:
                            pe.wait_ge(pool_scaled, g + 1)
                        for pos in range(4 * r, 4 * r + 4):
                            j = pos % 4
                            last = nc.tensor.matmul(acc[32 * j:32 * j + 32, gp % 4], v_pad[:, gp // 4, pos],
                                                    ex[:, gp % 2, pos], start=False, stop=False, skip_group_check=True)
                        if r == QUADS - 1:
                            last.then_inc(accumulated, 1)

                    if has(step, base, 2):
                        g2 = (phase + 2) % BODY
                        if g2 % 4 == 0:
                            t = (step + 2) // 4
                            pe.wait_ge(k_loaded[t % 2], 32 * (turns + t // 2 + 1))
                        scores(g2, SL * rounded_pass(base + step + 2), False, values if has(step, base, -1) else None)
                    elif has(step, base, -1):
                        for r in range(QUADS):
                            values(r)

                loop(pe, emit)
                for c in range(NC):
                    pe.wait_ge(out_copied, c + 1)
                    if c == 0:
                        pe.wait_ge(read, 2 * SL * GROUPS)
                    nc.tensor.matmul(slot[:, c // 2, c % 2], w_out, ex[:, 0, c], start=True,
                                     stop=True).then_inc(out_projected, 1)

            @block.scalar
            def _(act):
                nc.scalar.preload_act_table_set("natural_log_exp_and_others")

                def invert(g, b):
                    act.wait_ge(summed, g + 1)
                    nc.scalar.activation(total[:, b], total[:, b], ACT.Ln).then_inc(logged, 1)
                    act.wait_ge(logged, g + 1)
                    if not (isinstance(g, int) and g < 2):
                        act.wait_ge(dve_scaled, g - 1)
                        act.wait_ge(pool_scaled, g - 1)
                    nc.scalar.activation(rtot[:, b], total[:, b], ACT.Exp, scale=-1.0).then_inc(inverted, 1)

                def emit(step, base, phase, turns):
                    first_fill = SL * exp_pass(base + step)
                    if has(step, base, 0):
                        g = base + step
                        if not (isinstance(g, int) and g < 2):
                            act.wait_ge(accumulated, g - 1)
                        for j in range(SL):
                            act.wait_ge(filled, first_fill + j + 1)
                            nc.scalar.activation(ex[:, phase % 2, 2 * j:2 * j + 2], slot[:, j % 2], ACT.Exp,
                                                 scale=scale).then_inc(read, 1)
                            if j == INVERT_AFTER and has(step, base, -1):
                                invert(base + step - 1, (phase - 1) % 2)
                    elif has(step, base, -1):
                        invert(base + step - 1, (phase - 1) % 2)
                    if has(step, base, 2):
                        g = base + step + 2
                        if not (isinstance(g, int) and g < 2):
                            act.wait_ge(tree, 4 * (g - 2) + 4)
                        first_fill = SL * rounded_pass(g)
                        for j in range(SL):
                            act.wait_ge(filled, first_fill + j + 1)
                            nc.scalar.activation(rounded[:, phase % 2, 2 * j:2 * j + 2], slot[:, j % 2],
                                                 ACT.Copy).then_inc(read, 1)

                loop(act, emit)
                act.wait_ge(accumulated, GROUPS)
                act.wait_ge(zeroed, 1)
                for c in range(NC):
                    nc.scalar.activation(ex[:, 0, c], acc[:, c], ACT.Copy).then_inc(out_copied, 1)

            @block.vector
            def _(dve):
                nc.vector.memset(kt_stack[:], 0.0).then_inc(cleared, 1)

                def maxima(g, b, first_read):
                    dve.wait_ge(read, first_read)
                    r = rounded[:, b]
                    for k, m in enumerate((8, 4, 2, 1)):
                        if k:
                            dve.wait_ge(tree, 4 * g + k)
                        elif not (isinstance(g, int) and g < 2):
                            dve.wait_ge(filled, SL * (exp_pass(g - 2) + 1))
                        o = r[:, 0:m] if m > 1 else mx[:, b:b + 1]
                        nc.vector.tensor_tensor(o, r[:, 0:m], r[:, m:2 * m], ALU.max).then_inc(tree, 1)

                def emit(step, base, phase, turns):
                    if has(step, base, -1):
                        g = base + step - 1
                        b = (phase - 1) % 2
                        dve.wait_ge(read, SL * (exp_pass(g) + 1))
                        if not (isinstance(g, int) and g < 2):
                            dve.wait_ge(inverted, g - 1)
                        nc.vector.tensor_reduce(total[:, b], ex[:, b].rearrange("p n q -> p q n"), AX_X,
                                                ALU.add).then_inc(summed, 1)
                    if has(step, base, 1):
                        ahead = base + step + 1
                        maxima(ahead, (phase + 1) % 2, SL * (rounded_pass(ahead) + 1))
                    if has(step, base, -1):
                        dve.wait_ge(inverted, g + 1)
                        b = (phase - 1) % 2
                        nc.vector.tensor_tensor(ex[:, b, 0:DVE_HEADS], ex[:, b, 0:DVE_HEADS],
                                                rtot[:, b, None, :].broadcast_to([P, DVE_HEADS, CW]),
                                                ALU.mult).then_inc(dve_scaled, 1)

                loop(dve, emit)
                for c in range(NC):
                    dve.wait_ge(out_projected, c + 1)
                    nc.vector.scalar_tensor_tensor(x[:, chunk(c)], slot[:, c // 2, c % 2], b_out, x[:, chunk(c)],
                                                   ALU.add, ALU.add).then_inc(x_added, 1)
                dve.wait_ge(x_added, NC)



FF = 512
FT = FF // P
EXPERTS = 8


def modulated_ffn(nc, const, x, n, w, vec):
    with ExitStack() as stack:
        s = Scope(nc, stack, f"ff{const['ffn_runs']}")
        const["ffn_runs"] += 1
        relu = s.sb("relu", [P, CW])
        rsum = s.sb("relu_sum", [P, NC])
        rmean = s.sb("relu_mean", [P, 2])
        spread = s.sb("mean_spread", [P, P])
        gate = s.sb("gate", [P, EXPERTS])
        m1 = s.sb("mixed_w1", [P, FF])
        m2 = s.sb("mixed_w2", [P, FF])
        tmp = s.sb("tmp", [P, FT + 1, EXPERTS])
        mb = s.sb("mixed_b", [P, FT + 1])
        u = s.sb("hidden", [P, 2, FT, CW])
        ps = s.ps("acc", [P, 8, CW])
        gated = s.sem("gate_hidden")
        summed = s.sem("relu_summed")
        averaged = s.sem("averaged")
        gate_ps = s.sem("gate_product")
        gate_done = s.sem("gate_done")
        mixed1 = s.sem("w1_mixed")
        mixed2 = s.sem("w2_mixed")
        mixed_b = s.sem("b_mixed")
        hidden_ps = s.sem("hidden_product")
        hidden = s.sem("hidden_done")
        out_ps = s.sem("out_product")
        added = s.sem("x_added")

        with nc.Block(no_gpsimd_drain=True) as block:
            @block.tensor
            def _(pe):
                for c in range(NC):
                    nc.tensor.matmul(ps[:, c], w["gate1"], n[:, chunk(c)], start=True, stop=True).then_inc(gated, 1)
                pe.wait_ge(averaged, 3)
                nc.tensor.matmul(ps[:, 4, 0:EXPERTS], spread[:], w["gate2"], start=True, stop=True).then_inc(gate_ps, 1)
                pe.wait_ge(mixed1, EXPERTS)

                def up(c):
                    for f in range(FT):
                        k = c * FT + f
                        if k >= 4:
                            pe.wait_ge(hidden, k - 3)
                        nc.tensor.matmul(ps[:, k % 4], m1[:, tile(f)], n[:, chunk(c)], start=True,
                                         stop=True).then_inc(hidden_ps, 1)

                def down(c):
                    pe.wait_ge(hidden, c * FT + FT)
                    if c == 0:
                        pe.wait_ge(mixed2, EXPERTS)
                        pe.wait_ge(gate_done, 1)
                    if c >= 2:
                        pe.wait_ge(added, c - 1)
                    for f in range(FT):
                        last = nc.tensor.matmul(ps[:, 4 + c % 2], m2[:, tile(f)], u[:, c % 2, f], start=(f == 0),
                                                stop=(f == FT - 1))
                    last.then_inc(out_ps, 1)

                up(0)
                for c in range(1, NC):
                    up(c)
                    down(c - 1)
                down(NC - 1)

            @block.scalar
            def _(act):
                for c in range(NC):
                    act.wait_ge(gated, c + 1)
                    if c:
                        act.wait_ge(summed, c)
                    nc.scalar.activation(relu[:], ps[:, c], ACT.Relu, bias=vec["gate_b1"],
                                         accum_out=rsum[:, c:c + 1]).then_inc(summed, 1)
                act.wait_ge(mixed_b, 3)
                for c in range(NC):
                    for f in range(FT):
                        act.wait_ge(hidden_ps, c * FT + f + 1)
                        if c >= 2 and f == 0:
                            act.wait_ge(out_ps, c - 1)
                        nc.scalar.activation(u[:, c % 2, f], ps[:, (c * FT + f) % 4], ACT.Gelu_apprx_tanh,
                                             bias=mb[:, f:f + 1]).then_inc(hidden, 1)

            @block.vector
            def _(dve):
                dve.wait_ge(summed, NC)
                nc.vector.tensor_reduce(rmean[:, 0:1], rsum[:], AX_X, ALU.add).then_inc(averaged, 1)
                dve.wait_ge(averaged, 1)
                nc.vector.tensor_scalar(rmean[:, 1:2], rmean[:, 0:1], 1.0 / T, None, ALU.mult).then_inc(averaged, 1)
                dve.wait_ge(averaged, 2)
                nc.vector.tensor_scalar(spread[:], const["ones"][:], rmean[:, 1:2], None, ALU.mult).then_inc(averaged, 1)
                dve.wait_ge(gate_ps, 1)
                nc.vector.tensor_tensor(gate[:], ps[:, 4, 0:EXPERTS], w["gate_b2"], ALU.add).then_inc(gate_done, 1)
                dve.wait_ge(gate_done, 1)
                nc.vector.tensor_tensor(tmp[:], w["tb"], gate[:, None, :].broadcast_to([P, FT + 1, EXPERTS]),
                                        ALU.mult).then_inc(mixed_b, 1)
                dve.wait_ge(mixed_b, 1)
                nc.vector.tensor_reduce(mb[:], tmp[:], AX_X, ALU.add).then_inc(mixed_b, 1)
                dve.wait_ge(mixed_b, 2)
                nc.vector.tensor_tensor(mb[:], mb[:], vec["ffn_b"], ALU.add).then_inc(mixed_b, 1)
                for mixed, base, experts, done in ((m1, w["w1"], w["tw1"], mixed1), (m2, w["w2"], w["tw2"], mixed2)):
                    for e in range(EXPERTS):
                        if e:
                            dve.wait_ge(done, e)
                        nc.vector.scalar_tensor_tensor(mixed[:], experts[:, e * FF:(e + 1) * FF], gate[:, e:e + 1],
                                                       mixed[:] if e else base, ALU.mult, ALU.add).then_inc(done, 1)
                for c in range(NC):
                    dve.wait_ge(out_ps, c + 1)
                    if c == 0:
                        dve.wait_ge(mixed_b, 3)
                    nc.vector.scalar_tensor_tensor(x[:, chunk(c)], ps[:, 4 + c % 2], mb[:, FT:FT + 1], x[:, chunk(c)],
                                                   ALU.add, ALU.add).then_inc(added, 1)


def mix_ffn(nc, const, x, n, w, mu):
    with ExitStack() as stack:
        s = Scope(nc, stack, f"mf{const['mix_runs']}")
        const["mix_runs"] += 1
        rest = s.sb("one_less_mu", [P, 2])
        old = s.sb("before", [P, 2, T])
        xm = s.sb("mixed", [P, 2, T])
        r = s.sb("gate", [P, T])
        k = s.sb("relu", [P, T])
        k2 = s.sb("squared", [P, T])
        o = s.sb("product", [P, T])
        ps = s.ps("acc", [P, 8, CW])
        rested = s.sem("rest_done")
        scaled = s.sem("before_scaled")
        mixed = s.sem("mixed")
        product = s.sem("products")
        gated = s.sem("gated")
        relu = s.sem("relu_done")
        squared = s.sem("squared")
        value = s.sem("value_products")
        multiplied = s.sem("multiplied")
        added = s.sem("x_added")
        with nc.Block(no_gpsimd_drain=True) as block:
            @block.gpsimd
            def _(pool):
                pool.wait_ge(rested, 1)
                for c in range(NC):
                    for m in range(2):
                        nc.gpsimd.tensor_scalar(old[:, m, chunk(c)], n[:, c * CW:(c + 1) * CW], rest[:, m:m + 1], 0.0,
                                                ALU.mult, ALU.add).then_inc(scaled, 1)

            @block.vector
            def _(dve):
                nc.vector.tensor_scalar(rest[:], mu, -1.0, 1.0, ALU.mult, ALU.add).then_inc(rested, 1)
                for c in range(NC):
                    for m in range(2):
                        dve.wait_ge(scaled, 2 * c + m + 1)
                        nc.vector.scalar_tensor_tensor(xm[:, m, chunk(c)], n[:, 1 + c * CW:1 + (c + 1) * CW],
                                                       mu[:, m:m + 1], old[:, m, chunk(c)], ALU.mult,
                                                       ALU.add).then_inc(mixed, 1)
                for c in range(NC):
                    dve.wait_ge(relu, c + 1)
                    nc.vector.tensor_tensor(k2[:, chunk(c)], k[:, chunk(c)], k[:, chunk(c)], ALU.mult)\
                        .then_inc(squared, 1)
                for c in range(NC):
                    dve.wait_ge(value, c + 1)
                    dve.wait_ge(gated, c + 1)
                    nc.vector.tensor_tensor(o[:, chunk(c)], ps[:, c], r[:, chunk(c)], ALU.mult).then_inc(multiplied, 1)
                for c in range(NC):
                    dve.wait_ge(multiplied, c + 1)
                    nc.vector.tensor_tensor(x[:, chunk(c)], o[:, chunk(c)], x[:, chunk(c)], ALU.add).then_inc(added, 1)

            @block.tensor
            def _(pe):
                for c in range(NC):
                    for m in range(2):
                        pe.wait_ge(mixed, 2 * c + m + 1)
                        nc.tensor.matmul(ps[:, 4 * m + c], (w["r"], w["k"])[m], xm[:, m, chunk(c)], start=True,
                                         stop=True).then_inc(product, 1)
                for c in range(NC):
                    pe.wait_ge(squared, c + 1)
                    pe.wait_ge(gated, c + 1)
                    nc.tensor.matmul(ps[:, c], w["v"], k2[:, chunk(c)], start=True, stop=True).then_inc(value, 1)

            @block.scalar
            def _(act):
                for c in range(NC):
                    act.wait_ge(product, 2 * c + 1)
                    nc.scalar.activation(r[:, chunk(c)], ps[:, c], ACT.Sigmoid).then_inc(gated, 1)
                    act.wait_ge(product, 2 * c + 2)
                    nc.scalar.activation(k[:, chunk(c)], ps[:, 4 + c], ACT.Relu).then_inc(relu, 1)


GH = HEADS


def channel_attention(nc, const, x, n, w, vec):
    with ExitStack() as stack:
        s = Scope(nc, stack, "ca")
        q = s.sb("q", [P, T])
        kv = s.sb("kv", [P, NT, 2, GH, HD])
        cen = s.sb("centred", [P, NT, 2, GH, HD])
        sq = s.sb("squared", [P, NT, 2, GH, HD])
        mean = s.sb("mean", [P, NT, 2, GH])
        var = s.sb("var", [P, NT, 2, GH])
        std = s.sb("std", [P, NT, 2, GH])
        rstd = s.sb("rstd", [P, NT, 2, GH])
        head = s.sb("head_matrix", [P, 2, P])
        att = s.sb("att", [P, T])
        h = s.sb("gelu", [P, T])
        o = s.sb("out", [P, T])
        ps = s.ps("acc", [P, 8, CW])
        kv_ps = s.sem("kv_products")
        q_ps = s.sem("q_products")
        kv_in = s.sem("kv_in")
        q_in = s.sem("q_in")
        step = s.sem("norm_steps")
        squared = s.sem("squared")
        rooted = s.sem("rooted")
        gained = s.sem("gained")
        head_ps = s.sem("head_product")
        head_done = s.sem("head_done")
        att_ps = s.sem("att_products")
        att_done = s.sem("att_done")
        p1_ps = s.sem("p1_products")
        gelu = s.sem("gelu_done")
        p2_ps = s.sem("p2_products")
        out_done = s.sem("out_done")
        added = s.sem("x_added")
        STEPS = 8
        HALF = NT // 2

        with nc.Block(no_gpsimd_drain=True) as block:
            @block.tensor
            def _(pe):
                for g in range(NT // 2):
                    if g >= 6:
                        pe.wait_ge(kv_in, g - 5)
                    for j in range(2):
                        last = nc.tensor.matmul(ps[:, g % 6, 2 * P * j:2 * P * j + 2 * P], n[:, tile(2 * g + j)], w["kv"],
                                                start=True, stop=True)
                    last.then_inc(kv_ps, 1)
                for c in range(NC):
                    if c >= 2:
                        pe.wait_ge(q_in, c - 1)
                    nc.tensor.matmul(ps[:, 6 + c % 2], w["q"], n[:, chunk(c)], start=True, stop=True).then_inc(q_ps, 1)
                pe.wait_ge(kv_in, NT // 2)
                for t in range(NT):
                    pe.wait_ge(step, STEPS * (t // HALF + 1))
                    last = nc.tensor.matmul(ps[:, 0, 0:P], kv[:, t, 0].rearrange("p g d -> p (g d)"),
                                            kv[:, t, 1].rearrange("p g d -> p (g d)"), start=(t == 0),
                                            stop=(t == NT - 1))
                last.then_inc(head_ps, 1)
                pe.wait_ge(head_done, 2)
                pe.wait_ge(q_in, NC)
                for c in range(NC):
                    nc.tensor.matmul(ps[:, 1 + c], head[:, 1], q[:, chunk(c)], start=True, stop=True).then_inc(att_ps, 1)
                for c in range(NC):
                    pe.wait_ge(att_done, c + 1)
                    nc.tensor.matmul(ps[:, 1 + c], w["p1"], att[:, chunk(c)], start=True, stop=True).then_inc(p1_ps, 1)
                for c in range(NC):
                    pe.wait_ge(gelu, c + 1)
                    nc.tensor.matmul(ps[:, 1 + c], w["p2"], h[:, chunk(c)], start=True, stop=True).then_inc(p2_ps, 1)

            @block.scalar
            def _(act):
                for half in range(2):
                    t = slice(HALF * half, HALF * half + HALF)
                    act.wait_ge(step, STEPS * half + 3)
                    nc.scalar.activation(sq[:, t], cen[:, t], ACT.Square).then_inc(squared, 1)
                    act.wait_ge(step, STEPS * half + 4)
                    nc.scalar.activation(std[:, t], var[:, t], ACT.Sqrt, bias=const["eps"][:],
                                         scale=1.0 / HD).then_inc(rooted, 1)
                for c in range(NC):
                    act.wait_ge(p1_ps, c + 1)
                    nc.scalar.activation(h[:, chunk(c)], ps[:, 1 + c], ACT.Gelu, bias=vec["p1_b"]).then_inc(gelu, 1)

            @block.vector
            def _(dve):
                for g in range(NT // 2):
                    dve.wait_ge(kv_ps, g + 1)
                    nc.vector.tensor_tensor(kv[:, 2 * g:2 * g + 2].rearrange("p t k g d -> p t (k g d)"),
                                            ps[:, g % 6].rearrange("p (t e) -> p t e", t=2),
                                            w["kv_b"][:, None, :].broadcast_to([P, 2, 2 * P]), ALU.add).then_inc(kv_in, 1)
                for c in range(NC):
                    dve.wait_ge(q_ps, c + 1)
                    nc.vector.tensor_scalar(q[:, chunk(c)], ps[:, 6 + c % 2], vec["q_b"], None, ALU.add).then_inc(q_in, 1)
                dve.wait_ge(kv_in, NT // 2)

                def spread(a, t):
                    return a[:, t].rearrange("p t k g -> p (t k g)")[:, :, None].broadcast_to([P, HALF * 2 * GH, HD])

                def flat(a, t):
                    return a[:, t].rearrange("p t k g d -> p (t k g) d")

                for half in range(2):
                    t = slice(HALF * half, HALF * half + HALF)
                    b = STEPS * half
                    nc.vector.tensor_reduce(mean[:, t], kv[:, t], AX_X, ALU.add).then_inc(step, 1)
                    dve.wait_ge(step, b + 1)
                    nc.vector.tensor_scalar(mean[:, t], mean[:, t], 1.0 / HD, None, ALU.mult).then_inc(step, 1)
                    dve.wait_ge(step, b + 2)
                    nc.vector.tensor_tensor(flat(cen, t), flat(kv, t), spread(mean, t), ALU.subtract).then_inc(step, 1)
                    dve.wait_ge(squared, half + 1)
                    nc.vector.tensor_reduce(var[:, t], sq[:, t], AX_X, ALU.add).then_inc(step, 1)
                    dve.wait_ge(rooted, half + 1)
                    nc.vector.reciprocal(rstd[:, t], std[:, t]).then_inc(step, 1)
                    dve.wait_ge(step, b + 5)
                    nc.vector.tensor_tensor(flat(sq, t), flat(cen, t), spread(rstd, t), ALU.mult).then_inc(step, 1)
                    dve.wait_ge(step, b + 6)
                    for k in range(2):
                        view = lambda a: a[:, t, k].rearrange("p t g d -> p t (g d)")
                        gain = w["gain"][:, 2 * k, None, :].broadcast_to([P, HALF, P])
                        shift = w["gain"][:, 2 * k + 1, None, :].broadcast_to([P, HALF, P])
                        nc.vector.tensor_tensor(view(cen), view(sq), gain, ALU.mult).then_inc(gained, 1)
                        dve.wait_ge(gained, 2 * half + k + 1)
                        nc.vector.tensor_tensor(view(kv), view(cen), shift, ALU.add).then_inc(step, 1)
                dve.wait_ge(head_ps, 1)
                nc.vector.scalar_tensor_tensor(head[:, 0], ps[:, 0, 0:P], vec["temp"], w["head_mask"], ALU.mult,
                                               ALU.mult).then_inc(head_done, 1)
                dve.wait_ge(head_done, 1)
                nc.vector.scalar_tensor_tensor(head[:, 1], head[:, 0], 1.0 / T, w["att_bias"], ALU.mult,
                                               ALU.add).then_inc(head_done, 1)
                for c in range(NC):
                    dve.wait_ge(att_ps, c + 1)
                    nc.vector.tensor_tensor(att[:, chunk(c)], ps[:, 1 + c], n[:, chunk(c)], ALU.add).then_inc(att_done, 1)
                for c in range(NC):
                    dve.wait_ge(p2_ps, c + 1)
                    nc.vector.scalar_tensor_tensor(o[:, chunk(c)], ps[:, 1 + c], vec["p2_b"], n[:, chunk(c)], ALU.add,
                                                   ALU.add).then_inc(out_done, 1)
                for c in range(NC):
                    dve.wait_ge(out_done, c + 1)
                    nc.vector.tensor_tensor(x[:, chunk(c)], o[:, chunk(c)], x[:, chunk(c)], ALU.add).then_inc(added, 1)





def gated_projections(nc, const, n, xn, w, vec, q, k, v_ext):
    with ExitStack() as stack:
        s = Scope(nc, stack, "gp")
        xg = s.sb("gained", [P, T])
        gate = s.sb("gate", [P, T])
        gsum = s.sb("gate_mean", [P, T])
        rsum = s.sb("r_gate_mean", [P, T])
        gn = s.sb("gate_normed", [P, T])
        lin = s.sb("linear", [P, 2, T])
        low = s.sb("below_zero", [P, 2, T])
        ex = s.sb("exp", [P, 2, T])
        ps = s.ps("acc", [P, 8, CW])
        gained = s.sem("gained")
        gate_ps = s.sem("gate_products")
        gated = s.sem("gated")
        mean_ps = s.sem("mean_products")
        mean_in = s.sem("mean_in")
        inverted = s.sem("inverted")
        normed = s.sem("gate_normed")
        qk_ps = s.sem("qk_products")
        lin_done = s.sem("linear_done")
        low_done = s.sem("low_done")
        ex_done = s.sem("exp_done")
        elu_done = s.sem("elu_done")
        v_ps = s.sem("v_products")
        v_in = s.sem("v_in")
        ones_in = s.sem("ones_in")
        items = [(m, c) for c in range(NC) for m in range(2)]
        with nc.Block(no_gpsimd_drain=True) as block:
            @block.tensor
            def _(pe):
                for c in range(NC):
                    nc.tensor.matmul(ps[:, c], w["gate"], n[:, chunk(c)], start=True, stop=True).then_inc(gate_ps, 1)
                for c in range(NC):
                    pe.wait_ge(gated, c + 1)
                    nc.tensor.matmul(ps[:, c], const["mean"][:], gate[:, chunk(c)], start=True, stop=True).then_inc(mean_ps, 1)
                for i, (m, c) in enumerate(items):
                    pe.wait_ge(gained, c + 1)
                    if i >= 4:
                        pe.wait_ge(lin_done, i - 3)
                    nc.tensor.matmul(ps[:, 4 + i % 4], (w["q"], w["k"])[m], xg[:, chunk(c)], start=True,
                                     stop=True).then_inc(qk_ps, 1)
                for g in range(4):
                    pe.wait_ge(mean_in, g + 1)
                    for j in range(4):
                        last = nc.tensor.matmul(ps[:, g, tile(j)], xg[:, tile(4 * g + j)], w["v"], start=True, stop=True)
                    last.then_inc(v_ps, 1)

            @block.scalar
            def _(act):
                for c in range(NC):
                    act.wait_ge(gate_ps, c + 1)
                    nc.scalar.activation(gate[:, chunk(c)], ps[:, c], ACT.Sigmoid, bias=vec["gate_b"]).then_inc(gated, 1)
                for i, (m, c) in enumerate(items):
                    act.wait_ge(low_done, i + 1)
                    nc.scalar.activation(ex[:, m, chunk(c)], low[:, m, chunk(c)], ACT.Exp).then_inc(ex_done, 1)

            @block.gpsimd
            def _(pool):
                nc.gpsimd.memset(v_ext[:, :, P:2 * P], 1.0).then_inc(ones_in, 1)

            @block.vector
            def _(dve):
                for c in range(NC):
                    nc.vector.tensor_scalar(xg[:, chunk(c)], xn[:, chunk(c)], vec["ln_g"], vec["ln_b"], ALU.mult,
                                            ALU.add).then_inc(gained, 1)
                for c in range(NC):
                    dve.wait_ge(mean_ps, c + 1)
                    nc.vector.tensor_scalar(gsum[:, chunk(c)], ps[:, c], EPS, None, ALU.add).then_inc(mean_in, 1)
                    dve.wait_ge(mean_in, c + 1)
                    nc.vector.reciprocal(rsum[:, chunk(c)], gsum[:, chunk(c)]).then_inc(inverted, 1)
                    dve.wait_ge(inverted, c + 1)
                    nc.vector.tensor_tensor(gn[:, chunk(c)], gate[:, chunk(c)], rsum[:, chunk(c)],
                                            ALU.mult).then_inc(normed, 1)
                for i, (m, c) in enumerate(items):
                    dve.wait_ge(qk_ps, i + 1)
                    dve.wait_ge(normed, c + 1)
                    nc.vector.scalar_tensor_tensor(lin[:, m, chunk(c)], ps[:, 4 + i % 4], (vec["q_b"], vec["k_b"])[m],
                                                   gn[:, chunk(c)], ALU.add, ALU.mult).then_inc(lin_done, 1)
                    dve.wait_ge(lin_done, i + 1)
                    nc.vector.tensor_scalar(low[:, m, chunk(c)], lin[:, m, chunk(c)], 0.0, None,
                                            ALU.min).then_inc(low_done, 1)
                for g in range(4):
                    dve.wait_ge(v_ps, g + 1)
                    nc.vector.tensor_tensor(v_ext[:, 4 * g:4 * g + 4, 0:P], ps[:, g].rearrange("p (t e) -> p t e", t=4),
                                            w["v_b"][:, None, :].broadcast_to([P, 4, P]), ALU.add).then_inc(v_in, 1)
                for i, (m, c) in enumerate(items):
                    dve.wait_ge(ex_done, i + 1)
                    nc.vector.scalar_tensor_tensor((q, k)[m][:, chunk(c)], lin[:, m, chunk(c)], 0.0, ex[:, m, chunk(c)],
                                                   ALU.max, ALU.add).then_inc(elu_done, 1)


def linear_attention(nc, const, x, q, k, v_ext, w, vec):
    with ExitStack() as stack:
        s = Scope(nc, stack, "la")
        k_tile = s.sb("k_tile", [P, 2, P])
        v_pad = s.sb("v_padded", [P, 2, HEADS, 32])
        k_tok = s.sb("k_by_token", [P, 2, P])
        q_spread = s.sb("q_spread", [P, 2, HEADS, P])
        prod = s.sb("products", [P, 2, HEADS, P])
        state = s.sb("state", [P, 2, 2 * P])
        nd = s.sb("num_den", [P, 2, T])
        rden = s.sb("r_den", [P, T])
        att = s.sb("attended", [P, T])
        qk = s.ps("qk", [P, 4, CW])
        nd_ps = s.ps("num_den_acc", [P, 2, CW])
        st_ps = s.ps("state_acc", [P, CW])
        kt_ps = s.ps("k_turned", [P, CW])

        cleared = s.sem("cleared")
        staged = s.sem("staged")
        spread = s.sem("q_spread")
        qk_ps = s.sem("qk_products")
        turned = s.sem("k_turned")
        tok_in = s.sem("k_tok_in")
        masked = s.sem("masked")
        nd_done = s.sem("num_den_products")
        nd_out = s.sem("num_den_out")
        st_done = s.sem("state_products")
        st_out = s.sem("state_out")
        inverted = s.sem("inverted")
        scaled = s.sem("scaled")
        projected = s.sem("projected")
        added = s.sem("x_added")
        COPIES = 5

        def loop(eng, emit):
            for step in (-1, 0, 1):
                emit(step, 0)
            with eng.Fori(0, NT // 2 - 2) as i:
                for step in (2, 3):
                    emit(step, 2 * i)
            for step in (NT - 2, NT - 1):
                emit(step, 0)

        def has(step, base, shift):
            return not isinstance(base, int) or 0 <= step + base + shift < NT

        with nc.Block(no_gpsimd_drain=True) as block:
            @block.gpsimd
            def _(pool):
                nc.gpsimd.memset(v_pad[:], 0.0).then_inc(cleared, 1)
                pool.wait_ge(cleared, 1)

                def emit(step, base):
                    if not has(step, base, 1):
                        return
                    t, b = base + step + 1, (step + 1) % 2
                    if not (isinstance(t, int) and t < 2):
                        pool.wait_ge(turned, t - 1)
                        pool.wait_ge(nd_done, t - 1)
                    pool.wait_ge(cleared, 1)
                    nc.gpsimd.tensor_copy(k_tile[:, b], k[:, bass.ts(t, P)]).then_inc(staged, 1)
                    for r in range(4):
                        src = v_ext[:, bass.ts(t, 1), 0:P].rearrange("p o (j r d) -> p (o j) r d", j=4, r=4)[:, :, r]
                        nc.gpsimd.tensor_copy(v_pad[:, b, 4 * r:4 * r + 4, HD * r:HD * r + HD], src).then_inc(staged, 1)

                loop(pool, emit)

            @block.tensor
            def _(pe):
                pe.wait_ge(cleared, 1)

                def emit(step, base):
                    if has(step, base, 1):
                        t, b = base + step + 1, (step + 1) % 2
                        pe.wait_ge(spread, t + 1)
                        pe.wait_ge(staged, COPIES * (t + 1))
                        if not (isinstance(t, int) and t < 1):
                            pe.wait_ge(masked, t)
                            pe.wait_ge(tok_in, t)
                        for g in range(4):
                            last = nc.tensor.matmul(qk[:, g], k_tile[:, b], q_spread[:, b, 4 * g:4 * g + 4]
                                                    .rearrange("p h q -> p (h q)"), start=True, stop=True)
                        last.then_inc(qk_ps, 1)
                        nc.tensor.transpose(kt_ps[:, 0:P], k_tile[:, b], const["ident"][:]).then_inc(turned, 1)
                    if has(step, base, 0):
                        t, b = base + step, step % 2
                        pe.wait_ge(masked, t + 1)
                        pe.wait_ge(st_out, t + 1)
                        if not (isinstance(t, int) and t < 2):
                            pe.wait_ge(nd_out, 2 * (t - 1))
                        for m in range(2):
                            nc.tensor.matmul(nd_ps[:, b, tile(m)], state[:, b, tile(m)], q[:, bass.ts(t, P)],
                                             start=(m == 0), stop=False, skip_group_check=True)
                        for m in range(2):
                            for pos in range(HEADS):
                                j = pos % 4
                                h = pos // 4 + 4 * j
                                lhs = v_pad[:, b, pos] if m == 0 else w["ones_pad"][:, pos]
                                last = nc.tensor.matmul(nd_ps[32 * j:32 * j + 32, b, tile(m)], lhs, prod[:, b, h],
                                                        start=False, stop=(pos >= 12), skip_group_check=True)
                        last.then_inc(nd_done, 1)
                        pe.wait_ge(tok_in, t + 1)
                        nc.tensor.matmul(st_ps[:, 0:2 * P], k_tok[:, b], v_ext[:, bass.ts(t, 1)].rearrange("p o e -> p (o e)"),
                                         start=False, stop=False, skip_group_check=True).then_inc(st_done, 1)

                nc.tensor.matmul(st_ps[:, 0:2 * P], const["zero_bf"], const["zero_bf2"], start=True, stop=False,
                                 skip_group_check=True)
                loop(pe, emit)
                for c in range(NC):
                    pe.wait_ge(scaled, c + 1)
                    nc.tensor.matmul(qk[:, c], w["proj"], att[:, chunk(c)], start=True, stop=True).then_inc(projected, 1)

            @block.scalar
            def _(act):
                def emit(step, base):
                    if has(step, base, 0):
                        t, b = base + step, step % 2
                        act.wait_ge(nd_done, t + 1)
                        nc.scalar.activation(nd[:, 0, bass.ts(t, P)], nd_ps[:, b, tile(0)], ACT.Copy).then_inc(nd_out, 1)
                        nc.scalar.activation(nd[:, 1, bass.ts(t, P)], nd_ps[:, b, tile(1)], ACT.Identity,
                                             bias=const["eps"][:]).then_inc(nd_out, 1)
                    if has(step, base, 1):
                        t, b = base + step + 1, (step + 1) % 2
                        act.wait_ge(turned, t + 1)
                        if not (isinstance(t, int) and t < 2):
                            act.wait_ge(st_done, t - 1)
                        nc.scalar.activation(k_tok[:, b], kt_ps[:, 0:P], ACT.Copy).then_inc(tok_in, 1)

                loop(act, emit)

            @block.vector
            def _(dve):
                nc.vector.memset(state[:, 0], 0.0).then_inc(st_out, 1)

                def spread_q(t, b):
                    if not (isinstance(t, int) and t < 2):
                        dve.wait_ge(qk_ps, t - 1)
                    nc.vector.tensor_tensor(q_spread[:, b], q[:, bass.ts(t, P)][:, None, :].broadcast_to([P, HEADS, P]),
                                            w["head_cols"][:, :, None].broadcast_to([P, HEADS, P]),
                                            ALU.mult).then_inc(spread, 1)

                spread_q(0, 0)

                def emit(step, base):
                    if has(step, base, 2):
                        spread_q(base + step + 2, step % 2)
                    if has(step, base, 1):
                        t, b = base + step + 1, (step + 1) % 2
                        dve.wait_ge(qk_ps, t + 1)
                        if not (isinstance(t, int) and t < 2):
                            dve.wait_ge(nd_done, t - 1)
                        nc.vector.tensor_tensor(prod[:, b], qk[:].rearrange("p g (h q) -> p (g h) q", h=4),
                                                const["causal"][:, None, :].broadcast_to([P, HEADS, P]),
                                                ALU.mult).then_inc(masked, 1)
                    if has(step, base, 0) and has(step, base, 1):
                        t, b = base + step, step % 2
                        dve.wait_ge(st_done, t + 1)
                        nc.vector.tensor_tensor(state[:, 1 - b], st_ps[:, 0:2 * P], w["head_mask2"],
                                                ALU.mult).then_inc(st_out, 1)

                loop(dve, emit)
                for c in range(NC):
                    dve.wait_ge(nd_out, 2 * (4 * c + 4))
                    nc.vector.reciprocal(rden[:, chunk(c)], nd[:, 1, chunk(c)]).then_inc(inverted, 1)
                    dve.wait_ge(inverted, c + 1)
                    nc.vector.tensor_tensor(att[:, chunk(c)], nd[:, 0, chunk(c)], rden[:, chunk(c)],
                                            ALU.mult).then_inc(scaled, 1)
                for c in range(NC):
                    dve.wait_ge(projected, c + 1)
                    nc.vector.scalar_tensor_tensor(x[:, chunk(c)], qk[:, c], vec["proj_b"], x[:, chunk(c)], ALU.add,
                                                   ALU.add).then_inc(added, 1)



class Loads:

    def __init__(self, nc, scope, dram, names, label):
        self.nc, self.dram, self.names = nc, dram, names
        self.sem = scope.sem(f"{label}_loaded")
        self.tiles = {k: scope.sb(f"w_{k}", list(dram[k].shape), dram[k].dtype) for k in names}

    def start(self):
        with self.nc.Block(no_gpsimd_drain=True) as block:
            @block.sync
            def _(sp):
                for k in self.names:
                    sp.dma_start(self.tiles[k][:], self.dram[k]).then_inc(self.sem, 16)

    def finish(self):
        with self.nc.Block(no_gpsimd_drain=True) as block:
            @block.sync
            def _(sp):
                sp.wait_ge(self.sem, 16 * len(self.names))
        return self.tiles


CONST_NAMES = ("mean", "ones", "ident", "eps", "causal", "ident_bf", "neg_ident_bf", "mask_q", "mask_k", "zeros_bf")


def build(nc, dram, out):
    part_scratch = nc.dram_tensor("part_scratch", (2, PARTS, P, T), BF16, kind="Internal").ap()
    k_scratch = nc.dram_tensor("k_scratch", (2, KROWS, PAIRS_H, T), BF16, kind="Internal").ap()
    with ExitStack() as stack:
        s = Scope(nc, stack, "net")
        x = s.sb("x", [P, T])
        n_pad = s.sb("normed", [P, T + 1])
        n = n_pad[:, 1:T + 1]
        norm = Norm(s)
        x_loaded = s.sem("x_loaded")
        n_cleared = s.sem("n_cleared")
        stored = s.sem("stored")
        consts = Loads(nc, s, dram, CONST_NAMES, "const")
        consts.start()
        with nc.Block(no_gpsimd_drain=True) as block:
            @block.sync
            def _(sp):
                sp.dma_start(x[:], dram["x"]).then_inc(x_loaded, 16)
                sp.wait_ge(x_loaded, 16)

            @block.vector
            def _(dve):
                nc.vector.memset(n_pad[:, 0:1], 0.0).then_inc(n_cleared, 1)
                dve.wait_ge(n_cleared, 1)
        c = consts.finish()
        c["zero_bf"], c["zero_bf2"] = c["zeros_bf"][:, 0:P], c["zeros_bf"][:, 0:2 * P]
        c["ffn_runs"] = c["mix_runs"] = 0

        with ExitStack() as inner:
            trig = Loads(nc, Scope(nc, inner, "trig"), dram, ("trig",), "trig")
            trig.start()
            layernorm(nc, norm, c, x, n)
            tables = trig.finish()["trig"]
            attention_a(nc, c, x, n, dram["aa_pairs"], dram["aa_bias"], dram["aa_value_bias"], dram["aa_out_bias"],
                        tables)

        with ExitStack() as inner:
            weights = Loads(nc, Scope(nc, inner, "l0"), dram,
                            ("ff_gate1", "ff_gate2", "ff_gate_b2", "ff_vec", "ff_tb", "ff_w1", "ff_tw1", "ff_w2",
                             "ff_tw2", "ca_w", "ca_kv_b", "ca_gain", "ca_mats", "ca_vec"), "l0")
            weights.start()
            layernorm(nc, norm, c, x, n)
            w = weights.finish()
            ffn = dict(gate1=w["ff_gate1"][:], gate2=w["ff_gate2"][:], gate_b2=w["ff_gate_b2"][:], w1=w["ff_w1"][:],
                          w2=w["ff_w2"][:], tw1=w["ff_tw1"], tw2=w["ff_tw2"], tb=w["ff_tb"][:])
            ffn_vec = dict(gate_b1=w["ff_vec"][:, 0:1], ffn_b=w["ff_vec"][:, 1:FT + 2])
            modulated_ffn(nc, c, x, n, ffn, ffn_vec)
            layernorm(nc, norm, c, x, n)
            cw, cv = w["ca_w"], w["ca_vec"]
            channel_attention(nc, c, x, n,
                              dict(q=cw[:, 0:P], kv=cw[:, P:3 * P], p1=cw[:, 3 * P:4 * P], p2=cw[:, 4 * P:5 * P],
                                      kv_b=w["ca_kv_b"][:], gain=w["ca_gain"], head_mask=w["ca_mats"][:, 0:P],
                                      att_bias=w["ca_mats"][:, P:2 * P]),
                              dict(q_b=cv[:, 0:1], p1_b=cv[:, 1:2], p2_b=cv[:, 2:3], temp=cv[:, 3:4]))
            layernorm(nc, norm, c, x, n)
            modulated_ffn(nc, c, x, n, ffn, ffn_vec)

        with ExitStack() as inner:
            si = Scope(nc, inner, "l1a")
            weights = Loads(nc, si, dram, ("hs_w", "hs_vec", "hs_v_b"), "l1a")
            weights.start()
            q_stack = si.sb("q_stack", [P, PAIRS_H, T], BF16)
            q_cleared = si.sem("q_stack_cleared")
            with nc.Block(no_gpsimd_drain=True) as block:
                @block.gpsimd
                def _(pool):
                    nc.gpsimd.memset(q_stack[:], 0.0).then_inc(q_cleared, 1)
            layernorm(nc, norm, c, x, n)
            w = weights.finish()
            hw, hv = w["hs_w"], w["hs_vec"]
            v = si.sb("values", [P, NT, P])
            project_narrow(nc, n, hw[:, 0:P], hw[:, P:2 * P], hw[:, 2 * P:3 * P], hv[:, 0:1], hv[:, 1:2], w["hs_v_b"],
                           v, q_stack, q_cleared, part_scratch, k_scratch)
            softmax_over_heads(nc, c, x, q_stack, v, k_scratch, hw[:, 3 * P:4 * P], hv[:, 2:3])

        with ExitStack() as inner:
            si = Scope(nc, inner, "l1b")
            weights = Loads(nc, si, dram, ("mix_w", "mix_mu", "la_w", "la_vec", "la_v_b", "la_mask", "la_head_cols",
                                           "la_ones_pad"), "l1b")
            weights.start()
            layernorm(nc, norm, c, x, n)
            w = weights.finish()
            mw = w["mix_w"]
            mix = dict(r=mw[:, 0:P], k=mw[:, P:2 * P], v=mw[:, 2 * P:3 * P])
            mix_ffn(nc, c, x, n_pad, mix, w["mix_mu"][:])
            layernorm(nc, norm, c, x, n)
            with ExitStack() as deep:
                sd = Scope(nc, deep, "gla")
                xn = sd.sb("normed_twice", [P, T])
                q = sd.sb("q", [P, T])
                k = sd.sb("k", [P, T])
                v_ext = sd.sb("v_and_ones", [P, NT, 2 * P])
                layernorm(nc, norm, c, n, xn)
                lw, lv = w["la_w"], w["la_vec"]
                la = dict(q=lw[:, 0:P], k=lw[:, P:2 * P], v=lw[:, 2 * P:3 * P], gate=lw[:, 3 * P:4 * P],
                             proj=lw[:, 4 * P:5 * P], v_b=w["la_v_b"][:], head_mask2=w["la_mask"][:],
                             head_cols=w["la_head_cols"], ones_pad=w["la_ones_pad"])
                vec = dict(ln_g=lv[:, 0:1], ln_b=lv[:, 1:2], q_b=lv[:, 2:3], k_b=lv[:, 3:4], gate_b=lv[:, 4:5],
                              proj_b=lv[:, 5:6])
                gated_projections(nc, c, n, xn, la, vec, q, k, v_ext)
                linear_attention(nc, c, x, q, k, v_ext, la, vec)
            layernorm(nc, norm, c, x, n)
            mix_ffn(nc, c, x, n_pad, mix, w["mix_mu"][:])

        with nc.Block(no_gpsimd_drain=True) as block:
            @block.sync
            def _(sp):
                sp.dma_start(out, x[:]).then_inc(stored, 16)
                sp.wait_ge(stored, 16)



def shape_constants():
    f, b = np.float32, mybir.dt.np(BF16)
    masked = -1e30
    heads = np.kron(np.eye(HEADS), np.ones((HD, HD))).astype(f)
    ones_pad = np.zeros((P, HEADS, 32), f)
    for pos in range(HEADS):
        ones_pad[:, pos, HD * (pos // 4):HD * (pos // 4) + HD] = 1
    half = KD // 2
    theta = (f(1.0) * f(10000.0) ** (np.arange(half, dtype=f) / f(half - 1))).astype(f)
    angle = (np.arange(T, dtype=f)[:, None] / theta[None]).astype(f)
    sin, cos = np.sin(angle).astype(f).T, np.cos(angle).astype(f).T
    return {
        "mean": np.full((P, P), 1.0 / P, f), "ones": np.ones((P, P), f), "ident": np.eye(P, dtype=f),
        "eps": np.full((P, 1), EPS, f), "causal": np.triu(np.ones((P, P), f)),
        "ident_bf": np.eye(P).astype(b), "neg_ident_bf": (-np.eye(P)).astype(b),
        "mask_q": np.triu(np.full((P, P), masked), 1).astype(b), "mask_k": np.tril(np.full((P, P), masked), -1).astype(b),
        "zeros_bf": np.zeros((P, 2 * P), b),
        "trig": np.stack([np.concatenate([cos] * 4, 0), np.concatenate([sin, -sin, sin, -sin], 0)], 1),
        "heads": heads, "la_mask": np.concatenate([heads, heads], 1),
        "la_head_cols": np.repeat(np.eye(HEADS, dtype=f), HD, 0), "la_ones_pad": ones_pad,
    }


def lay_out(a):
    d = shape_constants()
    heads = d.pop("heads")
    rows = lambda r: np.broadcast_to(r, (P,) + r.shape)
    cols = lambda *v: np.stack(v, 1)
    weights = lambda *w: np.concatenate([m.T for m in w], 1)
    d["x"] = a["L0_attn_a_x"][0].T

    w, b, w_out = a["L0_attn_a_W_in"], a["L0_attn_a_b_in"], a["L0_attn_a_W_out"]
    hw = HEADS * KD
    swap = np.arange(hw).reshape(HEADS, 2, KD // 2)[:, ::-1].reshape(-1)
    pairs, biases = [], []
    for p in range(PAIRS):
        r = slice(P * p, P * p + P)
        qk = [(w[o:o + hw][i], b[o:o + hw][i]) for o in (0, hw) for i in (np.arange(hw)[r], swap[r])]
        pairs += [m.T for m, _ in qk] + [w[2 * hw:][r].T, w_out[:, r].T]
        biases += [v for _, v in qk]
    d["aa_pairs"] = np.concatenate(pairs, 1)
    d["aa_bias"] = cols(*biases)
    d["aa_value_bias"] = rows(b[2 * hw:])
    d["aa_out_bias"] = a["L0_attn_a_b_out"][:, None]

    f = {k[len("L0_ffn_"):]: v for k, v in a.items() if k.startswith("L0_ffn_")}
    down = lambda m: m.T.reshape(FT, P, P).transpose(1, 0, 2).reshape(P, FF)
    d["ff_gate1"], d["ff_gate2"], d["ff_gate_b2"] = f["gate_w1"].T, f["gate_w2"].T, rows(f["gate_b2"])
    d["ff_vec"] = cols(f["gate_b1"], *f["b1"].reshape(FT, P), f["b2"])
    d["ff_tb"] = np.concatenate([f["Tb1"].T.reshape(FT, P, EXPERTS), f["Tb2"].T[None]], 0).transpose(1, 0, 2)
    d["ff_w1"], d["ff_w2"] = f["W1"].T, down(f["W2"])
    d["ff_tw1"] = f["TW1"].transpose(2, 0, 1).reshape(P, EXPERTS * FF)
    d["ff_tw2"] = np.concatenate([down(m) for m in f["TW2"]], 1)

    c = {k[len("L0_attn_b_"):]: v for k, v in a.items() if k.startswith("L0_attn_b_")}
    d["ca_w"] = weights(c["qkv_w"], c["p1_w"], c["p2_w"])
    d["ca_kv_b"] = rows(c["qkv_b"][P:])
    d["ca_gain"] = rows(np.stack([np.tile(c[k], HEADS) for k in ("kn_g", "kn_b", "vn_g", "vn_b")]))
    bias = np.zeros((P, P), c["attn_bias"].dtype)
    for h in range(HEADS):
        bias[HD * h:HD * h + HD, HD * h:HD * h + HD] = c["attn_bias"][h]
    d["ca_mats"] = np.concatenate([heads, bias], 1)
    d["ca_vec"] = cols(c["qkv_b"][:P], c["p1_b"], c["p2_b"], np.repeat(c["temperature"].reshape(-1), HD))

    h = {k[len("L1_attn_a_"):]: v for k, v in a.items() if k.startswith("L1_attn_a_")}
    d["hs_w"] = weights(h["Wq"], h["Wk"], h["Wv"], h["Wo"])
    d["hs_vec"] = cols(h["bq"], h["bk"], h["bo"])
    d["hs_v_b"] = rows(h["bv"])

    m = {k[len("L1_ffn_"):]: v for k, v in a.items() if k.startswith("L1_ffn_")}
    d["mix_w"], d["mix_mu"] = weights(m["W_r"], m["W_k"], m["W_v"]), cols(m["mu_r"], m["mu_k"])

    g = {k[len("L1_attn_b_"):]: v for k, v in a.items() if k.startswith("L1_attn_b_")}
    d["la_w"] = weights(g["qkv_w"], g["gate_w"], g["proj_w"])
    d["la_vec"] = cols(g["ln_g"], g["ln_b"], g["qkv_b"][:P], g["qkv_b"][P:2 * P], g["gate_b"], g["proj_b"])
    d["la_v_b"] = rows(g["qkv_b"][2 * P:])
    return {k: np.ascontiguousarray(v) for k, v in d.items()}


def kernel(**inputs):
    import concourse.bacc as bacc
    from concourse.bass_utils import run_bass_kernel_spmd

    arrays = lay_out({k: np.asarray(v) for k, v in inputs.items()})
    nc = bacc.Bacc("TRN2", target_bir_lowering=False, num_devices=1)
    dram = {k: nc.dram_tensor(f"in_{k}", v.shape, mybir.dt.from_np(v.dtype), kind="ExternalInput").ap()
            for k, v in arrays.items()}
    out = nc.dram_tensor("out_x", (P, T), F32, kind="ExternalOutput").ap()
    build(nc, dram, out)
    result = run_bass_kernel_spmd(nc, [{f"in_{k}": v for k, v in arrays.items()}], core_ids=[0])
    return np.ascontiguousarray(result.results[0]["out_x"].T)[None]
```
